# Optimizing a Trainium2 kernel written in Bass

```python
import numpy as np
import jax
import jax.numpy as jnp

def _softmax(x, axis=-1):
    return jax.nn.softmax(x, axis=axis)

def _gelu(x):
    return jax.nn.gelu(x, approximate=True)

def _silu(x):
    return jax.nn.silu(x)

def _sigmoid(x):
    return jax.nn.sigmoid(x)

def _layernorm(x, axis=-1, eps=1e-05):
    m = jnp.mean(x, axis=axis, keepdims=True)
    v = jnp.var(x, axis=axis, keepdims=True)
    return (x - m) / jnp.sqrt(v + eps)

def _scatter_add(tgt, idx, src, axis=0):
    return tgt.at[idx].add(src)

def _segment_sum(src, seg, n):
    return jax.ops.segment_sum(src, seg, n)
kernel_name = 'mk_gnn_preln_d4_gnn_r8_54f507'

def setup_inputs(seed: int=0):
    np.random.seed(seed)
    _w = jnp.asarray

    def _rec_inputs():
        import jax
        import jax.numpy as jnp
        _gk = jax.random.key(seed)
        x = -0.0003019 + 1 * jax.random.normal(jax.random.fold_in(_gk, 1), (1250, 512), jnp.float32)
        _s = jax.random.randint(jax.random.fold_in(_gk, 2), (10000,), 0, 1250, jnp.int32)
        _d = jax.random.randint(jax.random.fold_in(_gk, 3), (10000,), 0, 1250, jnp.int32)
        _loop = jnp.arange(1250, dtype=jnp.int32)
        src = jnp.concatenate([_s, _d, _loop])
        dst = jnp.concatenate([_d, _s, _loop])
        _o = jnp.argsort(dst, stable=True)
        src = src[_o]
        dst = dst[_o]
        edge_attr_8 = 0.0012443 + 1.0001 * jax.random.normal(jax.random.fold_in(_gk, 11), (21250, 8), jnp.float32)
        return (x, src, dst, edge_attr_8)
    x, src, dst, edge_attr_8 = _rec_inputs()

    def _L0_gnn_setup():
        import jax, jax.numpy as jnp
        import numpy as np
        N_NODES = 5000
        N_EDGES = 80000
        DIM_H = 512
        N_HEADS = 8
        D_HEAD = DIM_H // N_HEADS

        def _exphormer_attn(x, edge_index, Wq, Wk, Wv):
            N, D = x.shape
            H, d = (N_HEADS, D_HEAD)
            Q = (x @ Wq).reshape(N, H, d)
            K = (x @ Wk).reshape(N, H, d)
            V = (x @ Wv).reshape(N, H, d)
            src, dst = (edge_index[0], edge_index[1])
            scale = np.float32(1.0 / np.sqrt(d))
            score = jnp.einsum('ehd,ehd->eh', K[src], Q[dst]) * scale
            score = jnp.exp(jnp.clip(score, -5.0, 5.0))[..., None]
            msg = V[src] * score
            wV = jax.ops.segment_sum(msg, dst, num_segments=N)
            Z = jax.ops.segment_sum(score, dst, num_segments=N)
            return (wV / (Z + 1e-06)).reshape(N, D)
        key = jax.random.key(seed)
        ks = jax.random.split(key, 8)
        x = jax.random.normal(ks[0], (N_NODES, DIM_H), dtype=jnp.float32)
        edge_index = jax.random.randint(ks[1], (2, N_EDGES), 0, N_NODES, dtype=jnp.int32)
        virt_h = jax.random.normal(ks[2], (1, DIM_H), dtype=jnp.float32)
        virt_edge_index = jnp.zeros((2, 1), dtype=jnp.int32)
        s = 1.0 / np.sqrt(DIM_H)
        Wq = jax.random.normal(ks[3], (DIM_H, DIM_H), dtype=jnp.float32) * s
        Wk = jax.random.normal(ks[4], (DIM_H, DIM_H), dtype=jnp.float32) * s
        Wv = jax.random.normal(ks[5], (DIM_H, DIM_H), dtype=jnp.float32) * s
        bn_gamma = jnp.ones((DIM_H,), dtype=jnp.float32)
        bn_beta = jnp.zeros((DIM_H,), dtype=jnp.float32)
        return {'x': x, 'edge_index': edge_index, 'virt_h': virt_h, 'virt_edge_index': virt_edge_index, 'Wq': Wq, 'Wk': Wk, 'Wv': Wv, 'bn_gamma': bn_gamma, 'bn_beta': bn_beta}
    _L0_gnn_all = _L0_gnn_setup()
    _L0_gnn_in = {k: v for k, v in _L0_gnn_all.items() if k in ('virt_h', 'virt_edge_index', 'Wq', 'Wk', 'Wv', 'bn_gamma', 'bn_beta')}
    del _L0_gnn_all

    def _L1_gnn_setup():
        import jax, jax.numpy as jnp
        import numpy as np
        N_NODES = 6250
        N_EDGES = 100000
        D_IN = 512
        D_OUT = 512

        def sage_conv(x, src, dst, Wl, Wr, b, num_nodes):
            msg = x[src]
            summed = jax.ops.segment_sum(msg, dst, num_segments=num_nodes)
            cnt = jax.ops.segment_sum(jnp.ones((src.shape[0],), dtype=x.dtype), dst, num_segments=num_nodes)
            mean = summed / jnp.maximum(cnt, 1.0)[:, None]
            return mean @ Wl.T + x @ Wr.T + b
        key = jax.random.key(seed)
        ks = jax.random.split(key, 8)
        s = 1.0 / np.sqrt(D_IN)
        x = jax.random.normal(ks[0], (N_NODES, D_IN), dtype=jnp.float32)
        edge_index = jax.random.randint(ks[1], (2, N_EDGES), 0, N_NODES, dtype=jnp.int64)
        Wl1 = jax.random.normal(ks[2], (D_OUT, D_IN), dtype=jnp.float32) * s
        Wr1 = jax.random.normal(ks[3], (D_OUT, D_IN), dtype=jnp.float32) * s
        b1 = jnp.zeros((D_OUT,), dtype=jnp.float32)
        Wl2 = jax.random.normal(ks[4], (D_IN, D_OUT), dtype=jnp.float32) * s
        Wr2 = jax.random.normal(ks[5], (D_IN, D_OUT), dtype=jnp.float32) * s
        b2 = jnp.zeros((D_IN,), dtype=jnp.float32)
        return {'x': x, 'edge_index': edge_index, 'Wl1': Wl1, 'Wr1': Wr1, 'b1': b1, 'Wl2': Wl2, 'Wr2': Wr2, 'b2': b2}
    _L1_gnn_all = _L1_gnn_setup()
    _L1_gnn_in = {k: v for k, v in _L1_gnn_all.items() if k in ('Wl1', 'Wr1', 'b1', 'Wl2', 'Wr2', 'b2')}
    del _L1_gnn_all

    def _L2_gnn_setup():
        import jax, jax.numpy as jnp
        import numpy as np
        N = 6250
        E = 100000
        D = 512

        def _gcn_conv(x, edge_index, W, b):
            n = x.shape[0]
            xw = x @ W.T
            loop = jnp.arange(n, dtype=edge_index.dtype)
            row = jnp.concatenate([edge_index[0], loop])
            col = jnp.concatenate([edge_index[1], loop])
            deg = jax.ops.segment_sum(jnp.ones_like(row, dtype=xw.dtype), col, num_segments=n)
            dinv = jnp.where(deg > 0, jax.lax.rsqrt(deg), 0.0)
            norm = dinv[row] * dinv[col]
            msgs = norm[:, None] * xw[row]
            out = jax.ops.segment_sum(msgs, col, num_segments=n)
            return out + b

        def _batch_norm(h, gamma, beta, eps=1e-05):
            mean = jnp.mean(h, axis=0)
            var = jnp.var(h, axis=0)
            return (h - mean) * jax.lax.rsqrt(var + eps) * gamma + beta
        key = jax.random.key(seed)
        k1, k2, k3, k4, k5, k6 = jax.random.split(key, 6)
        x = jax.random.normal(k1, (N, D), dtype=jnp.float32)
        edge_index = jax.random.randint(k2, (2, E), 0, N, dtype=jnp.int64)
        W = jax.random.normal(k3, (D, D), dtype=jnp.float32) * (1.0 / np.sqrt(D))
        b = jnp.zeros((D,), dtype=jnp.float32)
        gamma = jnp.ones((D,), dtype=jnp.float32)
        beta = jnp.zeros((D,), dtype=jnp.float32)
        return {'x': x, 'edge_index': edge_index, 'W': W, 'b': b, 'gamma': gamma, 'beta': beta}
    _L2_gnn_all = _L2_gnn_setup()
    _L2_gnn_in = {k: v for k, v in _L2_gnn_all.items() if k in ('W', 'b', 'gamma', 'beta')}
    del _L2_gnn_all

    def _L3_gnn_setup():
        import jax, jax.numpy as jnp
        import numpy as np
        N = 2500
        E = 40000
        D = 512
        H = 8
        DK = D // H
        key = jax.random.key(seed)
        ks = jax.random.split(key, 12)
        x = jax.random.normal(ks[0], (N, D), jnp.float32)
        rows = jnp.sort(jax.random.randint(ks[1], (E,), 0, N))
        cols = jax.random.randint(ks[2], (E,), 0, N)
        edge_index = jnp.stack([rows, cols]).astype(jnp.int32)
        att_bias = jax.random.normal(ks[3], (E, H), jnp.float32)
        s = float(1.0 / np.sqrt(D))
        Wq = jax.random.normal(ks[4], (D, D), jnp.float32) * s
        Wk = jax.random.normal(ks[5], (D, D), jnp.float32) * s
        Wv = jax.random.normal(ks[6], (D, D), jnp.float32) * s
        Wo = jax.random.normal(ks[7], (D, D), jnp.float32) * s
        bq = jnp.zeros((D,), jnp.float32)
        bk = jnp.zeros((D,), jnp.float32)
        bv = jnp.zeros((D,), jnp.float32)
        bo = jnp.zeros((D,), jnp.float32)
        return dict(x=x, edge_index=edge_index, att_bias=att_bias, Wq=Wq, bq=bq, Wk=Wk, bk=bk, Wv=Wv, bv=bv, Wo=Wo, bo=bo)
    _L3_gnn_all = _L3_gnn_setup()
    _L3_gnn_in = {k: v for k, v in _L3_gnn_all.items() if k in ('Wq', 'bq', 'Wk', 'bk', 'Wv', 'bv', 'Wo', 'bo')}
    del _L3_gnn_all
    return {'x': x, 'src': src, 'dst': dst, 'edge_attr_8': edge_attr_8, 'L0_gnn_virt_h': _L0_gnn_in['virt_h'], 'L0_gnn_virt_edge_index': _L0_gnn_in['virt_edge_index'], 'L0_gnn_Wq': _L0_gnn_in['Wq'], 'L0_gnn_Wk': _L0_gnn_in['Wk'], 'L0_gnn_Wv': _L0_gnn_in['Wv'], 'L0_gnn_bn_gamma': _L0_gnn_in['bn_gamma'], 'L0_gnn_bn_beta': _L0_gnn_in['bn_beta'], 'L1_gnn_Wl1': _L1_gnn_in['Wl1'], 'L1_gnn_Wr1': _L1_gnn_in['Wr1'], 'L1_gnn_b1': _L1_gnn_in['b1'], 'L1_gnn_Wl2': _L1_gnn_in['Wl2'], 'L1_gnn_Wr2': _L1_gnn_in['Wr2'], 'L1_gnn_b2': _L1_gnn_in['b2'], 'L2_gnn_W': _L2_gnn_in['W'], 'L2_gnn_b': _L2_gnn_in['b'], 'L2_gnn_gamma': _L2_gnn_in['gamma'], 'L2_gnn_beta': _L2_gnn_in['beta'], 'L3_gnn_Wq': _L3_gnn_in['Wq'], 'L3_gnn_bq': _L3_gnn_in['bq'], 'L3_gnn_Wk': _L3_gnn_in['Wk'], 'L3_gnn_bk': _L3_gnn_in['bk'], 'L3_gnn_Wv': _L3_gnn_in['Wv'], 'L3_gnn_bv': _L3_gnn_in['bv'], 'L3_gnn_Wo': _L3_gnn_in['Wo'], 'L3_gnn_bo': _L3_gnn_in['bo']}

def reference(x, src, dst, edge_attr_8, L0_gnn_virt_h, L0_gnn_virt_edge_index, L0_gnn_Wq, L0_gnn_Wk, L0_gnn_Wv, L0_gnn_bn_gamma, L0_gnn_bn_beta, L1_gnn_Wl1, L1_gnn_Wr1, L1_gnn_b1, L1_gnn_Wl2, L1_gnn_Wr2, L1_gnn_b2, L2_gnn_W, L2_gnn_b, L2_gnn_gamma, L2_gnn_beta, L3_gnn_Wq, L3_gnn_bq, L3_gnn_Wk, L3_gnn_bk, L3_gnn_Wv, L3_gnn_bv, L3_gnn_Wo, L3_gnn_bo):
    import jax
    import jax.numpy as jnp

    def _L0_gnn_ref(x, edge_index, virt_h, virt_edge_index, Wq, Wk, Wv, bn_gamma, bn_beta):
        import jax, jax.numpy as jnp
        import numpy as np
        N_NODES = 5000
        N_EDGES = 80000
        DIM_H = 512
        N_HEADS = 8
        D_HEAD = DIM_H // N_HEADS

        def _exphormer_attn(x, edge_index, Wq, Wk, Wv):
            N, D = x.shape
            H, d = (N_HEADS, D_HEAD)
            Q = (x @ Wq).reshape(N, H, d)
            K = (x @ Wk).reshape(N, H, d)
            V = (x @ Wv).reshape(N, H, d)
            src, dst = (edge_index[0], edge_index[1])
            scale = np.float32(1.0 / np.sqrt(d))
            score = jnp.einsum('ehd,ehd->eh', K[src], Q[dst]) * scale
            score = jnp.exp(jnp.clip(score, -5.0, 5.0))[..., None]
            msg = V[src] * score
            wV = jax.ops.segment_sum(msg, dst, num_segments=N)
            Z = jax.ops.segment_sum(score, dst, num_segments=N)
            return (wV / (Z + 1e-06)).reshape(N, D)
        h_attn = _exphormer_attn(x, edge_index, Wq, Wk, Wv)
        h = x + h_attn
        mean = jnp.mean(h, axis=0)
        var = jnp.mean(jnp.square(h - mean), axis=0)
        return (h - mean) * jax.lax.rsqrt(var + 1e-05) * bn_gamma + bn_beta

    def _L1_gnn_ref(x, edge_index, Wl1, Wr1, b1, Wl2, Wr2, b2):
        import jax, jax.numpy as jnp
        import numpy as np
        N_NODES = 6250
        N_EDGES = 100000
        D_IN = 512
        D_OUT = 512

        def sage_conv(x, src, dst, Wl, Wr, b, num_nodes):
            msg = x[src]
            summed = jax.ops.segment_sum(msg, dst, num_segments=num_nodes)
            cnt = jax.ops.segment_sum(jnp.ones((src.shape[0],), dtype=x.dtype), dst, num_segments=num_nodes)
            mean = summed / jnp.maximum(cnt, 1.0)[:, None]
            return mean @ Wl.T + x @ Wr.T + b
        src, dst = (edge_index[0], edge_index[1])
        n = x.shape[0]
        h = sage_conv(x, src, dst, Wl1, Wr1, b1, n)
        h = jax.nn.relu(h)
        return sage_conv(h, src, dst, Wl2, Wr2, b2, n)

    def _L2_gnn_ref(x, edge_index, W, b, gamma, beta):
        import jax, jax.numpy as jnp
        import numpy as np
        N = 6250
        E = 100000
        D = 512

        def _gcn_conv(x, edge_index, W, b):
            n = x.shape[0]
            xw = x @ W.T
            loop = jnp.arange(n, dtype=edge_index.dtype)
            row = jnp.concatenate([edge_index[0], loop])
            col = jnp.concatenate([edge_index[1], loop])
            deg = jax.ops.segment_sum(jnp.ones_like(row, dtype=xw.dtype), col, num_segments=n)
            dinv = jnp.where(deg > 0, jax.lax.rsqrt(deg), 0.0)
            norm = dinv[row] * dinv[col]
            msgs = norm[:, None] * xw[row]
            out = jax.ops.segment_sum(msgs, col, num_segments=n)
            return out + b

        def _batch_norm(h, gamma, beta, eps=1e-05):
            mean = jnp.mean(h, axis=0)
            var = jnp.var(h, axis=0)
            return (h - mean) * jax.lax.rsqrt(var + eps) * gamma + beta
        identity = x
        h = _gcn_conv(x, edge_index, W, b)
        h = _batch_norm(h, gamma, beta)
        h = jax.nn.gelu(h, approximate=False)
        return h + identity

    def _L3_gnn_ref(x, edge_index, att_bias, Wq, bq, Wk, bk, Wv, bv, Wo, bo):
        import jax, jax.numpy as jnp
        import numpy as np
        N = 2500
        E = 40000
        D = 512
        H = 8
        DK = D // H
        n = x.shape[0]
        rows, cols = (edge_index[0], edge_index[1])
        q = (x @ Wq + bq).reshape(n, H, DK)
        k = (x @ Wk + bk).reshape(n, H, DK)
        v = (x @ Wv + bv).reshape(n, H, DK)
        scale = 1.0 / jnp.sqrt(jnp.asarray(DK, x.dtype))
        logits = jnp.einsum('ehd,ehd->eh', q[rows] * scale, k[cols]) + att_bias
        row_max = jax.ops.segment_max(logits, rows, num_segments=n)
        p = jnp.exp(logits - row_max[rows])
        denom = jax.ops.segment_sum(p, rows, num_segments=n)
        att = p / denom[rows]
        y = jax.ops.segment_sum(att[:, :, None] * v[cols], rows, num_segments=n)
        out = y.reshape(n, H * DK) @ Wo + bo
        return out
    edge_index = jnp.stack([src, dst])
    h = jnp.maximum(_layernorm(x, axis=-1), 0.0)
    x = x + _L0_gnn_ref(h, edge_index, L0_gnn_virt_h, L0_gnn_virt_edge_index, L0_gnn_Wq, L0_gnn_Wk, L0_gnn_Wv, L0_gnn_bn_gamma, L0_gnn_bn_beta)
    h = jnp.maximum(_layernorm(x, axis=-1), 0.0)
    x = x + _L1_gnn_ref(h, edge_index, L1_gnn_Wl1, L1_gnn_Wr1, L1_gnn_b1, L1_gnn_Wl2, L1_gnn_Wr2, L1_gnn_b2)
    h = jnp.maximum(_layernorm(x, axis=-1), 0.0)
    x = x + _L2_gnn_ref(h, edge_index, L2_gnn_W, L2_gnn_b, L2_gnn_gamma, L2_gnn_beta)
    h = jnp.maximum(_layernorm(x, axis=-1), 0.0)
    x = x + _L3_gnn_ref(h, edge_index, edge_attr_8, L3_gnn_Wq, L3_gnn_bq, L3_gnn_Wk, L3_gnn_bk, L3_gnn_Wv, L3_gnn_bv, L3_gnn_Wo, L3_gnn_bo)
    return x

_drawn_inputs = setup_inputs


def setup_inputs(seed=0):
    import zlib

    import numpy as np

    out = dict(_drawn_inputs(seed))
    spreads = {'L0_gnn_bn_gamma': (1.0, 0.2),
     'L0_gnn_bn_beta': (0.0, 0.1),
     'L1_gnn_b1': (0.0, 0.1),
     'L1_gnn_b2': (0.0, 0.1),
     'L2_gnn_b': (0.0, 0.8),
     'L2_gnn_gamma': (1.0, 0.2),
     'L2_gnn_beta': (0.0, 0.334),
     'L3_gnn_bq': (0.0, 0.8),
     'L3_gnn_bk': (0.0, 0.8),
     'L3_gnn_bv': (0.0, 0.1),
     'L3_gnn_bo': (0.0, 0.1)}
    factors = {}
    for name, (base, spread) in spreads.items():
        noise = np.random.default_rng([zlib.crc32(name.encode()), seed]).standard_normal(out[name].shape)
        drawn = base * np.exp(spread * noise) if base else spread * noise
        out[name] = jnp.asarray(drawn.astype(out[name].dtype))
    for name, factor in factors.items():
        out[name] = (out[name] * factor).astype(out[name].dtype)
    return out
```

```python
from contextlib import ExitStack

import concourse.bass as bass
from concourse import mybir

ALU = mybir.AluOpType
ACT = mybir.ActivationFunctionType
AX = mybir.AxisListType
F32 = mybir.dt.float32
BF16 = mybir.dt.bfloat16
F16 = mybir.dt.float16
I32 = mybir.dt.int32

N = 1250
D = 512
HEADS = 8
DH = D // HEADS
PAIRS = HEADS // 2
B = 125
NB = N // B
EDGES = 21250
TILES = EDGES // B
KT = D // 128
CHUNKS = [(0, 417), (417, 417), (834, 416)]
BANK = 512
EPS = 1e-5
TINY = 2.0 ** -64
EMPTY = -1e10
EMPTY_SCALE = 1e26
FLOOR = -1e9
SCALE = DH ** -0.5
TABLE_ROWS = 128 * 12216
BATCH = 17
BAND = 21
BAND_MARGIN = 2
UNROLL = {BAND: 7, TILES: 5}
SLOTS = max(UNROLL.values())


class Mem:
    counts = 0
    hT = counts + NB * N
    probs = hT + KT * N
    cntB = probs
    dinvB = probs + N
    logw = (0, N * HEADS)
    probs3 = 2 * N * HEADS
    pad = probs + 4 * N
    xn = pad
    hn = pad + NB * D
    aT = pad + 2 * NB * D
    v = aT + KT * N
    w = v + NB * D
    wsum = w + 3 * KT * D
    widx = wsum + TILES * HEADS
    ident = widx + TILES
    ones = ident + 128
    small = ones + 128
    end = small + 1150
    pens = w + KT * D
    probs3b = pens + 2 * 625
    yT = probs3b + 2 * N
    xb = yT + 2 * KT * 125
    turned = small + 200
    end = turned + 4 * 500
    assert xb + D <= ident


def edge_windows(banded):
    if not banded:
        return [(0, TILES)] * NB
    return [(min(max(w * TILES // NB - BAND_MARGIN, 0), TILES - BAND), BAND) for w in range(NB)]


def tile_bounds():
    over = [[w for w, (first, count) in enumerate(edge_windows(True)) if first <= t < first + count]
            for t in range(TILES)]
    return [[o[0] * B for o in over], [(o[-1] + 1) * B for o in over]]


def graph_kernel(nc, x, src, dst, bounds, srcrow, dstrow, attr, wq0, wk0, wv0, bn0, wl1, wr1, b1, wl2, wr2, b2, w2, par2,
                 wq3, wk3, wv3, wo3, par3, bv3, bo3, out, table, xsave, keys, stop=None):
    with ExitStack() as ctx:
        mem = ctx.enter_context(nc.sbuf_tensor("mem", [128, Mem.end], F32))
        ps = ctx.enter_context(nc.psum_tensor("ps", [128, 8, BANK], F32))

        def sem(name):
            return ctx.enter_context(nc.semaphore(name))

        def view(at, *shape, p=128):
            size = 1
            for s in shape:
                size *= s
            v = mem[0:p, at:at + size]
            if len(shape) == 1:
                return v
            names = " ".join("abc"[:len(shape)])
            return v.rearrange(f"p ({names}) -> p {names}", **dict(zip("abc", shape)))

        counts = view(Mem.counts, NB, N, p=B)
        hT = view(Mem.hT, KT, N)
        pad = view(Mem.pad, HEADS, N)
        xn = view(Mem.xn, NB, D, p=B)
        hn = view(Mem.hn, NB, D, p=B)
        aT = view(Mem.aT, KT, N)
        vT = view(Mem.v, KT, N)
        vn = view(Mem.v, NB, D, p=B)
        w = [view(Mem.w + j * KT * D, KT, D) for j in range(3)]
        wsum = view(Mem.wsum, TILES, HEADS, p=B)
        widx = view(Mem.widx, TILES, p=B).bitcast(I32)
        ident = view(Mem.ident, 128)
        ones = view(Mem.ones, 128)
        cntB = view(Mem.cntB, N)
        dinvB = view(Mem.dinvB, N)
        s0 = Mem.small
        st = view(s0, 12, 6)
        mv = view(s0 + 72, NB, 2)
        sd = view(s0 + 92, NB)
        rstd = view(s0 + 102, NB)
        nmr = view(s0 + 112, NB)
        epst = view(s0 + 122, 1)
        tiny = view(s0 + 123, 1)
        dinv = view(s0 + 124, NB, p=B)
        bn0s = view(s0 + 134, 2, KT)
        b1s = view(s0 + 142, KT)
        par2s = view(s0 + 146, 3, KT)
        par3s = view(s0 + 158, 2, KT)
        mx = view(s0 + 166, 4, 3, p=B)
        neg = view(s0 + 178, 4, p=B)
        den = view(s0 + 182, 4, p=B)
        rden = view(s0 + 186, 4, p=B)
        bqs = view(s0 + 190, KT)
        zt = view(s0 + 200, 2, 417)

        def layer_norm(name, xin, hout, more_vector=None, more_scalar=None):
            stats, done = sem(name + "_stats"), sem(name + "_done")
            root, inv = sem(name + "_root"), sem(name + "_inv")

            def vector(dve):
                for i in range(NB):
                    nc.vector.bn_stats(st[0:B, i, :], xin[:, i, :]).then_inc(stats, 1)
                dve.wait_ge(stats, NB)
                for i in range(NB):
                    nc.vector.bn_aggr(mv[0:B, i, :], st[0:B, i, :]).then_inc(stats, 1)
                dve.wait_ge(root, 1)
                nc.vector.reciprocal(rstd[0:B, :], sd[0:B, :]).then_inc(inv, 1)
                dve.wait_ge(inv, 1)
                nc.vector.scalar_tensor_tensor(out=nmr[0:B, :], in0=mv[0:B, :, 0], scalar=-1.0, in1=rstd[0:B, :],
                                               op0=ALU.mult, op1=ALU.mult).then_inc(inv, 1)

            def scalar(act):
                act.wait_ge(stats, 2 * NB)
                nc.scalar.activation(sd[0:B, :], mv[0:B, :, 1], ACT.Sqrt, bias=epst[0:B, :]).then_inc(root, 1)
                act.wait_ge(inv, 2)
                for i in range(NB):
                    nc.scalar.activation(hout[:, i, :], xin[:, i, :], ACT.Relu, bias=nmr[0:B, i:i + 1],
                                         scale=rstd[0:B, i:i + 1]).then_inc(done, 1)

            return vector, scalar, done

        def unit_free(pe, u, banks, done):
            last = u - banks
            if last >= 0:
                pe.wait_ge(done[last % 2], last // 2 + 1)

        s_x = sem("x_loaded")
        s_edges = sem("edges_loaded")
        s_attr = sem("attr_loaded")
        s_w = [sem(f"w{j}_loaded") for j in range(3)]
        s_par = sem("parameters_loaded")
        s_const = sem("constants")
        s_key = sem("edge_keys")
        s_exp = sem("edge_weights_ready")
        s_zero = sem("zeros_ready")
        s_fill = sem("table_zeroed")
        e_int = view(Mem.aT, 2, TILES, p=B).bitcast(I32)
        e_src = view(Mem.aT + 2 * TILES, TILES, p=B)
        e_srcf = view(Mem.aT + 9 * TILES + 2 + 8 * B + 64 + N // 2, TILES, p=B)
        e_dst = view(Mem.aT + 3 * TILES, TILES, p=B)
        e_key = view(Mem.aT + 4 * TILES, TILES, p=B)
        e_rank = view(Mem.aT + 5 * TILES, TILES, p=B)
        e_tmp = view(Mem.aT + 6 * TILES, TILES, p=B)
        e_dummy = view(Mem.aT + 7 * TILES, 1, p=B)
        e_win = view(Mem.aT + 7 * TILES + 2, 2, TILES, p=B)
        e_bounds = view(Mem.aT + 9 * TILES + 2 + 8 * B + 64 + N // 2 + TILES, 2, TILES, p=B)
        e_outside = view(s0 + 194, 1, p=B)
        outside = view(s0 + 195, 1, p=1).bitcast(I32)
        e_rowkey = view(Mem.aT + 9 * TILES + 2, 4, 2 * B, p=TILES // 2)
        lower = view(Mem.aT + 9 * TILES + 2 + 8 * B, 64, p=B).bitcast(BF16)[:, 0:B]
        rows = view(Mem.counts, 2, BATCH, B, p=B)
        same = [view(Mem.counts + 2 * BATCH * B + j * BATCH * 64, BATCH, 64, p=B).bitcast(BF16) for j in range(2)]
        before = view(Mem.counts + 2 * BATCH * B + 2 * BATCH * 64, BATCH, 64, p=B).bitcast(BF16)
        e_parts = view(Mem.counts + 2 * BATCH * B + 3 * BATCH * 64, TILES * HEADS * 3 // 2, p=B).bitcast(BF16)
        e_parts = e_parts.rearrange("p (t h c) -> p t h c", h=HEADS, c=3)
        e_rest = view(Mem.counts + 2 * BATCH * B + 3 * BATCH * 64 + TILES * HEADS * 3 // 2, TILES, HEADS, p=B)
        assert 2 * BATCH * B + 3 * BATCH * 64 + TILES * HEADS * 5 // 2 <= NB * N
        e_iota = view(Mem.aT + 9 * TILES + 2 + 8 * B + 64, N // 2, p=B).bitcast(F16)
        e_exp = view(Mem.w + 2 * KT * D, TILES, HEADS, p=B)
        x0 = vn

        assert Mem.aT + 9 * TILES + 2 + 8 * B + 64 + N // 2 + 3 * TILES <= Mem.v
        FILLS = 24
        FILL = TABLE_ROWS * HEADS // 128 // FILLS
        zeros = view(Mem.probs, FILL)
        ln0_v, ln0_s, ln0_done = layer_norm("ln0", x0, hn)
        with nc.Block() as block:
            @block.sync
            def _(sp):
                for i in range(NB):
                    sp.dma_start(x0[:, i, :], x[i * B:(i + 1) * B, :]).then_inc(s_x, 16)
                sp.dma_start(e_int[:, 0, :], src).then_inc(s_edges, 16)
                sp.dma_start(e_int[:, 1, :], dst).then_inc(s_edges, 16)
                sp.dma_start(e_rowkey[:, 0, :].bitcast(I32), srcrow).then_inc(s_edges, 16)
                sp.dma_start(e_rowkey[:, 1, :].bitcast(I32), dstrow).then_inc(s_edges, 16)
                sp.dma_start(e_bounds.rearrange("p a b -> p (a b)"), bounds.to_broadcast([B, 2 * TILES])).then_inc(s_edges, 16)
                sp.dma_start(e_exp.rearrange("p a b -> p (a b)"), attr).then_inc(s_attr, 16)
                sp.dma_start(w[0], wq0.rearrange("(k p) n -> p k n", p=128)).then_inc(s_w[0], 16)
                sp.dma_start(w[1], wk0.rearrange("(k p) n -> p k n", p=128)).then_inc(s_w[1], 16)
                for a, b in ((bn0s, bn0), (par2s, par2), (par3s, par3)):
                    sp.dma_start(a.rearrange("p a b -> p (a b)"), b).then_inc(s_par, 16)
                sp.dma_start(b1s, b1).then_inc(s_par, 16)
                sp.wait_ge(s_zero, 1)
                for j in range(0, FILLS, 2):
                    sp.dma_start(table.rearrange("(p f r) h -> p f (r h)", p=128, f=FILLS)[:, j:j + 2, :],
                                 zeros.rearrange("p (a r) -> p a r", a=1).to_broadcast([128, 2, FILL])).then_inc(s_fill, 16)

            @block.gpsimd
            def _(pool):
                nc.gpsimd.memset(ident[:], 0.0).then_inc(s_const, 1)
                nc.gpsimd.memset(ones[:], 1.0).then_inc(s_const, 1)
                nc.gpsimd.memset(lower[:], 1.0).then_inc(s_const, 1)
                nc.gpsimd.memset(epst[:], EPS).then_inc(s_const, 1)
                nc.gpsimd.memset(tiny[:], TINY).then_inc(s_const, 1)
                pool.wait_ge(s_const, 5)
                nc.gpsimd.affine_select(out=ident[:], in_=ident[:], compare_op=ALU.not_equal, fill=1.0, base=0,
                                        pattern=[[-1, 128]], channel_multiplier=1).then_inc(s_const, 1)
                nc.gpsimd.affine_select(out=lower[:], in_=lower[:], compare_op=ALU.is_gt, fill=0.0, base=0,
                                        pattern=[[-1, B]], channel_multiplier=1).then_inc(s_const, 1)
                nc.gpsimd.iota(e_dummy.bitcast(I32), pattern=[[0, 1]], base=N * N, channel_multiplier=1).then_inc(s_const, 1)
                nc.gpsimd.iota(e_iota, pattern=[[1, N]], base=0, channel_multiplier=0,
                               allow_small_or_imprecise_dtypes=True).then_inc(s_const, 1)

            @block.vector
            def _(dve):
                nc.vector.memset(zeros, 0.0).then_inc(s_zero, 1)
                dve.wait_ge(s_x, 16 * NB)
                dve.wait_ge(s_const, 9)
                ln0_v(dve)
                dve.wait_ge(s_edges, 80)
                nc.vector.tensor_copy(e_srcf, e_int[:, 0, :]).then_inc(s_key, 1)
                nc.vector.tensor_copy(e_dst, e_int[:, 1, :]).then_inc(s_key, 1)
                dve.wait_ge(s_key, 2)
                nc.vector.scalar_tensor_tensor(out=e_key, in0=e_srcf, scalar=float(N), in1=e_dst,
                                               op0=ALU.mult, op1=ALU.add).then_inc(s_key, 1)
                nc.vector.tensor_copy(e_tmp[:, 0:1], e_dummy.bitcast(I32)).then_inc(s_key, 1)
                for j in range(2):
                    nc.vector.tensor_copy(e_rowkey[:, 2 + j, :], e_rowkey[:, j, :].bitcast(I32)).then_inc(s_key, 1)
                dve.wait_ge(s_key, 6)
                nc.vector.scalar_tensor_tensor(out=e_rowkey[:, 0, :], in0=e_rowkey[:, 2, :], scalar=float(N),
                                               in1=e_rowkey[:, 3, :], op0=ALU.mult, op1=ALU.add).then_inc(s_key, 1)

            @block.scalar
            def _(act):
                ln0_s(act)
                act.wait_ge(s_attr, 16)
                nc.scalar.activation(e_exp, e_exp, ACT.Exp).then_inc(s_exp, 1)

        def turn(name, source, target, blocks=NB):
            ready = sem(name + "_turned")
            done = (sem(name + "_by_act"), sem(name + "_by_dve"))

            def pe_(pe):
                for i in range(blocks):
                    unit_free(pe, i, 4, done)
                    for k in range(KT):
                        last = nc.tensor.transpose(ps[:, i % 4, k * B:(k + 1) * B],
                                                   source[:, i, k * 128:(k + 1) * 128], ident[0:B, 0:B])
                    last.then_inc(ready, 1)

            def unit(i):
                return (target[:, :, i * B:(i + 1) * B],
                        ps[:, i % 4, 0:KT * B].rearrange("p (k b) -> p k b", b=B))

            def act_(act):
                for i in range(0, blocks, 2):
                    act.wait_ge(ready, i + 1)
                    o, s = unit(i)
                    nc.scalar.activation(o, s, ACT.Copy).then_inc(done[0], 1)

            def dve_(dve):
                for i in range(1, blocks, 2):
                    dve.wait_ge(ready, i + 1)
                    o, s = unit(i)
                    nc.vector.tensor_copy(o, s).then_inc(done[1], 1)
            return pe_, act_, dve_

        t0_pe, t0_act, t0_dve = turn("h0", hn, hT)
        s_out, s_outsum = sem("edges_outside_bands"), sem("edges_outside_summed")
        s_keysave, s_rows = sem("keys_saved"), [sem(f"key_rows_loaded{j}") for j in range(2)]
        s_part, s_same, s_before, s_rank, s_sums, s_wsum, e0 = (sem(n) for n in (
            "weight_parts", "same_key", "same_before", "rank", "weights_summed", "weights_stored", "index_steps"))
        with nc.Block() as block:
            @block.sync
            def _(sp):
                sp.dma_start(keys.rearrange("(t b) -> t b", t=TILES // 2), e_rowkey[:, 0, :]).then_inc(s_keysave, 16)
                sp.wait_ge(s_keysave, 16)
                for n in range(TILES // BATCH):
                    if n >= 2:
                        sp.wait_ge(s_same, n - 1)
                    flat = keys[n * BATCH * B:(n + 1) * BATCH * B].rearrange("(a b) -> a b", a=1)
                    sp.dma_start(rows[:, n % 2, :, :].rearrange("p a b -> p (a b)"), flat.to_broadcast([B, BATCH * B])).then_inc(s_rows[n % 2], 16)

            @block.tensor
            def _(pe):
                t0_pe(pe)
                pe.wait_ge(s_out, 3)
                nc.tensor.matmul(ps[0:1, 7, 0:1], e_outside, ones[0:B, 0:1], start=True, stop=True).then_inc(s_outsum, 1)
                pe.wait_ge(s_part, 5)
                for n in range(TILES // BATCH):
                    pe.wait_ge(s_same, n + 1)
                    if n >= 2:
                        pe.wait_ge(s_wsum, n - 1)
                    for t in range(BATCH):
                        last = nc.tensor.matmul(ps[0:B, 4 + n % 2, t * 24:(t + 1) * 24], same[n % 2][:, t, 0:B],
                                                e_parts[:, n * BATCH + t, :, :].rearrange("p h c -> p (h c)"),
                                                start=True, stop=True)
                    last.then_inc(s_sums, 1)

            @block.vector
            def _(dve):
                nc.vector.tensor_tensor(e_win[:, 0, :], e_dst, e_bounds[:, 0, :], ALU.is_lt).then_inc(s_out, 1)
                nc.vector.tensor_tensor(e_win[:, 1, :], e_dst, e_bounds[:, 1, :], ALU.is_ge).then_inc(s_out, 1)
                dve.wait_ge(s_out, 2)
                nc.vector.tensor_reduce(e_outside, e_win.rearrange("p a b -> p (a b)"), AX.X, ALU.add).then_inc(s_out, 1)
                dve.wait_ge(s_exp, 1)
                for c in range(3):
                    rest = e_exp if c == 0 else e_rest
                    nc.vector.tensor_copy(e_parts[:, :, :, c], rest).then_inc(s_part, 1)
                    dve.wait_ge(s_part, 2 * c + 1)
                    if c < 2:
                        nc.vector.tensor_tensor(e_rest, rest, e_parts[:, :, :, c], ALU.subtract).then_inc(s_part, 1)
                        dve.wait_ge(s_part, 2 * c + 2)
                t0_dve(dve)
                dve.wait_ge(s_outsum, 1)
                nc.vector.tensor_copy(outside, ps[0:1, 7, 0:1]).then_inc(s_out, 1)
                for n in range(TILES // BATCH):
                    t0 = n * BATCH
                    dve.wait_ge(s_rows[n % 2], 16 * (n // 2 + 1))
                    if n >= 2:
                        dve.wait_ge(s_sums, n - 1)
                    keycols = e_key[:, t0:t0 + BATCH].rearrange("p (t a) -> p t a", a=1).to_broadcast([B, BATCH, B])
                    nc.vector.tensor_tensor(same[n % 2][:, :, 0:B], rows[:, n % 2, :, :], keycols, ALU.is_equal).then_inc(s_same, 1)
                    dve.wait_ge(s_same, n + 1)
                    if n >= 1:
                        dve.wait_ge(s_rank, n)
                    nc.vector.tensor_tensor(before[:, :, 0:B], same[n % 2][:, :, 0:B],
                                            lower.rearrange("p (a b) -> p a b", a=1).to_broadcast([B, BATCH, B]), ALU.mult).then_inc(s_before, 1)
                    dve.wait_ge(s_before, n + 1)
                    nc.vector.tensor_reduce(e_rank[:, t0:t0 + BATCH], before[:, :, 0:B], AX.X, ALU.add).then_inc(s_rank, 1)
                    dve.wait_ge(s_sums, n + 1)
                    nc.vector.tensor_reduce(wsum[:, t0:t0 + BATCH, :],
                                            ps[0:B, 4 + n % 2, 0:BATCH * 24].rearrange("p (t h c) -> p t h c", h=HEADS, c=3),
                                            AX.X, ALU.add).then_inc(s_wsum, 1)
                dve.wait_ge(s_rank, TILES // BATCH)
                nc.vector.tensor_scalar(e_rank, e_rank, 1.0, None, ALU.min).then_inc(e0, 1)
                nc.vector.tensor_scalar(e_src, e_key, -1.0, e_tmp[:, 0:1], ALU.mult, ALU.add).then_inc(e0, 1)
                dve.wait_ge(e0, 2)
                nc.vector.tensor_tensor(e_rank, e_rank, e_src, ALU.mult).then_inc(e0, 1)
                dve.wait_ge(e0, 3)
                nc.vector.tensor_tensor(widx, e_rank, e_key, ALU.add).then_inc(e0, 1)

            @block.scalar
            def _(act):
                t0_act(act)
        if stop == "edges":
            with nc.Block() as block:
                @block.sync
                def _(sp):
                    for q, n in ((s_w[0], 16), (s_w[1], 16), (s_par, 64), (s_fill, 16 * FILLS // 2)):
                        sp.wait_ge(q, n)
            return


        s_scat = sem("weights_scattered")

        def scatter(pool, t):
            if t == 0:
                pool.wait_ge(s_fill, 16 * FILLS // 2)
            else:
                pool.wait_ge(s_scat, 16 * t)
            pool.indirect_dma_start(table, bass.IndirectOffsetOnAxis(ap=widx[:, t:t + 1], axis=0), wsum[:, t, :], None,
                                    compute_op=ALU.add).then_inc(s_scat, 16)

        onehot_src = view(Mem.pad, SLOTS, N // 2, p=B).bitcast(BF16)
        onehot_dst = view(Mem.pad + SLOTS * N // 2, SLOTS, 64, p=B).bitcast(BF16)
        zero_bf = view(Mem.pad + SLOTS * N // 2 + SLOTS * 64, BANK // 2, p=B).bitcast(BF16)
        assert SLOTS * N // 2 + SLOTS * 64 + BANK // 2 <= 2 * NB * D
        s_win = sem("window_targets")
        s_oh = sem("onehot_ready")
        s_ohfree = sem("onehot_free")
        s_cw = sem("window_counted")
        s_cev = sem("window_stored")
        s_zbf = sem("zero_rows")
        blocks_of = [(0, 4), (4, 4), (8, 2)]

        with nc.Block() as block:
            @block.sync
            def _(sp):
                sp.dma_start(w[2], wv0.rearrange("(k p) n -> p k n", p=128)).then_inc(s_w[2], 16)

            @block.gpsimd
            def _(pool):
                for t in range(60):
                    scatter(pool, t)

            def make_onehots(dve, windows):
                made = 0
                for wd, (first, count) in enumerate(windows):
                    nc.vector.tensor_scalar(e_win[:, wd % 2, :], e_dst, float(-wd * B), None, ALU.add).then_inc(s_win, 1)
                    dve.wait_ge(s_win, wd + 1)
                    unroll = UNROLL[count]
                    with dve.Fori(0, count // unroll) as g:
                        for u in range(unroll):
                            slot = (made + u) % unroll
                            dve.wait_ge(s_ohfree, g * unroll + (made + u + 1))
                            at = bass.ds(g * unroll + (first + u), 1)
                            nc.vector.tensor_scalar(onehot_src[:, slot, :], e_iota, e_srcf[:, at], None, ALU.is_equal)
                            nc.vector.tensor_scalar(onehot_dst[:, slot, 0:B], e_iota[:, 0:B], e_win[:, wd % 2, at], None,
                                                    ALU.is_equal).then_inc(s_oh, 1)
                    made += count

            def count_windows(pe, windows):
                pe.sem_inc(s_ohfree, UNROLL[windows[0][1]])
                used = 0
                for wd, (first, count) in enumerate(windows):
                    base = 3 * (wd % 2)
                    if wd >= 2:
                        pe.wait_ge(s_cev, wd - 1)
                    for j in range(3):
                        nc.tensor.matmul(ps[0:B, base + j, :], zero_bf[:, 0:B], zero_bf[:, 0:BANK],
                                         start=True, stop=False)
                    unroll = UNROLL[count]
                    with pe.Fori(0, count // unroll) as g:
                        for u in range(unroll):
                            slot = (used + u) % unroll
                            pe.wait_ge(s_oh, g * unroll + (used + u + 1))
                            for j, (b0, nb) in enumerate(blocks_of):
                                for i in range(nb):
                                    last = nc.tensor.matmul(ps[0:B, base + j, i * B:(i + 1) * B],
                                                            onehot_src[:, slot, (b0 + i) * B:(b0 + i + 1) * B],
                                                            onehot_dst[:, slot, 0:B], start=False, stop=False,
                                                            skip_group_check=True)
                            last.then_inc(s_ohfree, 1)
                    used += count
                    for j in range(3):
                        last = nc.tensor.matmul(ps[0:B, base + j, :], zero_bf[:, 0:B], zero_bf[:, 0:BANK],
                                                start=False, stop=True)
                    last.then_inc(s_cw, 1)

            @block.vector
            def _(dve):
                nc.vector.memset(zero_bf, 0.0).then_inc(s_zbf, 1)
                found = dve.value_load(outside)
                with dve.If(found < 1):
                    make_onehots(dve, edge_windows(True))
                with dve.Else():
                    make_onehots(dve, edge_windows(False))

            @block.tensor
            def _(pe):
                pe.wait_ge(s_zbf, 1)
                found = pe.value_load(outside)
                with pe.If(found < 1):
                    count_windows(pe, edge_windows(True))
                with pe.Else():
                    count_windows(pe, edge_windows(False))

            @block.scalar
            def _(act):
                for wd in range(NB):
                    act.wait_ge(s_cw, wd + 1)
                    for j, (b0, nb) in enumerate(blocks_of):
                        last = nc.scalar.activation(counts[:, b0:b0 + nb, wd * B:(wd + 1) * B],
                                                    ps[0:B, 3 * (wd % 2) + j, 0:nb * B].rearrange("p (i b) -> p i b", b=B),
                                                    ACT.Copy)
                    last.then_inc(s_cev, 1)
        if stop == "counts":
            with nc.Block() as block:
                @block.sync
                def _(sp):
                    for q, n in ((s_w[0], 16), (s_w[1], 16), (s_w[2], 16), (s_par, 64), (s_fill, 16 * FILLS // 2)):
                        sp.wait_ge(q, n)
            return
        def products(name, units, rows, store, by, banks=8, first_bank=0):
            ready = sem(name + "_ready")
            done = {e: sem(f"{name}_stored_{e}") for e in set(by)}

            def engine_of(u):
                return by[u % len(by)]

            def stored(u):
                return sum(engine_of(v) == engine_of(u) for v in range(u + 1))

            def bank(u):
                return ps[0:rows, first_bank + u % banks, :]

            def pe_(pe, hook=None):
                for u, pairs in enumerate(units):
                    if u >= banks:
                        pe.wait_ge(done[engine_of(u - banks)], stored(u - banks))
                    for j, (left, right) in enumerate(pairs):
                        last = nc.tensor.matmul(bank(u)[:, 0:right.shape[-1]], left, right,
                                                start=(j == 0), stop=(j == len(pairs) - 1))
                    last.then_inc(ready, 1)

            def run(letter):
                def go(eng):
                    for u in range(len(units)):
                        if engine_of(u) == letter:
                            eng.wait_ge(ready, u + 1)
                            store(letter, u, bank(u)).then_inc(done[letter], 1)
                return go
            return pe_, run("a"), run("d"), done

        def copy_by(letter, o, s):
            return nc.scalar.activation(o, s, ACT.Copy) if letter == "a" else nc.vector.tensor_copy(o, s)

        MC = [(m, c0, cn) for m in range(KT) for c0, cn in CHUNKS]

        def turned_units(*terms):
            return [[(wt[:, k, m * 128:(m + 1) * 128], inp[:, k, c0:c0 + cn]) for wt, inp in terms for k in range(KT)]
                    for m, c0, cn in MC]

        def natural_units(*terms):
            return [[(inp[:, k, i * B:(i + 1) * B], wt[:, k, :]) for wt, inp in terms for k in range(KT)]
                    for i in range(NB)]

        def gather_units(inp):
            return [[(inp[:, i, m * 128:(m + 1) * 128], counts[:, i, c0:c0 + cn]) for i in range(NB)]
                    for m, c0, cn in MC]

        def turn_back(name, source, store, by):
            ready = sem(name + "_ready")
            done = {e: sem(f"{name}_stored_{e}") for e in set(by)}

            def engine_of(i):
                return by[i % len(by)]

            def pe_(pe):
                for i in range(NB):
                    if i >= 8:
                        pe.wait_ge(done[engine_of(i - 8)], sum(engine_of(v) == engine_of(i - 8) for v in range(i - 7)))
                    for k in range(KT):
                        last = nc.tensor.transpose(ps[0:B, i % 8, k * 128:(k + 1) * 128],
                                                   source[:, k, i * B:(i + 1) * B], ident)
                    last.then_inc(ready, 1)

            def run(letter):
                def go(eng):
                    for i in range(NB):
                        if engine_of(i) == letter:
                            eng.wait_ge(ready, i + 1)
                            store(letter, i, ps[0:B, i % 8, :]).then_inc(done[letter], 1)
                return go
            return pe_, run("a"), run("d"), done

        def batch_norm(name, scale_shift, func, gamma, beta):
            stats, root, steps, out_a = (sem(f"{name}_{n}") for n in ("stats", "root", "steps", "applied"))
            scale, shift = scale_shift

            def vector(dve):
                for j, (m, c0, cn) in enumerate(MC):
                    nc.vector.bn_stats(st[:, j, :], aT[:, m, c0:c0 + cn]).then_inc(stats, 1)
                dve.wait_ge(stats, len(MC))
                for m in range(KT):
                    nc.vector.bn_aggr(mv[:, m, :], st[:, 3 * m:3 * m + 3, :].rearrange("p a b -> p (a b)")).then_inc(stats, 1)
                dve.wait_ge(root, 1)
                nc.vector.reciprocal(rstd[:, 0:KT], sd[:, 0:KT]).then_inc(steps, 1)
                dve.wait_ge(steps, 1)
                nc.vector.tensor_tensor(scale, rstd[:, 0:KT], gamma, ALU.mult).then_inc(steps, 1)
                dve.wait_ge(steps, 2)
                nc.vector.tensor_tensor(nmr[:, 0:KT], mv[:, 0:KT, 0], scale, ALU.mult).then_inc(steps, 1)
                dve.wait_ge(steps, 3)
                nc.vector.tensor_tensor(shift, beta, nmr[:, 0:KT], ALU.subtract).then_inc(steps, 1)

            def scalar(act):
                act.wait_ge(stats, len(MC) + KT)
                nc.scalar.activation(sd[:, 0:KT], mv[:, 0:KT, 1], ACT.Sqrt, bias=epst[:, :]).then_inc(root, 1)
                act.wait_ge(steps, 4)
                for m in range(KT):
                    nc.scalar.activation(aT[:, m, :], aT[:, m, :], func, bias=shift[:, m:m + 1],
                                         scale=scale[:, m:m + 1]).then_inc(out_a, 1)
            return vector, scalar, out_a

        bn_scale = (view(s0 + 194, KT), view(s0 + 1040, KT))

        s_padz = sem("pad_halves_zero")

        def store_padded(e, m, c0, cn, bank, f):
            f(e, pad[0:64, 2 * m, c0:c0 + cn], bank[0:64, 0:cn], slice(0, 64))
            return f(e, pad[64:128, 2 * m + 1, c0:c0 + cn], bank[64:128, 0:cn], slice(64, 128))

        def store_qk0(e, u, bank):
            m, c0, cn = MC[u % 12]
            if u < 12:
                return store_padded(e, m, c0, cn, bank, lambda e, o, s, _: copy_by(e, o, s))
            return copy_by(e, aT[:, m, c0:c0 + cn], bank[:, 0:cn])

        qk0 = products("qk0", turned_units((w[1], hT)) + turned_units((w[0], hT)), 128, store_qk0, "ad", banks=4)
        v0 = products("v0", natural_units((w[2], hT)), B, lambda e, u, bank: copy_by(e, vn[:, u, :], bank), "ad",
                      banks=4, first_bank=4)

        def zero_halves(dve):
            nc.vector.memset(pad[64:128, 0:HEADS:2, :], 0.0).then_inc(s_padz, 1)
            nc.vector.memset(pad[0:64, 1:HEADS:2, :], 0.0).then_inc(s_padz, 1)

        with nc.Block() as block:
            @block.sync
            def _(sp):
                pass

            @block.gpsimd
            def _(pool):
                for t in range(60, 75):
                    scatter(pool, t)

            @block.tensor
            def _(pe):
                pe.wait_ge(s_w[0], 16)
                pe.wait_ge(s_w[1], 16)
                qk0[0](pe)
                pe.wait_ge(s_w[2], 16)
                v0[0](pe)

            @block.scalar
            def _(act):
                qk0[1](act)
                v0[1](act)

            @block.vector
            def _(dve):
                zero_halves(dve)
                qk0[2](dve)
                v0[2](dve)

        probs = view(Mem.probs, 4, N, p=B)
        psums = view(Mem.w, 4, N, p=B)
        s_sc, s_exp0, s_clip, s_mask = (sem(n) for n in ("scores0", "exps0", "clipped0", "masked0"))
        s_pv, s_sum, s_oev, s_z, s_zev, s_norm = (sem(n) for n in ("pv0", "sums0", "output0_stored", "z0", "z0_read", "norm0"))
        LO, HI = 6.737946999085467e-03, 148.4131591025766
        STEPS = PAIRS * NB
        tiles = [(q, q // 2, q % 2) for q in range(2 * STEPS)]

        with nc.Block() as block:
            @block.gpsimd
            def _(pool):
                for q, s, hh in tiles:
                    i, pr = s % NB, s // NB
                    acc = psums[:, (pr % 2) * 2 + hh, :]
                    pool.wait_ge(s_mask, q + 1)
                    if i == 0:
                        if pr >= 2:
                            pool.wait_ge(s_z, 3 * (pr - 1))
                        nc.gpsimd.tensor_scalar(acc, probs[:, q % 4, :], 1.0, 0.0, ALU.mult, ALU.add).then_inc(s_sum, 1)
                    else:
                        pool.wait_ge(s_sum, q - 1)
                        nc.gpsimd.tensor_tensor(acc, acc, probs[:, q % 4, :], ALU.add).then_inc(s_sum, 1)
                    scatter(pool, 75 + q)

            @block.tensor
            def _(pe):
                def scores(s):
                    i, pr = s % NB, s // NB
                    for hh in range(2):
                        for c, (c0, cn) in enumerate(CHUNKS):
                            u = 6 * s + 3 * hh + c
                            if u >= 4:
                                pe.wait_ge(s_exp0, u - 3)
                            nc.tensor.matmul(ps[0:B, 3 + u % 4, 0:cn], pad[:, 2 * pr + hh, i * B:(i + 1) * B],
                                             aT[:, pr, c0:c0 + cn], start=True, stop=True).then_inc(s_sc, 1)

                def weighted(s):
                    i, pr = s % NB, s // NB
                    pe.wait_ge(s_mask, 2 * s + 2)
                    if i == 0 and pr >= 1:
                        pe.wait_ge(s_oev, pr)
                    for c, (c0, cn) in enumerate(CHUNKS):
                        for hh in range(2):
                            h = 2 * pr + hh
                            last = nc.tensor.matmul(ps[64 * hh:64 * hh + 64, c, 0:cn], vn[:, i, h * DH:(h + 1) * DH],
                                                    probs[:, (2 * s + hh) % 4, c0:c0 + cn], start=(i == 0), stop=(i == NB - 1))
                    last.then_inc(s_pv, 1)

                def denominators(pr, c):
                    c0, cn = CHUNKS[c]
                    if c == 0:
                        pe.wait_ge(s_sum, 2 * NB * (pr + 1))
                    if pr or c:
                        pe.wait_ge(s_zev, 3 * pr + c)
                    for hh in range(2):
                        last = nc.tensor.matmul(ps[64 * hh:64 * hh + 64, 7, 0:cn], ones[0:B, 0:64],
                                                psums[:, (pr % 2) * 2 + hh, c0:c0 + cn], start=True, stop=True)
                    last.then_inc(s_z, 1)

                scores(0)
                for s in range(STEPS):
                    if s + 1 < STEPS:
                        scores(s + 1)
                    weighted(s)
                    if 3 <= s % NB < 6 and s > NB:
                        denominators(s // NB - 1, s % NB - 3)
                for c in range(3):
                    denominators(PAIRS - 1, c)

            def store_outputs(act, pr):
                act.wait_ge(s_pv, NB * (pr + 1))
                for c, (c0, cn) in enumerate(CHUNKS):
                    last = nc.scalar.activation(aT[:, pr, c0:c0 + cn], ps[:, c, 0:cn], ACT.Copy)
                last.then_inc(s_oev, 1)

            @block.scalar
            def _(act):
                for q, s, hh in tiles:
                    for c, (c0, cn) in enumerate(CHUNKS):
                        act.wait_ge(s_sc, 3 * q + c + 1)
                        if c == 0 and q >= 4:
                            act.wait_ge(s_pv, (q - 4) // 2 + 1)
                            act.wait_ge(s_sum, q - 3)
                        nc.scalar.activation(probs[:, q % 4, c0:c0 + cn], ps[0:B, 3 + (3 * q + c) % 4, 0:cn], ACT.Exp,
                                             scale=SCALE).then_inc(s_exp0, 1)
                    if s % NB == 0 and s > 0 and hh == 1:
                        store_outputs(act, s // NB - 1)
                store_outputs(act, PAIRS - 1)

            @block.vector
            def _(dve):
                def normalise(pr, pieces):
                    for c in pieces:
                        c0, cn = CHUNKS[c]
                        n = 3 * pr + c
                        z = zt[:, n % 2, 0:cn]
                        dve.wait_ge(s_z, n + 1)
                        nc.vector.tensor_scalar(z, ps[:, 7, 0:cn], 1e-6, None, ALU.add).then_inc(s_zev, 1)
                        dve.wait_ge(s_zev, n + 1)
                        nc.vector.reciprocal(z, z).then_inc(s_norm, 1)
                        dve.wait_ge(s_norm, 3 * n + 1)
                        if c == 0:
                            dve.wait_ge(s_oev, pr + 1)
                        nc.vector.tensor_tensor(aT[:, pr, c0:c0 + cn], aT[:, pr, c0:c0 + cn], z, ALU.mult).then_inc(s_norm, 1)
                        dve.wait_ge(s_norm, 3 * n + 2)
                        nc.vector.tensor_tensor(aT[:, pr, c0:c0 + cn], aT[:, pr, c0:c0 + cn], hT[:, pr, c0:c0 + cn],
                                                ALU.add).then_inc(s_norm, 1)

                for q, s, hh in tiles:
                    dve.wait_ge(s_exp0, 3 * q + 3)
                    nc.vector.tensor_scalar(probs[:, q % 4, :], probs[:, q % 4, :], LO, HI, ALU.max, ALU.min).then_inc(s_clip, 1)
                    dve.wait_ge(s_clip, q + 1)
                    nc.vector.tensor_tensor(probs[:, q % 4, :], probs[:, q % 4, :], counts[:, s % NB, :], ALU.mult).then_inc(s_mask, 1)
                    if 4 <= s % NB < 7 and s > NB and hh == 1:
                        normalise(s // NB - 1, [s % NB - 4])
                normalise(PAIRS - 1, range(3))
        if stop == "att0":
            return
        xld = hn
        s_xre, s_wl = sem("x_reloaded"), [sem(f"l1_w{j}_loaded") for j in range(3)]
        s_b2 = sem("b2_loaded")
        b2B = view(Mem.probs + 2 * N, D, p=B)
        deg_units = [[(ones[0:B, :], counts[:, i, c0:c0 + cn]) for i in range(NB)] for c0, cn in CHUNKS]
        deg = products("degree", deg_units, 128,
                       lambda e, u, bank: copy_by(e, cntB[:, CHUNKS[u][0]:CHUNKS[u][0] + CHUNKS[u][1]], bank[:, 0:CHUNKS[u][1]]), "a")
        bn0_v, bn0_s, bn0_done = batch_norm("bn0", bn_scale, ACT.Identity, bn0s[:, 0, :], bn0s[:, 1, :])
        s_deg = sem("degree_steps")
        with nc.Block() as block:
            @block.sync
            def _(sp):
                for i in range(NB):
                    sp.dma_start(xld[:, i, :], x[i * B:(i + 1) * B, :]).then_inc(s_xre, 16)
                for j, a in enumerate((wl1, wr1, wl2)):
                    sp.dma_start(w[j], a.rearrange("(k p) n -> p k n", p=128)).then_inc(s_wl[j], 16)
                sp.dma_start(b2B, b2.to_broadcast([B, D])).then_inc(s_b2, 16)

            @block.gpsimd
            def _(pool):
                for t in range(155, TILES):
                    scatter(pool, t)

            @block.tensor
            def _(pe):
                deg[0](pe)

            @block.scalar
            def _(act):
                act.wait_ge(s_par, 64)
                bn0_s(act)
                deg[1](act)
                act.wait_ge(deg[3]["a"], 3)
                nc.scalar.activation(dinvB, cntB, ACT.Sqrt, bias=ones[:, 0:1]).then_inc(s_deg, 1)

            @block.vector
            def _(dve):
                dve.wait_ge(s_par, 64)
                bn0_v(dve)

        def add_x(dest, other):
            def store(e, i, bank):
                return nc.vector.tensor_tensor(dest[:, i, :], bank, other[:, i, :], ALU.add)
            return store

        s_rc = sem("reciprocals")
        tb0 = turn_back("bn0_back", aT, add_x(xn, xld), "d")
        with nc.Block() as block:
            @block.tensor
            def _(pe):
                tb0[0](pe)

            @block.vector
            def _(dve):
                dve.wait_ge(s_xre, 16 * NB)
                tb0[2](dve)
                nc.vector.tensor_scalar(cntB, cntB, 1.0, None, ALU.max).then_inc(s_rc, 1)
                nc.vector.reciprocal(dinvB, dinvB).then_inc(s_rc, 1)
                dve.wait_ge(s_rc, 2)
                nc.vector.reciprocal(cntB, cntB).then_inc(s_rc, 1)

        ln1_v, ln1_s, ln1_done = layer_norm("ln1", xn, hn)
        with nc.Block() as block:
            @block.vector
            def _(dve):
                ln1_v(dve)

            @block.scalar
            def _(act):
                ln1_s(act)

        def store_mean(e, u, bank):
            m, c0, cn = MC[u]
            return nc.vector.tensor_tensor(aT[:, m, c0:c0 + cn], bank[:, 0:cn], cntB[:, c0:c0 + cn], ALU.mult)

        t1 = turn("h1", hn, hT)
        g1 = products("mean1", gather_units(hn), 128, store_mean, "d", banks=4, first_bank=4)
        s_b2add = sem("x_plus_b2")
        with nc.Block() as block:
            @block.gpsimd
            def _(pool):
                pool.wait_ge(s_b2, 16)
                for i in range(NB):
                    nc.gpsimd.tensor_tensor(xn[:, i, :], xn[:, i, :], b2B, ALU.add).then_inc(s_b2add, 1)

            @block.tensor
            def _(pe):
                t1[0](pe)
                g1[0](pe)

            @block.scalar
            def _(act):
                t1[1](act)

            @block.vector
            def _(dve):
                t1[2](dve)
                g1[2](dve)

        def store_relu(e, u, bank):
            m, c0, cn = MC[u]
            return nc.scalar.activation(vT[:, m, c0:c0 + cn], bank[:, 0:cn], ACT.Relu, bias=b1s[:, m:m + 1])

        z1 = products("z1", turned_units((w[0], aT), (w[1], hT)), 128, store_relu, "a")
        with nc.Block() as block:
            @block.tensor
            def _(pe):
                pe.wait_ge(s_wl[0], 16)
                pe.wait_ge(s_wl[1], 16)
                z1[0](pe)

            @block.scalar
            def _(act):
                z1[1](act)

        s_wr2, s_w2 = sem("wr2_loaded"), sem("gcn_w_loaded")
        tb1 = turn_back("z1_back", vT, lambda e, i, bank: copy_by(e, hn[:, i, :], bank), "ad")
        with nc.Block() as block:
            @block.sync
            def _(sp):
                sp.dma_start(w[0], wr2.rearrange("(k p) n -> p k n", p=128)).then_inc(s_wr2, 16)
                sp.dma_start(w[1], w2.rearrange("(k p) n -> p k n", p=128)).then_inc(s_w2, 16)

            @block.tensor
            def _(pe):
                tb1[0](pe)

            @block.scalar
            def _(act):
                tb1[1](act)

            @block.vector
            def _(dve):
                tb1[2](dve)

        g2 = products("mean2", gather_units(hn), 128, store_mean, "d")
        with nc.Block() as block:
            @block.tensor
            def _(pe):
                g2[0](pe)

            @block.vector
            def _(dve):
                g2[2](dve)

        x2 = products("x2", natural_units((w[2], aT), (w[0], vT)), B, add_x(xn, xn), "d")
        with nc.Block() as block:
            @block.tensor
            def _(pe):
                pe.wait_ge(s_wl[2], 16)
                pe.wait_ge(s_wr2, 16)
                x2[0](pe)

            @block.vector
            def _(dve):
                x2[2](dve)
        if stop == "x2":
            return

        ln2_v, ln2_s, ln2_done = layer_norm("ln2", xn, hn)
        s_dt, s_dc = sem("dinv_turned"), sem("dinv_copied")
        with nc.Block() as block:
            @block.vector
            def _(dve):
                ln2_v(dve)
                dve.wait_ge(s_dt, 1)
                nc.vector.tensor_copy(dinv, ps[0:B, 0:3, :].rearrange("p a (b c) -> p (a b) c", c=128)[:, 0:NB, 0]).then_inc(s_dc, 1)

            @block.scalar
            def _(act):
                ln2_s(act)

            @block.tensor
            def _(pe):
                for i in range(NB):
                    last = nc.tensor.transpose(ps[0:B, i // 4, (i % 4) * 128:(i % 4) * 128 + 128],
                                               dinvB[:, i * B:(i + 1) * B], ident)
                last.then_inc(s_dt, 1)

        t2 = turn("h2", hn, hT)

        def store_scaled(e, u, bank):
            if e == "a":
                return nc.scalar.activation(vn[:, u, :], bank, ACT.Copy, scale=dinv[:, u:u + 1])
            return nc.vector.tensor_scalar(vn[:, u, :], bank, dinv[:, u:u + 1], None, ALU.mult)

        s_self = sem("self_loops")
        with nc.Block() as block:
            @block.tensor
            def _(pe):
                t2[0](pe)

            @block.scalar
            def _(act):
                t2[1](act)

            @block.vector
            def _(dve):
                t2[2](dve)
                for i in range(NB):
                    nc.vector.tensor_tensor(counts[:, i, i * B:(i + 1) * B], counts[:, i, i * B:(i + 1) * B],
                                            ident[0:B, 0:B], ALU.add).then_inc(s_self, 1)

        xw = products("xw", natural_units((w[1], hT)), B, store_scaled, "ad")
        with nc.Block() as block:
            @block.tensor
            def _(pe):
                pe.wait_ge(s_w2, 16)
                xw[0](pe)

            @block.scalar
            def _(act):
                xw[1](act)

            @block.vector
            def _(dve):
                xw[2](dve)

        def store_gcn(e, u, bank):
            m, c0, cn = MC[u]
            return nc.vector.tensor_tensor(aT[:, m, c0:c0 + cn], bank[:, 0:cn], dinvB[:, c0:c0 + cn], ALU.mult)

        g3 = products("gcn", gather_units(vn), 128, store_gcn, "d")
        s_w3 = [sem(f"l3_w{j}_loaded") for j in range(3)]
        s_gb = sem("gcn_bias")
        with nc.Block() as block:
            @block.sync
            def _(sp):
                for j, a in enumerate((wq3, wk3, wv3)):
                    sp.dma_start(w[j], a.rearrange("(k p) n -> p k n", p=128)).then_inc(s_w3[j], 16)

            @block.tensor
            def _(pe):
                g3[0](pe)

            @block.vector
            def _(dve):
                g3[2](dve)

        with nc.Block() as block:
            @block.vector
            def _(dve):
                for m in range(KT):
                    nc.vector.tensor_scalar(aT[:, m, :], aT[:, m, :], par2s[:, 0, m:m + 1], None, ALU.add).then_inc(s_gb, 1)

        bn2_v, bn2_s, bn2_done = batch_norm("bn2", bn_scale, ACT.Gelu, par2s[:, 1, :], par2s[:, 2, :])
        s_res = sem("gelu_plus_h2")
        with nc.Block() as block:
            @block.vector
            def _(dve):
                bn2_v(dve)
                for m in range(KT):
                    dve.wait_ge(bn2_done, m + 1)
                    nc.vector.tensor_tensor(aT[:, m, :], aT[:, m, :], hT[:, m, :], ALU.add).then_inc(s_res, 1)

            @block.scalar
            def _(act):
                bn2_s(act)

        tb2 = turn_back("gcn_back", aT, add_x(xn, xn), "d")
        with nc.Block() as block:
            @block.tensor
            def _(pe):
                tb2[0](pe)

            @block.vector
            def _(dve):
                tb2[2](dve)
        if stop == "x3":
            with nc.Block() as block:
                @block.sync
                def _(sp):
                    for q in s_w3:
                        sp.wait_ge(q, 16)
            return

        bv3B = view(Mem.probs, D, p=B)
        bo3B = view(Mem.probs + D, D, p=B)
        s_b3, s_bo, s_xs = sem("b3_loaded"), sem("x_plus_bo"), sem("x_saved_sem")
        ln3_v, ln3_s, ln3_done = layer_norm("ln3", xn, hn)
        with nc.Block() as block:
            @block.sync
            def _(sp):
                sp.dma_start(bv3B, bv3.to_broadcast([B, D])).then_inc(s_b3, 16)
                sp.dma_start(bo3B, bo3.to_broadcast([B, D])).then_inc(s_b3, 16)

            @block.vector
            def _(dve):
                ln3_v(dve)
                nc.vector.tensor_scalar(bqs, par3s[:, 0, :], SCALE, None, ALU.mult)

            @block.scalar
            def _(act):
                ln3_s(act)

        t3 = turn("h3", hn, hT)
        with nc.Block() as block:
            @block.gpsimd
            def _(pool):
                pool.wait_ge(s_b3, 32)
                for i in range(NB):
                    nc.gpsimd.tensor_tensor(xn[:, i, :], xn[:, i, :], bo3B, ALU.add).then_inc(s_bo, 1)

            @block.sync
            def _(sp):
                for i in range(NB):
                    sp.wait_ge(s_bo, i + 1)
                    sp.dma_start(xsave[i * B:(i + 1) * B, :], xn[:, i, :]).then_inc(s_xs, 16)
                sp.wait_ge(s_xs, 16 * NB)

            @block.tensor
            def _(pe):
                t3[0](pe)

            @block.scalar
            def _(act):
                t3[1](act)

            @block.vector
            def _(dve):
                t3[2](dve)

        def store_qk3(e, u, bank):
            m, c0, cn = MC[u % 12]

            def scaled(e, o, s, rows):
                if e == "a":
                    return nc.scalar.activation(o, s, ACT.Identity, bias=bqs[rows, m:m + 1], scale=SCALE)
                return nc.vector.tensor_scalar(o, s, par3s[rows, 0, m:m + 1], SCALE, ALU.add, ALU.mult)
            if u < 12:
                return store_padded(e, m, c0, cn, bank, scaled)
            if e == "a":
                return nc.scalar.activation(aT[:, m, c0:c0 + cn], bank[:, 0:cn], ACT.Identity, bias=par3s[:, 1, m:m + 1])
            return nc.vector.tensor_scalar(aT[:, m, c0:c0 + cn], bank[:, 0:cn], par3s[:, 1, m:m + 1], None, ALU.add)

        qk3 = products("qk3", turned_units((w[0], hT)) + turned_units((w[1], hT)), 128, store_qk3, "ad", banks=4)
        v3 = products("v3", natural_units((w[2], hT)), B, lambda e, u, bank: nc.vector.tensor_tensor(
            vn[:, u, :], bank, bv3B, ALU.add), "d", banks=4, first_bank=4)
        with nc.Block() as block:
            @block.tensor
            def _(pe):
                for q in s_w3:
                    pe.wait_ge(q, 16)
                qk3[0](pe)
                v3[0](pe)

            @block.scalar
            def _(act):
                qk3[1](act)

            @block.vector
            def _(dve):
                zero_halves(dve)
                qk3[2](dve)
                v3[2](dve)

        PEN = 625
        PIECES = N * HEADS // PEN
        logw = [view(a, N * HEADS, p=B) for a in Mem.logw]
        pslot = [view(a, N, p=B) for a in (Mem.probs3, Mem.probs3 + N, Mem.probs3b, Mem.probs3b + N)]
        wo = w[0]
        pens = [view(Mem.w + KT * D + j * PEN, PEN, p=B) for j in range(2)]
        turnedp = [view(Mem.turned + 4 * j * B, 4, B, p=B) for j in range(4)]
        yT = [view(Mem.yT + j * KT * B, KT, B) for j in range(2)]
        xb = view(Mem.xb, D, p=B)
        GROUPS = [(0, 4), (4, 4), (8, 2)]
        s_tab = [sem(f"table_loaded{j}") for j in range(2)]
        s_wo, s_pen, s_ln, s_log = (sem(n) for n in ("wo_loaded", "penalty", "logarithm", "log_weights"))
        s_qk, s_logit, s_neg, s_e3, s_rd, s_p3 = (sem(n) for n in ("scores3", "logits3", "neg_max3", "exps3", "recip_den3", "probs3"))
        s_tp, s_tps, s_y, s_ys, s_o, s_ob, s_xb, s_out = (sem(n) for n in (
            "probs_turned", "turned_stored", "y3", "y3_stored", "out3", "out3_added", "x_row_loaded", "out_stored"))
        HT = NB * HEADS

        def prepare(i):
            return [(i, j, i * PIECES + j) for j in range(PIECES)]

        with nc.Block() as block:
            @block.sync
            def _(sp):
                sp.wait_ge(s_scat, 16 * TILES)
                sp.dma_start(wo, wo3.rearrange("(k p) n -> p k n", p=128)).then_inc(s_wo, 16)
                rows = table[0:N * N, :].rearrange("(s t) h -> s (t h)", t=N)

                def load(i):
                    if i >= 2:
                        sp.wait_ge(s_logit, 3 * HEADS * (i - 1))
                    for a, b in ((0, 112), (112, B)):
                        sp.dma_start(logw[i % 2][a:b, :], rows[i * B + a:i * B + b, :]).then_inc(s_tab[i % 2], 16)
                load(0)
                load(1)
                sp.dma_start(xb, xsave[0:B, :]).then_inc(s_xb, 16)
                for i in range(NB):
                    if i + 2 < NB:
                        load(i + 2)
                    sp.wait_ge(s_ob, i + 1)
                    sp.dma_start(out[i * B:(i + 1) * B, :], xb).then_inc(s_out, 16)
                    if i + 1 < NB:
                        sp.wait_ge(s_out, 16 * (i + 1))
                        sp.dma_start(xb, xsave[(i + 1) * B:(i + 2) * B, :]).then_inc(s_xb, 16)
                sp.wait_ge(s_out, 16 * NB)

            @block.gpsimd
            def _(pool):
                def penalty(i, j, n):
                    if j == 0:
                        pool.wait_ge(s_tab[i % 2], 32 * (i // 2 + 1))
                    if n >= 2:
                        pool.wait_ge(s_log, n - 1)
                    nc.gpsimd.tensor_scalar(pens[n % 2], logw[i % 2][:, j * PEN:(j + 1) * PEN], EMPTY_SCALE, EMPTY,
                                            ALU.mult, ALU.add).then_inc(s_pen, 1)
                for k in prepare(0):
                    penalty(*k)
                for q in range(HT):
                    i, h = divmod(q, HEADS)
                    if i + 1 < NB and h >= 4:
                        for k in prepare(i + 1)[4 * (h - 4):4 * (h - 3)]:
                            penalty(*k)
                    pool.wait_ge(s_rd, 2 * q + 2)
                    nc.gpsimd.tensor_scalar(pslot[q % 4], pslot[q % 4], rden[:, q % 4:q % 4 + 1], 1.0,
                                            ALU.mult, ALU.mult).then_inc(s_p3, 1)

            @block.tensor
            def _(pe):
                def scores(q):
                    i, h = divmod(q, HEADS)
                    for c, (c0, cn) in enumerate(CHUNKS):
                        u = 3 * q + c
                        if u >= 4:
                            pe.wait_ge(s_logit, u - 3)
                        nc.tensor.matmul(ps[0:B, u % 4, 0:cn], pad[:, h, i * B:(i + 1) * B], aT[:, h // 2, c0:c0 + cn],
                                         start=True, stop=True).then_inc(s_qk, 1)

                def turn_and_weigh(i, pr):
                    q0 = i * HEADS + 2 * pr
                    for g, (j0, nj) in enumerate(GROUPS):
                        for hh in range(2):
                            n = (q0 + hh - hh) // 2 * 6 + 2 * g + hh
                            if g == 0:
                                pe.wait_ge(s_p3, q0 + hh + 1)
                            if n >= 2:
                                pe.wait_ge(s_tps, n - 1)
                            for j in range(nj):
                                last = nc.tensor.transpose(ps[0:B, 4 + n % 2, j * B:(j + 1) * B],
                                                           pslot[(q0 + hh) % 4][:, (j0 + j) * B:(j0 + j + 1) * B],
                                                           ident[0:B, 0:B])
                            last.then_inc(s_tp, 1)
                        if g >= 1:
                            weigh(i, pr, g - 1)
                    weigh(i, pr, 2)

                def weigh(i, pr, g):
                    q0 = i * HEADS + 2 * pr
                    j0, nj = GROUPS[g]
                    n = q0 // 2 * 6 + 2 * g
                    pe.wait_ge(s_tps, n + 2)
                    if pr == 0 and g == 0 and i >= 1:
                        pe.wait_ge(s_ys, i)
                    for j in range(nj):
                        for hh in range(2):
                            h = 2 * pr + hh
                            last = nc.tensor.matmul(ps[64 * hh:64 * hh + 64, 6, pr * B:(pr + 1) * B],
                                                    vn[:, j0 + j, h * DH:(h + 1) * DH], turnedp[(n + hh) % 4][:, j, :],
                                                    start=(pr == 0 and j0 + j == 0), stop=(pr == PAIRS - 1 and j0 + j == NB - 1),
                                                    skip_group_check=True)
                    last.then_inc(s_y, 1)

                def project(i):
                    pe.wait_ge(s_ys, i + 1)
                    if i >= 1:
                        pe.wait_ge(s_ob, i)
                    for k in range(KT):
                        last = nc.tensor.matmul(ps[0:B, 7, :], yT[i % 2][:, k, :], wo[:, k, :], start=(k == 0), stop=(k == KT - 1))
                    last.then_inc(s_o, 1)

                pe.wait_ge(s_wo, 16)
                scores(0)
                scores(1)
                for s in range(NB * PAIRS):
                    i, pr = divmod(s, PAIRS)
                    if s + 1 < NB * PAIRS:
                        scores(2 * s + 2)
                        scores(2 * s + 3)
                    turn_and_weigh(i, pr)
                    if pr == 1 and i >= 1:
                        project(i - 1)
                project(NB - 1)

            @block.scalar
            def _(act):
                def logarithm(i, j, n):
                    act.wait_ge(s_pen, n + 1)
                    piece = logw[i % 2][:, j * PEN:(j + 1) * PEN]
                    nc.scalar.activation(piece, piece, ACT.Ln, bias=tiny[0:B, :]).then_inc(s_ln, 1)

                def exps(q):
                    act.wait_ge(s_neg, q + 1)
                    nc.scalar.activation(pslot[q % 4], pslot[q % 4], ACT.Exp, bias=neg[:, q % 4:q % 4 + 1],
                                         accum_out=den[:, q % 4:q % 4 + 1]).then_inc(s_e3, 1)
                    i, h = divmod(q, HEADS)
                    if i + 1 < NB and h >= 4:
                        for k in prepare(i + 1)[4 * (h - 4):4 * (h - 3)]:
                            logarithm(*k)

                def store_turned(s):
                    for g, (j0, nj) in enumerate(GROUPS):
                        for hh in range(2):
                            n = 6 * s + 2 * g + hh
                            act.wait_ge(s_tp, n + 1)
                            if n >= 4:
                                act.wait_ge(s_y, (n - 4) // 2 + 1)
                            nc.scalar.activation(turnedp[n % 4][:, 0:nj, :], ps[0:B, 4 + n % 2, 0:nj * B].rearrange("p (j b) -> p j b", b=B),
                                                 ACT.Copy).then_inc(s_tps, 1)

                def store_y(i):
                    act.wait_ge(s_y, 12 * (i + 1))
                    if i >= 2:
                        act.wait_ge(s_o, i - 1)
                    nc.scalar.activation(yT[i % 2], ps[:, 6, 0:KT * B].rearrange("p (k b) -> p k b", b=B), ACT.Copy).then_inc(s_ys, 1)

                for k in prepare(0):
                    logarithm(*k)
                exps(0)
                exps(1)
                for s in range(NB * PAIRS):
                    i, pr = divmod(s, PAIRS)
                    if s + 1 < NB * PAIRS:
                        exps(2 * s + 2)
                        exps(2 * s + 3)
                    store_turned(s)
                    if pr == PAIRS - 1:
                        store_y(i)

            @block.vector
            def _(dve):
                def log_weights(i, j, n):
                    dve.wait_ge(s_ln, n + 1)
                    piece = logw[i % 2][:, j * PEN:(j + 1) * PEN]
                    nc.vector.tensor_tensor(piece, piece, pens[n % 2], ALU.min).then_inc(s_log, 1)

                def logits(q):
                    i, h = divmod(q, HEADS)
                    lw = logw[i % 2].rearrange("p (t h) -> p t h", h=HEADS)[:, :, h]
                    if h == 0:
                        dve.wait_ge(s_log, PIECES * (i + 1))
                    if q >= 4:
                        dve.wait_ge(s_tp, ((q - 4) // 2) * 6 + 6)
                        dve.wait_ge(s_p3, q - 3)
                    for c, (c0, cn) in enumerate(CHUNKS):
                        dve.wait_ge(s_qk, 3 * q + c + 1)
                        if c:
                            dve.wait_ge(s_logit, 3 * q + c)
                        nc.vector.tensor_tensor_reduce(pslot[q % 4][:, c0:c0 + cn], ps[0:B, (3 * q + c) % 4, 0:cn], lw[:, c0:c0 + cn],
                                                       1.0, mx[:, q % 4, c - 1:c] if c else FLOOR, ALU.add, ALU.max,
                                                       mx[:, q % 4, c:c + 1]).then_inc(s_logit, 1)
                    dve.wait_ge(s_logit, 3 * q + 3)
                    nc.vector.tensor_scalar(neg[:, q % 4:q % 4 + 1], mx[:, q % 4, 2:3], -1.0, None, ALU.mult).then_inc(s_neg, 1)

                def reciprocals(q):
                    dve.wait_ge(s_e3, q + 1)
                    nc.vector.tensor_scalar(rden[:, q % 4:q % 4 + 1], den[:, q % 4:q % 4 + 1], 1e-30, None, ALU.add).then_inc(s_rd, 1)
                    dve.wait_ge(s_rd, 2 * q + 1)
                    nc.vector.reciprocal(rden[:, q % 4:q % 4 + 1], rden[:, q % 4:q % 4 + 1]).then_inc(s_rd, 1)

                def add_out(i):
                    dve.wait_ge(s_o, i + 1)
                    dve.wait_ge(s_xb, 16 * (i + 1))
                    nc.vector.tensor_tensor(xb, ps[0:B, 7, :], xb, ALU.add).then_inc(s_ob, 1)

                for k in prepare(0):
                    log_weights(*k)
                for q in range(HT):
                    logits(q)
                    if q >= 1:
                        reciprocals(q - 1)
                    i, h = divmod(q, HEADS)
                    if i + 1 < NB and h >= 4:
                        for k in prepare(i + 1)[4 * (h - 4):4 * (h - 3)]:
                            log_weights(*k)
                    if h == 6 and i >= 1:
                        add_out(i - 1)
                reciprocals(HT - 1)
                add_out(NB - 1)


def layout(x, src, dst, edge_attr_8, **p):
    import numpy as np

    def cols(*vectors):
        return np.concatenate([np.asarray(v).reshape(KT, 128).T for v in vectors], axis=1)

    return {
        "x": x, "src": src.reshape(TILES, B).T, "dst": dst.reshape(TILES, B).T,
        "bounds": np.asarray(tile_bounds(), np.float32).reshape(1, 2 * TILES),
        "srcrow": src.reshape(TILES // 2, 2 * B), "dstrow": dst.reshape(TILES // 2, 2 * B),
        "attr": edge_attr_8.reshape(TILES, B, HEADS).transpose(1, 0, 2).reshape(B, TILES * HEADS),
        "wq0": p["L0_gnn_Wq"], "wk0": p["L0_gnn_Wk"], "wv0": p["L0_gnn_Wv"],
        "bn0": cols(p["L0_gnn_bn_gamma"], p["L0_gnn_bn_beta"]),
        "wl1": p["L1_gnn_Wl1"].T, "wr1": p["L1_gnn_Wr1"].T, "b1": cols(p["L1_gnn_b1"]),
        "wl2": p["L1_gnn_Wl2"].T, "wr2": p["L1_gnn_Wr2"].T, "b2": p["L1_gnn_b2"].reshape(1, D),
        "w2": p["L2_gnn_W"].T, "par2": cols(p["L2_gnn_b"], p["L2_gnn_gamma"], p["L2_gnn_beta"]),
        "wq3": p["L3_gnn_Wq"], "wk3": p["L3_gnn_Wk"], "wv3": p["L3_gnn_Wv"], "wo3": p["L3_gnn_Wo"],
        "par3": cols(p["L3_gnn_bq"], p["L3_gnn_bk"]), "bv3": p["L3_gnn_bv"].reshape(1, D),
        "bo3": p["L3_gnn_bo"].reshape(1, D),
    }


def kernel(**inputs):
    import numpy as np
    import concourse.bacc as bacc
    from concourse.bass_utils import run_bass_kernel_spmd

    nc = bacc.Bacc("TRN2", target_bir_lowering=False, num_devices=1)
    arrays, args = {}, {}
    for name, a in layout(**{k: np.asarray(v) for k, v in inputs.items()}).items():
        a = np.ascontiguousarray(a)
        arrays[f"in_{name}"] = a
        args[name] = nc.dram_tensor(f"in_{name}", a.shape, mybir.dt.from_np(a.dtype), kind="ExternalInput").ap()
    out = nc.dram_tensor("out_x", (N, D), F32, kind="ExternalOutput").ap()
    table = nc.dram_tensor("edge_weights", (TABLE_ROWS, HEADS), F32, kind="Internal").ap()
    xsave = nc.dram_tensor("x_saved", (N, D), F32, kind="Internal").ap()
    keys = nc.dram_tensor("edge_keys_row", (EDGES,), F32, kind="Internal").ap()
    graph_kernel(nc, **args, out=out, table=table, xsave=xsave, keys=keys)
    r = run_bass_kernel_spmd(nc, [arrays], core_ids=[0])
    return r.results[0]["out_x"]
```

```python
from contextlib import ExitStack

import concourse.bass as bass
from concourse import mybir

ALU = mybir.AluOpType
ACT = mybir.ActivationFunctionType
AX = mybir.AxisListType
F32 = mybir.dt.float32
BF16 = mybir.dt.bfloat16
F16 = mybir.dt.float16
I32 = mybir.dt.int32

N = 1250
D = 512
HEADS = 8
DH = D // HEADS
PAIRS = HEADS // 2
B = 125
NB = N // B
EDGES = 21250
TILES = EDGES // B
KT = D // 128
CHUNKS = [(0, 417), (417, 417), (834, 416)]
BANK = 512
EPS = 1e-5
EMPTY = 1e10
NOTHING = 1e-30
CEILING = 1e9
SCALE = DH ** -0.5
TABLE_ROWS = 128 * 12216
BATCH = 17
BAND = 21
BAND_MARGIN = 2
UNROLL = {BAND: 7, TILES: 5}
SLOTS = max(UNROLL.values())


class Mem:
    counts = 0
    hT = counts + NB * N
    probs = hT + KT * N
    cntB = probs
    dinvB = probs + N
    weights = (0, N * HEADS)
    probs3 = 2 * N * HEADS
    pad = probs + 4 * N
    xn = pad
    hn = pad + NB * D
    aT = pad + 2 * NB * D
    v = aT + KT * N
    w = v + NB * D
    wsum = w + 3 * KT * D
    widx = wsum + TILES * HEADS
    ident = widx + TILES
    ones = ident + 128
    small = ones + 128
    end = small + 1150
    masks = w + KT * D
    probs3b = masks + N
    yT = probs3b + 2 * N
    xb = yT + 2 * KT * 125
    turned = small + 200
    zeros = small + 1048
    end = turned + 4 * 500
    assert xb + D <= ident


def edge_windows(banded):
    if not banded:
        return [(0, TILES)] * NB
    return [(min(max(w * TILES // NB - BAND_MARGIN, 0), TILES - BAND), BAND) for w in range(NB)]


def tile_bounds():
    over = [[w for w, (first, count) in enumerate(edge_windows(True)) if first <= t < first + count]
            for t in range(TILES)]
    return [[o[0] * B for o in over], [(o[-1] + 1) * B for o in over]]


def graph_kernel(nc, x, src, dst, bounds, srcrow, dstrow, attr, wq0, wk0, wv0, bn0, wl1, wr1, b1, wl2, wr2, b2, w2, par2,
                 wq3, wk3, wv3, wo3, par3, bv3, bo3, out, table, xsave, keys, stop=None):
    with ExitStack() as ctx:
        mem = ctx.enter_context(nc.sbuf_tensor("mem", [128, Mem.end], F32))
        ps = ctx.enter_context(nc.psum_tensor("ps", [128, 8, BANK], F32))

        def sem(name):
            return ctx.enter_context(nc.semaphore(name))

        def view(at, *shape, p=128):
            size = 1
            for s in shape:
                size *= s
            v = mem[0:p, at:at + size]
            if len(shape) == 1:
                return v
            names = " ".join("abc"[:len(shape)])
            return v.rearrange(f"p ({names}) -> p {names}", **dict(zip("abc", shape)))

        counts = view(Mem.counts, NB, N, p=B)
        hT = view(Mem.hT, KT, N)
        pad = view(Mem.pad, HEADS, N)
        xn = view(Mem.xn, NB, D, p=B)
        hn = view(Mem.hn, NB, D, p=B)
        aT = view(Mem.aT, KT, N)
        vT = view(Mem.v, KT, N)
        vn = view(Mem.v, NB, D, p=B)
        w = [view(Mem.w + j * KT * D, KT, D) for j in range(3)]
        wsum = view(Mem.wsum, TILES, HEADS, p=B)
        widx = view(Mem.widx, TILES, p=B).bitcast(I32)
        ident = view(Mem.ident, 128)
        ones = view(Mem.ones, 128)
        cntB = view(Mem.cntB, N)
        dinvB = view(Mem.dinvB, N)
        s0 = Mem.small
        st = view(s0, 12, 6)
        mv = view(s0 + 72, NB, 2)
        sd = view(s0 + 92, NB)
        rstd = view(s0 + 102, NB)
        nmr = view(s0 + 112, NB)
        epst = view(s0 + 122, 1)
        dinv = view(s0 + 124, NB, p=B)
        bn0s = view(s0 + 134, 2, KT)
        b1s = view(s0 + 142, KT)
        par2s = view(s0 + 146, 3, KT)
        par3s = view(s0 + 158, 2, KT)
        mx = view(s0 + 166, 4, 3, p=B)
        den = view(s0 + 182, 4, p=B)
        rden = view(s0 + 186, 4, p=B)
        bqs = view(s0 + 190, KT)
        zt = view(s0 + 200, 2, 417)

        def layer_norm(name, xin, hout, more_vector=None, more_scalar=None):
            stats, done = sem(name + "_stats"), sem(name + "_done")
            root, inv = sem(name + "_root"), sem(name + "_inv")

            def vector(dve):
                for i in range(NB):
                    nc.vector.bn_stats(st[0:B, i, :], xin[:, i, :]).then_inc(stats, 1)
                dve.wait_ge(stats, NB)
                for i in range(NB):
                    nc.vector.bn_aggr(mv[0:B, i, :], st[0:B, i, :]).then_inc(stats, 1)
                dve.wait_ge(root, 1)
                nc.vector.reciprocal(rstd[0:B, :], sd[0:B, :]).then_inc(inv, 1)
                dve.wait_ge(inv, 1)
                nc.vector.scalar_tensor_tensor(out=nmr[0:B, :], in0=mv[0:B, :, 0], scalar=-1.0, in1=rstd[0:B, :],
                                               op0=ALU.mult, op1=ALU.mult).then_inc(inv, 1)

            def scalar(act):
                act.wait_ge(stats, 2 * NB)
                nc.scalar.activation(sd[0:B, :], mv[0:B, :, 1], ACT.Sqrt, bias=epst[0:B, :]).then_inc(root, 1)
                act.wait_ge(inv, 2)
                for i in range(NB):
                    nc.scalar.activation(hout[:, i, :], xin[:, i, :], ACT.Relu, bias=nmr[0:B, i:i + 1],
                                         scale=rstd[0:B, i:i + 1]).then_inc(done, 1)

            return vector, scalar, done

        def unit_free(pe, u, banks, done):
            last = u - banks
            if last >= 0:
                pe.wait_ge(done[last % 2], last // 2 + 1)

        s_x = sem("x_loaded")
        s_edges = sem("edges_loaded")
        s_attr = sem("attr_loaded")
        s_w = [sem(f"w{j}_loaded") for j in range(3)]
        s_par = sem("parameters_loaded")
        s_const = sem("constants")
        s_key = sem("edge_keys")
        s_exp = sem("edge_weights_ready")
        s_zero = sem("zeros_ready")
        s_keysave, s_rows = sem("keys_saved"), [sem(f"key_rows_loaded{j}") for j in range(2)]
        s_fill = sem("table_zeroed")
        E = Mem.probs
        e_int = view(E, 2, TILES, p=B).bitcast(I32)
        e_src = view(E + 2 * TILES, TILES, p=B)
        e_dst = view(E + 3 * TILES, TILES, p=B)
        e_key = view(E + 4 * TILES, TILES, p=B)
        e_rank = view(E + 5 * TILES, TILES, p=B)
        e_tmp = view(E + 6 * TILES, TILES, p=B)
        e_win = view(E + 7 * TILES, 2, TILES, p=B)
        e_srcf = view(E + 9 * TILES, TILES, p=B)
        e_bounds = view(E + 10 * TILES, 2, TILES, p=B)
        e_dummy = view(E + 12 * TILES, 1, p=B)
        e_rowkey = view(E + 12 * TILES + 2, 4, 2 * B, p=TILES // 2)
        lower = view(E + 12 * TILES + 2 + 8 * B, 64, p=B).bitcast(BF16)[:, 0:B]
        e_iota = view(E + 12 * TILES + 2 + 8 * B + 64, N // 2, p=B).bitcast(F16)
        assert E + 12 * TILES + 2 + 8 * B + 64 + N // 2 <= Mem.pad
        e_outside = view(s0 + 194, 1, p=B)
        outside = view(s0 + 195, 1, p=1).bitcast(I32)
        rows = view(Mem.counts, 2, BATCH, B, p=B)
        at = Mem.counts + 2 * BATCH * B
        same = [view(at + j * BATCH * 64, BATCH, 64, p=B).bitcast(BF16) for j in range(2)]
        before = view(at + 2 * BATCH * 64, BATCH, 64, p=B).bitcast(BF16)
        at += 3 * BATCH * 64
        e_parts = view(at, TILES * HEADS * 3 // 2, p=B).bitcast(BF16)
        e_parts = e_parts.rearrange("p (t h c) -> p t h c", h=HEADS, c=3)
        e_exp = view(at + TILES * HEADS * 3 // 2, TILES, HEADS, p=B)
        assert at + TILES * HEADS * 5 // 2 <= Mem.hT
        h0 = vn
        FILLS = 96
        FILL = TABLE_ROWS * HEADS // 128 // FILLS
        FILL_DMAS = 12
        zeros = view(Mem.zeros, FILL)
        ln0_v, ln0_s, ln0_done = layer_norm("ln0", h0, h0)
        with nc.Block() as block:
            @block.sync
            def _(sp):
                sp.dma_start(e_int[:, 0, :], src).then_inc(s_edges, 16)
                sp.dma_start(e_int[:, 1, :], dst).then_inc(s_edges, 16)
                sp.dma_start(e_rowkey[:, 0, :].bitcast(I32), srcrow).then_inc(s_edges, 16)
                sp.dma_start(e_rowkey[:, 1, :].bitcast(I32), dstrow).then_inc(s_edges, 16)
                sp.dma_start(e_bounds.rearrange("p a b -> p (a b)"), bounds.to_broadcast([B, 2 * TILES])).then_inc(s_edges, 16)
                for i in range(NB):
                    sp.dma_start(h0[:, i, :], x[i * B:(i + 1) * B, :]).then_inc(s_x, 16)
                sp.dma_start(e_exp.rearrange("p a b -> p (a b)"), attr).then_inc(s_attr, 16)
                for j, a in ((1, wk0), (0, wq0), (2, wv0)):
                    sp.dma_start(w[j], a.rearrange("(k p) n -> p k n", p=128)).then_inc(s_w[j], 16)
                for a, b in ((bn0s, bn0), (par2s, par2), (par3s, par3)):
                    sp.dma_start(a.rearrange("p a b -> p (a b)"), b).then_inc(s_par, 16)
                sp.dma_start(b1s, b1).then_inc(s_par, 16)
                sp.wait_ge(s_key, 7)
                sp.dma_start(keys.rearrange("(t b) -> t b", t=TILES // 2), e_rowkey[:, 0, :]).then_inc(s_keysave, 16)

            @block.gpsimd
            def _(pool):
                nc.gpsimd.memset(ident[:], 0.0).then_inc(s_const, 1)
                nc.gpsimd.memset(ones[:], 1.0).then_inc(s_const, 1)
                nc.gpsimd.memset(lower[:], 1.0).then_inc(s_const, 1)
                nc.gpsimd.memset(epst[:], EPS).then_inc(s_const, 1)
                pool.wait_ge(s_const, 4)
                nc.gpsimd.affine_select(out=ident[:], in_=ident[:], compare_op=ALU.not_equal, fill=1.0, base=0,
                                        pattern=[[-1, 128]], channel_multiplier=1).then_inc(s_const, 1)
                nc.gpsimd.affine_select(out=lower[:], in_=lower[:], compare_op=ALU.is_gt, fill=0.0, base=0,
                                        pattern=[[-1, B]], channel_multiplier=1).then_inc(s_const, 1)
                nc.gpsimd.iota(e_dummy.bitcast(I32), pattern=[[0, 1]], base=N * N, channel_multiplier=1).then_inc(s_const, 1)
                nc.gpsimd.iota(e_iota, pattern=[[1, N]], base=0, channel_multiplier=0,
                               allow_small_or_imprecise_dtypes=True).then_inc(s_const, 1)

            @block.vector
            def _(dve):
                nc.vector.memset(zeros, 0.0).then_inc(s_zero, 1)
                dve.wait_ge(s_const, 8)
                dve.wait_ge(s_edges, 80)
                nc.vector.tensor_copy(e_srcf, e_int[:, 0, :]).then_inc(s_key, 1)
                nc.vector.tensor_copy(e_dst, e_int[:, 1, :]).then_inc(s_key, 1)
                dve.wait_ge(s_key, 2)
                nc.vector.scalar_tensor_tensor(out=e_key, in0=e_srcf, scalar=float(N), in1=e_dst,
                                               op0=ALU.mult, op1=ALU.add).then_inc(s_key, 1)
                nc.vector.tensor_copy(e_tmp[:, 0:1], e_dummy.bitcast(I32)).then_inc(s_key, 1)
                for j in range(2):
                    nc.vector.tensor_copy(e_rowkey[:, 2 + j, :], e_rowkey[:, j, :].bitcast(I32)).then_inc(s_key, 1)
                dve.wait_ge(s_key, 6)
                nc.vector.scalar_tensor_tensor(out=e_rowkey[:, 0, :], in0=e_rowkey[:, 2, :], scalar=float(N),
                                               in1=e_rowkey[:, 3, :], op0=ALU.mult, op1=ALU.add).then_inc(s_key, 1)
                dve.wait_ge(s_x, 16 * NB)
                ln0_v(dve)

            @block.scalar
            def _(act):
                ln0_s(act)
                act.wait_ge(s_attr, 16)
                nc.scalar.activation(e_exp, e_exp, ACT.Exp).then_inc(s_exp, 1)

        def products(name, units, store, by, banks=8, first_bank=0):
            ready = sem(name + "_ready")
            done = {e: sem(f"{name}_stored_{e}") for e in set(by)}

            def engine_of(u):
                return by[u % len(by)]

            def stored(u):
                return sum(engine_of(v) == engine_of(u) for v in range(u + 1))

            def bank(u):
                return ps[0:units[u][0][0].shape[-1], first_bank + u % banks, :]

            def pe_(pe, before=None):
                for u, pairs in enumerate(units):
                    if before:
                        before(u)
                    if u >= banks:
                        pe.wait_ge(done[engine_of(u - banks)], stored(u - banks))
                    for j, (left, right) in enumerate(pairs):
                        last = nc.tensor.matmul(bank(u)[:, 0:right.shape[-1]], left, right,
                                                start=(j == 0), stop=(j == len(pairs) - 1))
                    last.then_inc(ready, 1)

            def run(letter):
                def go(eng):
                    for u in range(len(units)):
                        if engine_of(u) == letter:
                            eng.wait_ge(ready, u + 1)
                            store(letter, u, bank(u)).then_inc(done[letter], 1)
                return go
            return pe_, run("a"), run("d"), done

        def copy_by(letter, o, s):
            return nc.scalar.activation(o, s, ACT.Copy) if letter == "a" else nc.vector.tensor_copy(o, s)

        MC = [(m, c0, cn) for m in range(KT) for c0, cn in CHUNKS]

        def turned_units(*terms):
            return [[(wt[:, k, m * 128:(m + 1) * 128], inp[:, k, c0:c0 + cn]) for wt, inp in terms for k in range(KT)]
                    for m, c0, cn in MC]

        def natural_units(*terms):
            return [[(inp[:, k, i * B:(i + 1) * B], wt[:, k, :]) for wt, inp in terms for k in range(KT)]
                    for i in range(NB)]

        def gather_units(inp):
            return [[(inp[:, i, m * 128:(m + 1) * 128], counts[:, i, c0:c0 + cn]) for i in range(NB)]
                    for m, c0, cn in MC]

        def turn_back(name, source, store, by):
            ready = sem(name + "_ready")
            done = {e: sem(f"{name}_stored_{e}") for e in set(by)}

            def engine_of(i):
                return by[i % len(by)]

            def pe_(pe):
                for i in range(NB):
                    if i >= 8:
                        pe.wait_ge(done[engine_of(i - 8)], sum(engine_of(v) == engine_of(i - 8) for v in range(i - 7)))
                    for k in range(KT):
                        last = nc.tensor.transpose(ps[0:B, i % 8, k * 128:(k + 1) * 128],
                                                   source[:, k, i * B:(i + 1) * B], ident)
                    last.then_inc(ready, 1)

            def run(letter):
                def go(eng):
                    for i in range(NB):
                        if engine_of(i) == letter:
                            eng.wait_ge(ready, i + 1)
                            store(letter, i, ps[0:B, i % 8, :]).then_inc(done[letter], 1)
                return go
            return pe_, run("a"), run("d"), done

        def batch_norm(name, scale_shift, func, gamma, beta):
            stats, root, steps, out_a = (sem(f"{name}_{n}") for n in ("stats", "root", "steps", "applied"))
            scale, shift = scale_shift

            def vector(dve):
                for j, (m, c0, cn) in enumerate(MC):
                    nc.vector.bn_stats(st[:, j, :], aT[:, m, c0:c0 + cn]).then_inc(stats, 1)
                dve.wait_ge(stats, len(MC))
                for m in range(KT):
                    nc.vector.bn_aggr(mv[:, m, :], st[:, 3 * m:3 * m + 3, :].rearrange("p a b -> p (a b)")).then_inc(stats, 1)
                dve.wait_ge(root, 1)
                nc.vector.reciprocal(rstd[:, 0:KT], sd[:, 0:KT]).then_inc(steps, 1)
                dve.wait_ge(steps, 1)
                nc.vector.tensor_tensor(scale, rstd[:, 0:KT], gamma, ALU.mult).then_inc(steps, 1)
                dve.wait_ge(steps, 2)
                nc.vector.tensor_tensor(nmr[:, 0:KT], mv[:, 0:KT, 0], scale, ALU.mult).then_inc(steps, 1)
                dve.wait_ge(steps, 3)
                nc.vector.tensor_tensor(shift, beta, nmr[:, 0:KT], ALU.subtract).then_inc(steps, 1)

            def scalar(act):
                act.wait_ge(stats, len(MC) + KT)
                nc.scalar.activation(sd[:, 0:KT], mv[:, 0:KT, 1], ACT.Sqrt, bias=epst[:, :]).then_inc(root, 1)
                act.wait_ge(steps, 4)
                for m in range(KT):
                    nc.scalar.activation(aT[:, m, :], aT[:, m, :], func, bias=shift[:, m:m + 1],
                                         scale=scale[:, m:m + 1]).then_inc(out_a, 1)
            return vector, scalar, out_a

        def turn(name, source, target, blocks=NB):
            ready = sem(name + "_turned")
            done = (sem(name + "_by_act"), sem(name + "_by_dve"))

            def pe_(pe):
                for i in range(blocks):
                    unit_free(pe, i, 4, done)
                    for k in range(KT):
                        last = nc.tensor.transpose(ps[:, i % 4, k * B:(k + 1) * B],
                                                   source[:, i, k * 128:(k + 1) * 128], ident[0:B, 0:B])
                    last.then_inc(ready, 1)

            def unit(i):
                return (target[:, :, i * B:(i + 1) * B],
                        ps[:, i % 4, 0:KT * B].rearrange("p (k b) -> p k b", b=B))

            def act_(act):
                for i in range(0, blocks, 2):
                    act.wait_ge(ready, i + 1)
                    o, s = unit(i)
                    nc.scalar.activation(o, s, ACT.Copy).then_inc(done[0], 1)

            def dve_(dve):
                for i in range(1, blocks, 2):
                    dve.wait_ge(ready, i + 1)
                    o, s = unit(i)
                    nc.vector.tensor_copy(o, s).then_inc(done[1], 1)
            return pe_, act_, dve_, done

        s_padz = sem("pad_halves_zero")

        def store_padded(e, m, c0, cn, bank, f):
            f(e, pad[0:64, 2 * m, c0:c0 + cn], bank[0:64, 0:cn], slice(0, 64))
            return f(e, pad[64:128, 2 * m + 1, c0:c0 + cn], bank[64:128, 0:cn], slice(64, 128))

        def store_qk0(e, u, bank):
            m, c0, cn = MC[u % 12]
            if u < 12:
                return store_padded(e, m, c0, cn, bank, lambda e, o, s, _: copy_by(e, o, s))
            return copy_by(e, aT[:, m, c0:c0 + cn], bank[:, 0:cn])

        def store_qkv0(e, u, bank):
            return store_qk0(e, u, bank) if u < 24 else copy_by(e, vn[:, u - 24, :], bank)

        qkv0 = products("qkv0", turned_units((w[1], hT)) + turned_units((w[0], hT)) + natural_units((w[2], hT)),
                        store_qkv0, "a", banks=4)

        def zero_halves(engine):
            engine.memset(pad[64:128, 0:HEADS:2, :], 0.0).then_inc(s_padz, 1)
            engine.memset(pad[0:64, 1:HEADS:2, :], 0.0).then_inc(s_padz, 1)

        t0_pe, t0_act, t0_dve, turned_by = turn("h0", h0, hT)
        s_out, s_outsum = sem("edges_outside_bands"), sem("edges_outside_summed")
        s_part, s_same, s_before, s_rank, s_sums, s_wsum, e0 = (sem(n) for n in (
            "weight_parts", "same_key", "same_before", "rank", "weights_summed", "weights_stored", "index_steps"))
        BATCHES = TILES // BATCH
        with nc.Block() as block:
            @block.sync
            def _(sp):
                sp.wait_ge(s_keysave, 16)
                for n in range(BATCHES):
                    if n >= 2:
                        sp.wait_ge(s_same, n - 1)
                    flat = keys[n * BATCH * B:(n + 1) * BATCH * B].rearrange("(a b) -> a b", a=1)
                    sp.dma_start(rows[:, n % 2, :, :].rearrange("p a b -> p (a b)"), flat.to_broadcast([B, BATCH * B])).then_inc(s_rows[n % 2], 16)
                each = FILLS // FILL_DMAS
                for j in range(0, FILLS, each):
                    part = table.rearrange("(p r) h -> p (r h)", p=128)[:, j * FILL:(j + each) * FILL]
                    sp.dma_start(part.rearrange("p (f r) -> p f r", f=each),
                                 zeros.rearrange("p (a r) -> p a r", a=1).to_broadcast([128, each, FILL])).then_inc(s_fill, 16)

            @block.gpsimd
            def _(pool):
                zero_halves(nc.gpsimd)

            @block.tensor
            def _(pe):
                def sum_equal_edges(n):
                    if n == 0:
                        pe.wait_ge(s_out, 3)
                        nc.tensor.matmul(ps[0:1, 7, 0:1], e_outside, ones[0:B, 0:1], start=True, stop=True).then_inc(s_outsum, 1)
                        pe.wait_ge(s_part, 5)
                    pe.wait_ge(s_same, n + 1)
                    if n >= 2:
                        pe.wait_ge(s_wsum, n - 1)
                    for t in range(BATCH):
                        last = nc.tensor.matmul(ps[0:B, 4 + n % 2, t * 24:(t + 1) * 24], same[n % 2][:, t, 0:B],
                                                e_parts[:, n * BATCH + t, :, :].rearrange("p h c -> p (h c)"),
                                                start=True, stop=True)
                    last.then_inc(s_sums, 1)

                def before_unit(u):
                    if u == 12:
                        pe.wait_ge(s_w[0], 16)
                    if u == 24:
                        pe.wait_ge(s_w[2], 16)
                    if u >= 5 and (u - 5) % 3 == 0 and (u - 5) // 3 < BATCHES:
                        sum_equal_edges((u - 5) // 3)

                t0_pe(pe)
                for q in turned_by:
                    pe.wait_ge(q, NB // 2)
                pe.wait_ge(s_w[1], 16)
                qkv0[0](pe, before_unit)

            @block.vector
            def _(dve):
                nc.vector.tensor_tensor(e_win[:, 0, :], e_dst, e_bounds[:, 0, :], ALU.is_lt).then_inc(s_out, 1)
                nc.vector.tensor_tensor(e_win[:, 1, :], e_dst, e_bounds[:, 1, :], ALU.is_ge).then_inc(s_out, 1)
                dve.wait_ge(s_out, 2)
                nc.vector.tensor_reduce(e_outside, e_win.rearrange("p a b -> p (a b)"), AX.X, ALU.add).then_inc(s_out, 1)
                t0_dve(dve)
                dve.wait_ge(s_exp, 1)
                for c in range(3):
                    nc.vector.tensor_copy(e_parts[:, :, :, c], e_exp).then_inc(s_part, 1)
                    dve.wait_ge(s_part, 2 * c + 1)
                    if c < 2:
                        nc.vector.tensor_tensor(e_exp, e_exp, e_parts[:, :, :, c], ALU.subtract).then_inc(s_part, 1)
                        dve.wait_ge(s_part, 2 * c + 2)

                def store_sums(n):
                    dve.wait_ge(s_sums, n + 1)
                    nc.vector.tensor_reduce(wsum[:, n * BATCH:(n + 1) * BATCH, :],
                                            ps[0:B, 4 + n % 2, 0:BATCH * 24].rearrange("p (t h c) -> p t h c", h=HEADS, c=3),
                                            AX.X, ALU.add).then_inc(s_wsum, 1)

                for n in range(BATCHES):
                    t0 = n * BATCH
                    dve.wait_ge(s_rows[n % 2], 16 * (n // 2 + 1))
                    if n >= 2:
                        dve.wait_ge(s_sums, n - 1)
                    keycols = e_key[:, t0:t0 + BATCH].rearrange("p (t a) -> p t a", a=1).to_broadcast([B, BATCH, B])
                    nc.vector.tensor_tensor(same[n % 2][:, :, 0:B], rows[:, n % 2, :, :], keycols, ALU.is_equal).then_inc(s_same, 1)
                    dve.wait_ge(s_same, n + 1)
                    if n >= 1:
                        dve.wait_ge(s_rank, n)
                    nc.vector.tensor_tensor(before[:, :, 0:B], same[n % 2][:, :, 0:B],
                                            lower.rearrange("p (a b) -> p a b", a=1).to_broadcast([B, BATCH, B]), ALU.mult).then_inc(s_before, 1)
                    dve.wait_ge(s_before, n + 1)
                    nc.vector.tensor_reduce(e_rank[:, t0:t0 + BATCH], before[:, :, 0:B], AX.X, ALU.add).then_inc(s_rank, 1)
                    if n == 0:
                        dve.wait_ge(s_outsum, 1)
                        nc.vector.tensor_copy(outside, ps[0:1, 7, 0:1]).then_inc(s_out, 1)
                    else:
                        store_sums(n - 1)
                store_sums(BATCHES - 1)
                dve.wait_ge(s_rank, BATCHES)
                nc.vector.tensor_scalar(e_rank, e_rank, 1.0, None, ALU.min).then_inc(e0, 1)
                nc.vector.tensor_scalar(e_src, e_key, -1.0, e_tmp[:, 0:1], ALU.mult, ALU.add).then_inc(e0, 1)
                dve.wait_ge(e0, 2)
                nc.vector.tensor_tensor(e_rank, e_rank, e_src, ALU.mult).then_inc(e0, 1)
                dve.wait_ge(e0, 3)
                nc.vector.tensor_tensor(widx, e_rank, e_key, ALU.add).then_inc(e0, 1)

            @block.scalar
            def _(act):
                t0_act(act)
                qkv0[1](act)
        if stop == "edges":
            with nc.Block() as block:
                @block.sync
                def _(sp):
                    for q, n in ((s_w[0], 16), (s_w[1], 16), (s_par, 64), (s_fill, 16 * FILL_DMAS)):
                        sp.wait_ge(q, n)
            return


        s_scat = sem("weights_scattered")

        scattered = [0]

        def scatter(pool, tiles):
            for t in range(scattered[0], scattered[0] + tiles):
                if t == 0:
                    pool.wait_ge(s_fill, 16 * FILL_DMAS)
                else:
                    pool.wait_ge(s_scat, 16 * t)
                pool.indirect_dma_start(table, bass.IndirectOffsetOnAxis(ap=widx[:, t:t + 1], axis=0), wsum[:, t, :],
                                        None, compute_op=ALU.add).then_inc(s_scat, 16)
            scattered[0] += tiles

        def scatter_in(block, tiles):
            @block.gpsimd
            def _(pool):
                scatter(pool, tiles)

        onehot_src = view(Mem.w, SLOTS, N // 2, p=B).bitcast(BF16)
        onehot_dst = view(Mem.w + SLOTS * N // 2, SLOTS, 64, p=B).bitcast(BF16)
        zero_bf = view(Mem.w + SLOTS * N // 2 + SLOTS * 64, BANK // 2, p=B).bitcast(BF16)
        assert SLOTS * N // 2 + SLOTS * 64 + BANK // 2 <= 3 * KT * D
        s_win = sem("window_targets")
        s_oh = sem("onehot_ready")
        s_ohfree = sem("onehot_free")
        s_cw = sem("window_counted")
        s_cev = sem("window_stored")
        s_zbf = sem("zero_rows")
        blocks_of = [(0, 4), (4, 4), (8, 2)]

        with nc.Block() as block:
            @block.gpsimd
            def _(pool):
                scatter(pool, 12)

            def make_onehots(dve, windows):
                made = 0
                for wd, (first, count) in enumerate(windows):
                    nc.vector.tensor_scalar(e_win[:, wd % 2, :], e_dst, float(-wd * B), None, ALU.add).then_inc(s_win, 1)
                    dve.wait_ge(s_win, wd + 1)
                    unroll = UNROLL[count]
                    with dve.Fori(0, count // unroll) as g:
                        for u in range(unroll):
                            slot = (made + u) % unroll
                            dve.wait_ge(s_ohfree, g * unroll + (made + u + 1))
                            at = bass.ds(g * unroll + (first + u), 1)
                            nc.vector.tensor_scalar(onehot_src[:, slot, :], e_iota, e_srcf[:, at], None, ALU.is_equal)
                            nc.vector.tensor_scalar(onehot_dst[:, slot, 0:B], e_iota[:, 0:B], e_win[:, wd % 2, at], None,
                                                    ALU.is_equal).then_inc(s_oh, 1)
                    made += count

            def count_windows(pe, windows):
                pe.sem_inc(s_ohfree, UNROLL[windows[0][1]])
                used = 0
                for wd, (first, count) in enumerate(windows):
                    base = 3 * (wd % 2)
                    if wd >= 2:
                        pe.wait_ge(s_cev, wd - 1)
                    for j in range(3):
                        nc.tensor.matmul(ps[0:B, base + j, :], zero_bf[:, 0:B], zero_bf[:, 0:BANK],
                                         start=True, stop=False)
                    unroll = UNROLL[count]
                    with pe.Fori(0, count // unroll) as g:
                        for u in range(unroll):
                            slot = (used + u) % unroll
                            pe.wait_ge(s_oh, g * unroll + (used + u + 1))
                            for j, (b0, nb) in enumerate(blocks_of):
                                for i in range(nb):
                                    last = nc.tensor.matmul(ps[0:B, base + j, i * B:(i + 1) * B],
                                                            onehot_src[:, slot, (b0 + i) * B:(b0 + i + 1) * B],
                                                            onehot_dst[:, slot, 0:B], start=False, stop=False,
                                                            skip_group_check=True)
                            last.then_inc(s_ohfree, 1)
                    used += count
                    for j in range(3):
                        last = nc.tensor.matmul(ps[0:B, base + j, :], zero_bf[:, 0:B], zero_bf[:, 0:BANK],
                                                start=False, stop=True)
                    last.then_inc(s_cw, 1)

            @block.vector
            def _(dve):
                nc.vector.memset(zero_bf, 0.0).then_inc(s_zbf, 1)
                found = dve.value_load(outside)
                with dve.If(found < 1):
                    make_onehots(dve, edge_windows(True))
                with dve.Else():
                    make_onehots(dve, edge_windows(False))

            @block.tensor
            def _(pe):
                pe.wait_ge(s_zbf, 1)
                found = pe.value_load(outside)
                with pe.If(found < 1):
                    count_windows(pe, edge_windows(True))
                with pe.Else():
                    count_windows(pe, edge_windows(False))

            @block.scalar
            def _(act):
                for wd in range(NB):
                    act.wait_ge(s_cw, wd + 1)
                    for j, (b0, nb) in enumerate(blocks_of):
                        last = nc.scalar.activation(counts[:, b0:b0 + nb, wd * B:(wd + 1) * B],
                                                    ps[0:B, 3 * (wd % 2) + j, 0:nb * B].rearrange("p (i b) -> p i b", b=B),
                                                    ACT.Copy)
                    last.then_inc(s_cev, 1)
        if stop == "counts":
            with nc.Block() as block:
                @block.sync
                def _(sp):
                    for q, n in ((s_w[0], 16), (s_w[1], 16), (s_w[2], 16), (s_par, 64), (s_fill, 16 * FILL_DMAS)):
                        sp.wait_ge(q, n)
            return
        bn_scale = (view(s0 + 194, KT), view(s0 + 1040, KT))

        probs = view(Mem.probs, 4, N, p=B)
        psums = view(Mem.w, 4, N, p=B)
        s_sc, s_exp0, s_clip, s_mask = (sem(n) for n in ("scores0", "exps0", "clipped0", "masked0"))
        s_pv, s_sum, s_oev, s_z, s_zev, s_norm = (sem(n) for n in ("pv0", "sums0", "output0_stored", "z0", "z0_read", "norm0"))
        LO, HI = 6.737946999085467e-03, 148.4131591025766
        STEPS = PAIRS * NB
        tiles = [(q, q // 2, q % 2) for q in range(2 * STEPS)]

        with nc.Block() as block:
            @block.gpsimd
            def _(pool):
                for q, s, hh in tiles:
                    i, pr = s % NB, s // NB
                    acc = psums[:, (pr % 2) * 2 + hh, :]
                    pool.wait_ge(s_mask, q + 1)
                    if i == 0:
                        if pr >= 2:
                            pool.wait_ge(s_z, 3 * (pr - 1))
                        nc.gpsimd.tensor_scalar(acc, probs[:, q % 4, :], 1.0, 0.0, ALU.mult, ALU.add).then_inc(s_sum, 1)
                    else:
                        pool.wait_ge(s_sum, q - 1)
                        nc.gpsimd.tensor_tensor(acc, acc, probs[:, q % 4, :], ALU.add).then_inc(s_sum, 1)

            @block.tensor
            def _(pe):
                def scores(s):
                    i, pr = s % NB, s // NB
                    for hh in range(2):
                        for c, (c0, cn) in enumerate(CHUNKS):
                            u = 6 * s + 3 * hh + c
                            if u >= 4:
                                pe.wait_ge(s_exp0, u - 3)
                            nc.tensor.matmul(ps[0:B, 3 + u % 4, 0:cn], pad[:, 2 * pr + hh, i * B:(i + 1) * B],
                                             aT[:, pr, c0:c0 + cn], start=True, stop=True).then_inc(s_sc, 1)

                def weighted(s):
                    i, pr = s % NB, s // NB
                    pe.wait_ge(s_mask, 2 * s + 2)
                    if i == 0 and pr >= 1:
                        pe.wait_ge(s_oev, pr)
                    for c, (c0, cn) in enumerate(CHUNKS):
                        for hh in range(2):
                            h = 2 * pr + hh
                            last = nc.tensor.matmul(ps[64 * hh:64 * hh + 64, c, 0:cn], vn[:, i, h * DH:(h + 1) * DH],
                                                    probs[:, (2 * s + hh) % 4, c0:c0 + cn], start=(i == 0), stop=(i == NB - 1))
                    last.then_inc(s_pv, 1)

                def denominators(pr, c):
                    c0, cn = CHUNKS[c]
                    if c == 0:
                        pe.wait_ge(s_sum, 2 * NB * (pr + 1))
                    if pr or c:
                        pe.wait_ge(s_zev, 3 * pr + c)
                    for hh in range(2):
                        last = nc.tensor.matmul(ps[64 * hh:64 * hh + 64, 7, 0:cn], ones[0:B, 0:64],
                                                psums[:, (pr % 2) * 2 + hh, c0:c0 + cn], start=True, stop=True)
                    last.then_inc(s_z, 1)

                scores(0)
                for s in range(STEPS):
                    if s + 1 < STEPS:
                        scores(s + 1)
                    weighted(s)
                    if 3 <= s % NB < 6 and s > NB:
                        denominators(s // NB - 1, s % NB - 3)
                for c in range(3):
                    denominators(PAIRS - 1, c)

            def store_outputs(act, pr):
                act.wait_ge(s_pv, NB * (pr + 1))
                for c, (c0, cn) in enumerate(CHUNKS):
                    last = nc.scalar.activation(aT[:, pr, c0:c0 + cn], ps[:, c, 0:cn], ACT.Copy)
                last.then_inc(s_oev, 1)

            @block.scalar
            def _(act):
                for q, s, hh in tiles:
                    for c, (c0, cn) in enumerate(CHUNKS):
                        act.wait_ge(s_sc, 3 * q + c + 1)
                        if c == 0 and q >= 4:
                            act.wait_ge(s_pv, (q - 4) // 2 + 1)
                            act.wait_ge(s_sum, q - 3)
                        nc.scalar.activation(probs[:, q % 4, c0:c0 + cn], ps[0:B, 3 + (3 * q + c) % 4, 0:cn], ACT.Exp,
                                             scale=SCALE).then_inc(s_exp0, 1)
                    if s % NB == 0 and s > 0 and hh == 1:
                        store_outputs(act, s // NB - 1)
                store_outputs(act, PAIRS - 1)

            @block.vector
            def _(dve):
                def normalise(pr, pieces):
                    for c in pieces:
                        c0, cn = CHUNKS[c]
                        n = 3 * pr + c
                        z = zt[:, n % 2, 0:cn]
                        dve.wait_ge(s_z, n + 1)
                        nc.vector.tensor_scalar(z, ps[:, 7, 0:cn], 1e-6, None, ALU.add).then_inc(s_zev, 1)
                        dve.wait_ge(s_zev, n + 1)
                        nc.vector.reciprocal(z, z).then_inc(s_norm, 1)
                        dve.wait_ge(s_norm, 3 * n + 1)
                        if c == 0:
                            dve.wait_ge(s_oev, pr + 1)
                        nc.vector.tensor_tensor(aT[:, pr, c0:c0 + cn], aT[:, pr, c0:c0 + cn], z, ALU.mult).then_inc(s_norm, 1)
                        dve.wait_ge(s_norm, 3 * n + 2)
                        nc.vector.tensor_tensor(aT[:, pr, c0:c0 + cn], aT[:, pr, c0:c0 + cn], hT[:, pr, c0:c0 + cn],
                                                ALU.add).then_inc(s_norm, 1)

                for q, s, hh in tiles:
                    dve.wait_ge(s_exp0, 3 * q + 3)
                    nc.vector.tensor_scalar(probs[:, q % 4, :], probs[:, q % 4, :], LO, HI, ALU.max, ALU.min).then_inc(s_clip, 1)
                    dve.wait_ge(s_clip, q + 1)
                    nc.vector.tensor_tensor(probs[:, q % 4, :], probs[:, q % 4, :], counts[:, s % NB, :], ALU.mult).then_inc(s_mask, 1)
                    if 4 <= s % NB < 7 and s > NB and hh == 1:
                        normalise(s // NB - 1, [s % NB - 4])
                normalise(PAIRS - 1, range(3))
        if stop == "att0":
            return
        xld = hn
        s_xre, s_wl = sem("x_reloaded"), [sem(f"l1_w{j}_loaded") for j in range(3)]
        s_b2 = sem("b2_loaded")
        b2B = view(Mem.probs + 2 * N, D, p=B)
        deg_units = [[(ones[0:B, :], counts[:, i, c0:c0 + cn]) for i in range(NB)] for c0, cn in CHUNKS]
        deg = products("degree", deg_units,
                       lambda e, u, bank: copy_by(e, cntB[:, CHUNKS[u][0]:CHUNKS[u][0] + CHUNKS[u][1]], bank[:, 0:CHUNKS[u][1]]), "a")
        bn0_v, bn0_s, bn0_done = batch_norm("bn0", bn_scale, ACT.Identity, bn0s[:, 0, :], bn0s[:, 1, :])
        s_deg = sem("degree_steps")
        with nc.Block() as block:
            @block.sync
            def _(sp):
                for i in range(NB):
                    sp.dma_start(xld[:, i, :], x[i * B:(i + 1) * B, :]).then_inc(s_xre, 16)
                for j, a in enumerate((wl1, wr1, wl2)):
                    sp.dma_start(w[j], a.rearrange("(k p) n -> p k n", p=128)).then_inc(s_wl[j], 16)
                sp.dma_start(b2B, b2.to_broadcast([B, D])).then_inc(s_b2, 16)

            @block.gpsimd
            def _(pool):
                scatter(pool, 8)

            @block.tensor
            def _(pe):
                deg[0](pe)

            @block.scalar
            def _(act):
                act.wait_ge(s_par, 64)
                bn0_s(act)
                deg[1](act)
                act.wait_ge(deg[3]["a"], 3)
                nc.scalar.activation(dinvB, cntB, ACT.Sqrt, bias=ones[:, 0:1]).then_inc(s_deg, 1)

            @block.vector
            def _(dve):
                dve.wait_ge(s_par, 64)
                bn0_v(dve)

        def add_x(dest, other):
            def store(e, i, bank):
                return nc.vector.tensor_tensor(dest[:, i, :], bank, other[:, i, :], ALU.add)
            return store

        s_rc = sem("reciprocals")
        tb0 = turn_back("bn0_back", aT, add_x(xn, xld), "d")
        with nc.Block() as block:
            scatter_in(block, 3)

            @block.tensor
            def _(pe):
                tb0[0](pe)

            @block.vector
            def _(dve):
                dve.wait_ge(s_xre, 16 * NB)
                tb0[2](dve)
                nc.vector.tensor_scalar(cntB, cntB, 1.0, None, ALU.max).then_inc(s_rc, 1)
                nc.vector.reciprocal(dinvB, dinvB).then_inc(s_rc, 1)
                dve.wait_ge(s_rc, 2)
                nc.vector.reciprocal(cntB, cntB).then_inc(s_rc, 1)

        ln1_v, ln1_s, ln1_done = layer_norm("ln1", xn, hn)
        with nc.Block() as block:
            scatter_in(block, 6)

            @block.vector
            def _(dve):
                ln1_v(dve)

            @block.scalar
            def _(act):
                ln1_s(act)

        def store_mean(e, u, bank):
            m, c0, cn = MC[u]
            return nc.vector.tensor_tensor(aT[:, m, c0:c0 + cn], bank[:, 0:cn], cntB[:, c0:c0 + cn], ALU.mult)

        t1 = turn("h1", hn, hT)
        g1 = products("mean1", gather_units(hn), store_mean, "d", banks=4, first_bank=4)
        s_b2add = sem("x_plus_b2")
        with nc.Block() as block:
            @block.gpsimd
            def _(pool):
                pool.wait_ge(s_b2, 16)
                for i in range(NB):
                    nc.gpsimd.tensor_tensor(xn[:, i, :], xn[:, i, :], b2B, ALU.add).then_inc(s_b2add, 1)
                scatter(pool, 22)

            @block.tensor
            def _(pe):
                t1[0](pe)
                g1[0](pe)

            @block.scalar
            def _(act):
                t1[1](act)

            @block.vector
            def _(dve):
                t1[2](dve)
                g1[2](dve)

        def store_relu(e, u, bank):
            m, c0, cn = MC[u]
            return nc.scalar.activation(vT[:, m, c0:c0 + cn], bank[:, 0:cn], ACT.Relu, bias=b1s[:, m:m + 1])

        z1 = products("z1", turned_units((w[0], aT), (w[1], hT)), store_relu, "a")
        with nc.Block() as block:
            scatter_in(block, 22)

            @block.tensor
            def _(pe):
                pe.wait_ge(s_wl[0], 16)
                pe.wait_ge(s_wl[1], 16)
                z1[0](pe)

            @block.scalar
            def _(act):
                z1[1](act)

        s_wr2, s_w2 = sem("wr2_loaded"), sem("gcn_w_loaded")
        tb1 = turn_back("z1_back", vT, lambda e, i, bank: copy_by(e, hn[:, i, :], bank), "ad")
        with nc.Block() as block:
            scatter_in(block, 3)

            @block.sync
            def _(sp):
                sp.dma_start(w[0], wr2.rearrange("(k p) n -> p k n", p=128)).then_inc(s_wr2, 16)
                sp.dma_start(w[1], w2.rearrange("(k p) n -> p k n", p=128)).then_inc(s_w2, 16)

            @block.tensor
            def _(pe):
                tb1[0](pe)

            @block.scalar
            def _(act):
                tb1[1](act)

            @block.vector
            def _(dve):
                tb1[2](dve)

        g2 = products("mean2", gather_units(hn), store_mean, "d")
        with nc.Block() as block:
            scatter_in(block, 28)

            @block.tensor
            def _(pe):
                g2[0](pe)

            @block.vector
            def _(dve):
                g2[2](dve)

        x2 = products("x2", natural_units((w[2], aT), (w[0], vT)), add_x(xn, xn), "d")
        with nc.Block() as block:
            scatter_in(block, 23)

            @block.tensor
            def _(pe):
                pe.wait_ge(s_wl[2], 16)
                pe.wait_ge(s_wr2, 16)
                x2[0](pe)

            @block.vector
            def _(dve):
                x2[2](dve)
        if stop == "x2":
            return

        ln2_v, ln2_s, ln2_done = layer_norm("ln2", xn, hn)
        s_dt, s_dc = sem("dinv_turned"), sem("dinv_copied")
        with nc.Block() as block:
            scatter_in(block, 6)

            @block.vector
            def _(dve):
                ln2_v(dve)
                dve.wait_ge(s_dt, 1)
                nc.vector.tensor_copy(dinv, ps[0:B, 0:3, :].rearrange("p a (b c) -> p (a b) c", c=128)[:, 0:NB, 0]).then_inc(s_dc, 1)

            @block.scalar
            def _(act):
                ln2_s(act)

            @block.tensor
            def _(pe):
                for i in range(NB):
                    last = nc.tensor.transpose(ps[0:B, i // 4, (i % 4) * 128:(i % 4) * 128 + 128],
                                               dinvB[:, i * B:(i + 1) * B], ident)
                last.then_inc(s_dt, 1)

        t2 = turn("h2", hn, hT)

        def store_scaled(e, u, bank):
            if e == "a":
                return nc.scalar.activation(vn[:, u, :], bank, ACT.Copy, scale=dinv[:, u:u + 1])
            return nc.vector.tensor_scalar(vn[:, u, :], bank, dinv[:, u:u + 1], None, ALU.mult)

        s_self = sem("self_loops")
        with nc.Block() as block:
            scatter_in(block, 4)

            @block.tensor
            def _(pe):
                t2[0](pe)

            @block.scalar
            def _(act):
                t2[1](act)

            @block.vector
            def _(dve):
                t2[2](dve)
                for i in range(NB):
                    nc.vector.tensor_tensor(counts[:, i, i * B:(i + 1) * B], counts[:, i, i * B:(i + 1) * B],
                                            ident[0:B, 0:B], ALU.add).then_inc(s_self, 1)

        xw = products("xw", natural_units((w[1], hT)), store_scaled, "ad")
        with nc.Block() as block:
            scatter_in(block, 11)

            @block.tensor
            def _(pe):
                pe.wait_ge(s_w2, 16)
                xw[0](pe)

            @block.scalar
            def _(act):
                xw[1](act)

            @block.vector
            def _(dve):
                xw[2](dve)

        def store_gcn(e, u, bank):
            m, c0, cn = MC[u]
            return nc.vector.tensor_tensor(aT[:, m, c0:c0 + cn], bank[:, 0:cn], dinvB[:, c0:c0 + cn], ALU.mult)

        g3 = products("gcn", gather_units(vn), store_gcn, "d")
        s_w3 = [sem(f"l3_w{j}_loaded") for j in range(3)]
        s_gb = sem("gcn_bias")
        with nc.Block() as block:
            scatter_in(block, 22)

            @block.sync
            def _(sp):
                for j, a in enumerate((wq3, wk3, wv3)):
                    sp.dma_start(w[j], a.rearrange("(k p) n -> p k n", p=128)).then_inc(s_w3[j], 16)

            @block.tensor
            def _(pe):
                g3[0](pe)

            @block.vector
            def _(dve):
                g3[2](dve)

        with nc.Block() as block:
            @block.vector
            def _(dve):
                for m in range(KT):
                    nc.vector.tensor_scalar(aT[:, m, :], aT[:, m, :], par2s[:, 0, m:m + 1], None, ALU.add).then_inc(s_gb, 1)

        bn2_v, bn2_s, bn2_done = batch_norm("bn2", bn_scale, ACT.Gelu, par2s[:, 1, :], par2s[:, 2, :])
        s_res = sem("gelu_plus_h2")
        with nc.Block() as block:
            @block.vector
            def _(dve):
                bn2_v(dve)
                for m in range(KT):
                    dve.wait_ge(bn2_done, m + 1)
                    nc.vector.tensor_tensor(aT[:, m, :], aT[:, m, :], hT[:, m, :], ALU.add).then_inc(s_res, 1)

            @block.scalar
            def _(act):
                bn2_s(act)

        tb2 = turn_back("gcn_back", aT, add_x(xn, xn), "d")
        with nc.Block() as block:
            @block.tensor
            def _(pe):
                tb2[0](pe)

            @block.vector
            def _(dve):
                tb2[2](dve)
        if stop == "x3":
            with nc.Block() as block:
                @block.sync
                def _(sp):
                    for q in s_w3:
                        sp.wait_ge(q, 16)
            return

        bv3B = view(Mem.probs, D, p=B)
        bo3B = view(Mem.probs + D, D, p=B)
        s_b3, s_bo, s_xs = sem("b3_loaded"), sem("x_plus_bo"), sem("x_saved_sem")
        ln3_v, ln3_s, ln3_done = layer_norm("ln3", xn, hn)
        with nc.Block() as block:
            @block.sync
            def _(sp):
                sp.dma_start(bv3B, bv3.to_broadcast([B, D])).then_inc(s_b3, 16)
                sp.dma_start(bo3B, bo3.to_broadcast([B, D])).then_inc(s_b3, 16)

            @block.vector
            def _(dve):
                ln3_v(dve)
                nc.vector.tensor_scalar(bqs, par3s[:, 0, :], -SCALE, None, ALU.mult)

            @block.scalar
            def _(act):
                ln3_s(act)

        t3 = turn("h3", hn, hT)
        with nc.Block() as block:
            @block.gpsimd
            def _(pool):
                pool.wait_ge(s_b3, 32)
                for i in range(NB):
                    nc.gpsimd.tensor_tensor(xn[:, i, :], xn[:, i, :], bo3B, ALU.add).then_inc(s_bo, 1)

            @block.sync
            def _(sp):
                for i in range(NB):
                    sp.wait_ge(s_bo, i + 1)
                    sp.dma_start(xsave[i * B:(i + 1) * B, :], xn[:, i, :]).then_inc(s_xs, 16)
                sp.wait_ge(s_xs, 16 * NB)

            @block.tensor
            def _(pe):
                t3[0](pe)

            @block.scalar
            def _(act):
                t3[1](act)

            @block.vector
            def _(dve):
                t3[2](dve)

        def store_qk3(e, u, bank):
            m, c0, cn = MC[u % 12]

            def scaled(e, o, s, rows):
                if e == "a":
                    return nc.scalar.activation(o, s, ACT.Identity, bias=bqs[rows, m:m + 1], scale=-SCALE)
                return nc.vector.tensor_scalar(o, s, par3s[rows, 0, m:m + 1], -SCALE, ALU.add, ALU.mult)
            if u < 12:
                return store_padded(e, m, c0, cn, bank, scaled)
            if e == "a":
                return nc.scalar.activation(aT[:, m, c0:c0 + cn], bank[:, 0:cn], ACT.Identity, bias=par3s[:, 1, m:m + 1])
            return nc.vector.tensor_scalar(aT[:, m, c0:c0 + cn], bank[:, 0:cn], par3s[:, 1, m:m + 1], None, ALU.add)

        qk3 = products("qk3", turned_units((w[0], hT)) + turned_units((w[1], hT)), store_qk3, "ad", banks=4)
        v3 = products("v3", natural_units((w[2], hT)), lambda e, u, bank: nc.vector.tensor_tensor(
            vn[:, u, :], bank, bv3B, ALU.add), "d", banks=4, first_bank=4)
        with nc.Block() as block:
            @block.tensor
            def _(pe):
                for q in s_w3:
                    pe.wait_ge(q, 16)
                qk3[0](pe)
                v3[0](pe)

            @block.scalar
            def _(act):
                qk3[1](act)

            @block.vector
            def _(dve):
                zero_halves(nc.vector)
                qk3[2](dve)
                v3[2](dve)

        weights = [view(a, N * HEADS, p=B).rearrange("p (t h) -> p t h", h=HEADS) for a in Mem.weights]
        pslot = [view(a, N, p=B) for a in (Mem.probs3, Mem.probs3 + N, Mem.probs3b, Mem.probs3b + N)]
        wo = w[0]
        masks = [view(Mem.masks + j * N // 2, N // 2, p=B).bitcast(BF16) for j in range(2)]
        turnedp = [view(Mem.turned + 4 * j * B, 4, B, p=B) for j in range(4)]
        yT = [view(Mem.yT + j * KT * B, KT, B) for j in range(2)]
        xb = view(Mem.xb, D, p=B)
        GROUPS = [(0, 4), (4, 4), (8, 2)]
        s_tab = [sem(f"table_loaded{j}") for j in range(2)]
        s_wo, s_mask3 = sem("wo_loaded"), sem("masks3")
        s_qk, s_max, s_e3, s_wt, s_rd, s_p3 = (sem(n) for n in (
            "scores3", "masked3", "exps3", "weighted3", "recip_den3", "probs3"))
        s_tp, s_tps, s_y, s_ys, s_o, s_ob, s_xb, s_out = (sem(n) for n in (
            "probs_turned", "turned_stored", "y3", "y3_stored", "out3", "out3_added", "x_row_loaded", "out_stored"))
        HT = NB * HEADS

        SB, TB = 3, 3

        with nc.Block() as block:
            @block.sync
            def _(sp):
                assert scattered[0] == TILES
                sp.wait_ge(s_scat, 16 * TILES)
                sp.dma_start(wo, wo3.rearrange("(k p) n -> p k n", p=128)).then_inc(s_wo, 16)
                rows = table[0:N * N, :].rearrange("(s t) h -> s (t h)", t=N)

                def load(i):
                    if i >= 2:
                        sp.wait_ge(s_wt, HEADS * (i - 1))
                        sp.wait_ge(s_mask3, HEADS * (i - 1))
                    for a, b in ((0, 112), (112, B)):
                        sp.dma_start(weights[i % 2][a:b].rearrange("p t h -> p (t h)"), rows[i * B + a:i * B + b, :]).then_inc(s_tab[i % 2], 16)
                load(0)
                load(1)
                sp.dma_start(xb, xsave[0:B, :]).then_inc(s_xb, 16)
                for i in range(NB):
                    if i + 2 < NB:
                        load(i + 2)
                    sp.wait_ge(s_ob, i + 1)
                    sp.dma_start(out[i * B:(i + 1) * B, :], xb).then_inc(s_out, 16)
                    if i + 1 < NB:
                        sp.wait_ge(s_out, 16 * (i + 1))
                        sp.dma_start(xb, xsave[(i + 1) * B:(i + 2) * B, :]).then_inc(s_xb, 16)
                sp.wait_ge(s_out, 16 * NB)

            @block.gpsimd
            def _(pool):
                for q in range(HT):
                    pool.wait_ge(s_rd, q + 1)
                    nc.gpsimd.tensor_scalar(pslot[q % 4], pslot[q % 4], rden[:, q % 4:q % 4 + 1], 1.0,
                                            ALU.mult, ALU.mult).then_inc(s_p3, 1)

            @block.tensor
            def _(pe):
                def scores(q):
                    i, h = divmod(q, HEADS)
                    for c, (c0, cn) in enumerate(CHUNKS):
                        u = 3 * q + c
                        if u >= SB:
                            pe.wait_ge(s_max, u - SB + 1)
                        nc.tensor.matmul(ps[0:B, u % SB, 0:cn], pad[:, h, i * B:(i + 1) * B], aT[:, h // 2, c0:c0 + cn],
                                         start=True, stop=True).then_inc(s_qk, 1)

                def turn_and_weigh(i, pr):
                    q0 = i * HEADS + 2 * pr
                    for g, (j0, nj) in enumerate(GROUPS):
                        for hh in range(2):
                            n = q0 // 2 * 6 + 2 * g + hh
                            if g == 0:
                                pe.wait_ge(s_p3, q0 + hh + 1)
                            if n >= TB:
                                pe.wait_ge(s_tps, n - TB + 1)
                            for j in range(nj):
                                last = nc.tensor.transpose(ps[0:B, SB + n % TB, j * B:(j + 1) * B],
                                                           pslot[(q0 + hh) % 4][:, (j0 + j) * B:(j0 + j + 1) * B],
                                                           ident[0:B, 0:B])
                            last.then_inc(s_tp, 1)
                        if g >= 1:
                            weigh(i, pr, g - 1)

                def weigh(i, pr, g):
                    q0 = i * HEADS + 2 * pr
                    j0, nj = GROUPS[g]
                    n = q0 // 2 * 6 + 2 * g
                    pe.wait_ge(s_tps, n + 2)
                    if pr == 0 and g == 0 and i >= 1:
                        pe.wait_ge(s_ys, i)
                    for j in range(nj):
                        for hh in range(2):
                            h = 2 * pr + hh
                            last = nc.tensor.matmul(ps[64 * hh:64 * hh + 64, 6, pr * B:(pr + 1) * B],
                                                    vn[:, j0 + j, h * DH:(h + 1) * DH], turnedp[(n + hh) % 4][:, j, :],
                                                    start=(pr == 0 and j0 + j == 0), stop=(pr == PAIRS - 1 and j0 + j == NB - 1),
                                                    skip_group_check=True)
                    last.then_inc(s_y, 1)

                def project(i):
                    pe.wait_ge(s_ys, i + 1)
                    if i >= 1:
                        pe.wait_ge(s_ob, i)
                    for k in range(KT):
                        last = nc.tensor.matmul(ps[0:B, 7, :], yT[i % 2][:, k, :], wo[:, k, :], start=(k == 0), stop=(k == KT - 1))
                    last.then_inc(s_o, 1)

                pe.wait_ge(s_wo, 16)
                scores(0)
                scores(1)
                for s in range(NB * PAIRS):
                    i, pr = divmod(s, PAIRS)
                    if s + 1 < NB * PAIRS:
                        scores(2 * s + 2)
                    if s >= 1:
                        weigh(*divmod(s - 1, PAIRS), 2)
                    if s + 1 < NB * PAIRS:
                        scores(2 * s + 3)
                    turn_and_weigh(i, pr)
                    if pr == 1 and i >= 1:
                        project(i - 1)
                weigh(NB - 1, PAIRS - 1, 2)
                project(NB - 1)

            @block.scalar
            def _(act):
                def exps(q):
                    act.wait_ge(s_max, 3 * q + 3)
                    nc.scalar.activation(pslot[q % 4], pslot[q % 4], ACT.Exp, bias=mx[:, q % 4, 2:3], scale=-1.0).then_inc(s_e3, 1)

                def store_turned(s, g):
                    j0, nj = GROUPS[g]
                    for hh in range(2):
                        n = 6 * s + 2 * g + hh
                        act.wait_ge(s_tp, n + 1)
                        if n >= 4:
                            act.wait_ge(s_y, (n - 4) // 2 + 1)
                        nc.scalar.activation(turnedp[n % 4][:, 0:nj, :], ps[0:B, SB + n % TB, 0:nj * B].rearrange("p (j b) -> p j b", b=B),
                                             ACT.Copy).then_inc(s_tps, 1)

                def store_y(i):
                    act.wait_ge(s_y, 12 * (i + 1))
                    if i >= 2:
                        act.wait_ge(s_o, i - 1)
                    nc.scalar.activation(yT[i % 2], ps[:, 6, 0:KT * B].rearrange("p (k b) -> p k b", b=B), ACT.Copy).then_inc(s_ys, 1)

                exps(0)
                exps(1)
                for s in range(NB * PAIRS):
                    i, pr = divmod(s, PAIRS)
                    more = s + 1 < NB * PAIRS
                    if more:
                        exps(2 * s + 2)
                    if pr == 0 and i >= 1:
                        store_y(i - 1)
                    store_turned(s, 0)
                    store_turned(s, 1)
                    if more:
                        exps(2 * s + 3)
                    store_turned(s, 2)
                store_y(NB - 1)

            @block.vector
            def _(dve):
                def mask(q):
                    i, h = divmod(q, HEADS)
                    if h == 0:
                        dve.wait_ge(s_tab[i % 2], 32 * (i // 2 + 1))
                    if q >= 2:
                        dve.wait_ge(s_max, 3 * (q - 1))
                    nc.vector.tensor_scalar(masks[q % 2], weights[i % 2][:, :, h], 0.0, EMPTY,
                                            ALU.is_le, ALU.mult).then_inc(s_mask3, 1)

                def masked(q):
                    dve.wait_ge(s_mask3, q + 1)
                    if q >= 4:
                        dve.wait_ge(s_tp, ((q - 4) // 2) * 6 + 6)
                        dve.wait_ge(s_p3, q - 3)
                    for c, (c0, cn) in enumerate(CHUNKS):
                        dve.wait_ge(s_qk, 3 * q + c + 1)
                        if c:
                            dve.wait_ge(s_max, 3 * q + c)
                        nc.vector.tensor_tensor_reduce(pslot[q % 4][:, c0:c0 + cn], ps[0:B, (3 * q + c) % SB, 0:cn], masks[q % 2][:, c0:c0 + cn],
                                                       1.0, mx[:, q % 4, c - 1:c] if c else CEILING, ALU.add, ALU.min,
                                                       mx[:, q % 4, c:c + 1]).then_inc(s_max, 1)

                def weigh(q):
                    i, h = divmod(q, HEADS)
                    dve.wait_ge(s_e3, q + 1)
                    nc.vector.tensor_tensor_reduce(pslot[q % 4], pslot[q % 4], weights[i % 2][:, :, h], 1.0, NOTHING,
                                                   ALU.mult, ALU.add, den[:, q % 4:q % 4 + 1]).then_inc(s_wt, 1)
                    dve.wait_ge(s_wt, q + 1)
                    nc.vector.reciprocal(rden[:, q % 4:q % 4 + 1], den[:, q % 4:q % 4 + 1]).then_inc(s_rd, 1)

                def add_out(i):
                    dve.wait_ge(s_o, i + 1)
                    dve.wait_ge(s_xb, 16 * (i + 1))
                    nc.vector.tensor_tensor(xb, ps[0:B, 7, :], xb, ALU.add).then_inc(s_ob, 1)

                mask(0)
                for q in range(HT):
                    masked(q)
                    if q + 1 < HT:
                        mask(q + 1)
                    if q % 2:
                        weigh(q - 1)
                        weigh(q)
                    i, h = divmod(q, HEADS)
                    if h == 6 and i >= 1:
                        add_out(i - 1)
                add_out(NB - 1)


def layout(x, src, dst, edge_attr_8, **p):
    import numpy as np

    def cols(*vectors):
        return np.concatenate([np.asarray(v).reshape(KT, 128).T for v in vectors], axis=1)

    return {
        "x": x, "src": src.reshape(TILES, B).T, "dst": dst.reshape(TILES, B).T,
        "bounds": np.asarray(tile_bounds(), np.float32).reshape(1, 2 * TILES),
        "srcrow": src.reshape(TILES // 2, 2 * B), "dstrow": dst.reshape(TILES // 2, 2 * B),
        "attr": edge_attr_8.reshape(TILES, B, HEADS).transpose(1, 0, 2).reshape(B, TILES * HEADS),
        "wq0": p["L0_gnn_Wq"], "wk0": p["L0_gnn_Wk"], "wv0": p["L0_gnn_Wv"],
        "bn0": cols(p["L0_gnn_bn_gamma"], p["L0_gnn_bn_beta"]),
        "wl1": p["L1_gnn_Wl1"].T, "wr1": p["L1_gnn_Wr1"].T, "b1": cols(p["L1_gnn_b1"]),
        "wl2": p["L1_gnn_Wl2"].T, "wr2": p["L1_gnn_Wr2"].T, "b2": p["L1_gnn_b2"].reshape(1, D),
        "w2": p["L2_gnn_W"].T, "par2": cols(p["L2_gnn_b"], p["L2_gnn_gamma"], p["L2_gnn_beta"]),
        "wq3": p["L3_gnn_Wq"], "wk3": p["L3_gnn_Wk"], "wv3": p["L3_gnn_Wv"], "wo3": p["L3_gnn_Wo"],
        "par3": cols(p["L3_gnn_bq"], p["L3_gnn_bk"]), "bv3": p["L3_gnn_bv"].reshape(1, D),
        "bo3": p["L3_gnn_bo"].reshape(1, D),
    }


def kernel(**inputs):
    import numpy as np
    import concourse.bacc as bacc
    from concourse.bass_utils import run_bass_kernel_spmd

    nc = bacc.Bacc("TRN2", target_bir_lowering=False, num_devices=1)
    arrays, args = {}, {}
    for name, a in layout(**{k: np.asarray(v) for k, v in inputs.items()}).items():
        a = np.ascontiguousarray(a)
        arrays[f"in_{name}"] = a
        args[name] = nc.dram_tensor(f"in_{name}", a.shape, mybir.dt.from_np(a.dtype), kind="ExternalInput").ap()
    out = nc.dram_tensor("out_x", (N, D), F32, kind="ExternalOutput").ap()
    table = nc.dram_tensor("edge_weights", (TABLE_ROWS, HEADS), F32, kind="Internal").ap()
    xsave = nc.dram_tensor("x_saved", (N, D), F32, kind="Internal").ap()
    keys = nc.dram_tensor("edge_keys_row", (EDGES,), F32, kind="Internal").ap()
    graph_kernel(nc, **args, out=out, table=table, xsave=xsave, keys=keys)
    r = run_bass_kernel_spmd(nc, [arrays], core_ids=[0])
    return r.results[0]["out_x"]
```

```python
from contextlib import ExitStack

import concourse.bass as bass
from concourse import mybir

ALU = mybir.AluOpType
ACT = mybir.ActivationFunctionType
AX = mybir.AxisListType
F32 = mybir.dt.float32
BF16 = mybir.dt.bfloat16
F16 = mybir.dt.float16
I32 = mybir.dt.int32

N = 1250
D = 512
HEADS = 8
DH = D // HEADS
PAIRS = HEADS // 2
B = 125
NB = N // B
EDGES = 21250
TILES = EDGES // B
KT = D // 128
CHUNKS = [(0, 417), (417, 417), (834, 416)]
BANK = 512
EPS = 1e-5
EMPTY = 1e10
NOTHING = 1e-30
CEILING = 1e9
SCALE = DH ** -0.5
TABLE_ROWS = 128 * 12216
BATCH = 17
BAND = 21
BAND_MARGIN = 2
UNROLL = {BAND: 7, TILES: 5}
SLOTS = max(UNROLL.values())


class Mem:
    counts = 0
    hT = counts + NB * N
    probs = hT + KT * N
    cntB = probs
    dinvB = probs + N
    weights = (0, N * HEADS)
    probs3 = 2 * N * HEADS
    pad = probs + 4 * N
    xn = pad
    hn = pad + NB * D
    aT = pad + 2 * NB * D
    v = aT + KT * N
    w = v + NB * D
    wsum = w + 3 * KT * D
    widx = wsum + TILES * HEADS
    ident = widx + TILES
    ones = ident + 128
    small = ones + 128
    end = small + 1150
    masks = w + KT * D
    probs3b = masks + N
    yT = probs3b + 2 * N
    xb = yT + 2 * KT * 125
    turned = small + 200
    zeros = small + 1048
    end = turned + 4 * 500
    assert xb + D <= ident


def edge_windows(banded):
    if not banded:
        return [(0, TILES)] * NB
    return [(min(max(w * TILES // NB - BAND_MARGIN, 0), TILES - BAND), BAND) for w in range(NB)]


def tile_bounds():
    over = [[w for w, (first, count) in enumerate(edge_windows(True)) if first <= t < first + count]
            for t in range(TILES)]
    return [[o[0] * B for o in over], [(o[-1] + 1) * B for o in over]]


def graph_kernel(nc, x, src, dst, bounds, srcrow, dstrow, attr, wq0, wk0, wv0, bn0, wl1, wr1, b1, wl2, wr2, b2, w2, par2,
                 wq3, wk3, wv3, wo3, par3, bv3, bo3, out, table, xsave, keys, stop=None):
    with ExitStack() as ctx:
        mem = ctx.enter_context(nc.sbuf_tensor("mem", [128, Mem.end], F32))
        ps = ctx.enter_context(nc.psum_tensor("ps", [128, 8, BANK], F32))

        def sem(name):
            return ctx.enter_context(nc.semaphore(name))

        def view(at, *shape, p=128):
            size = 1
            for s in shape:
                size *= s
            v = mem[0:p, at:at + size]
            if len(shape) == 1:
                return v
            names = " ".join("abc"[:len(shape)])
            return v.rearrange(f"p ({names}) -> p {names}", **dict(zip("abc", shape)))

        counts = view(Mem.counts, NB, N, p=B)
        hT = view(Mem.hT, KT, N)
        pad = view(Mem.pad, HEADS, N)
        xn = view(Mem.xn, NB, D, p=B)
        hn = view(Mem.hn, NB, D, p=B)
        aT = view(Mem.aT, KT, N)
        vT = view(Mem.v, KT, N)
        vn = view(Mem.v, NB, D, p=B)
        w = [view(Mem.w + j * KT * D, KT, D) for j in range(3)]
        wsum = view(Mem.wsum, TILES, HEADS, p=B)
        widx = view(Mem.widx, TILES, p=B).bitcast(I32)
        ident = view(Mem.ident, 128)
        ones = view(Mem.ones, 128)
        cntB = view(Mem.cntB, N)
        dinvB = view(Mem.dinvB, N)
        s0 = Mem.small
        st = view(s0, 12, 6)
        mv = view(s0 + 72, NB, 2)
        sd = view(s0 + 92, NB)
        rstd = view(s0 + 102, NB)
        nmr = view(s0 + 112, NB)
        epst = view(s0 + 122, 1)
        dinv = view(s0 + 124, NB, p=B)
        bn0s = view(s0 + 134, 2, KT)
        b1s = view(s0 + 142, KT)
        par2s = view(s0 + 146, 3, KT)
        par3s = view(s0 + 158, 2, KT)
        mx = view(s0 + 166, 4, 3, p=B)
        den = view(s0 + 182, 4, p=B)
        rden = view(s0 + 186, 4, p=B)
        bqs = view(s0 + 190, KT)
        zt = view(s0 + 200, 2, 417)

        def norm_and_turn(name, xin, hout, arrive, produce=None, ahead=3, turn_banks=(4, 4)):
            stats, aggr, root, inv, done, turned, stored = (sem(f"{name}_{n}") for n in (
                "stats", "mean_var", "root", "inverse", "normed", "turned", "turned_stored"))
            bank0, banks = turn_banks

            def vector(dve):
                def inverse(i, part):
                    if part == 0:
                        dve.wait_ge(root, i + 1)
                        nc.vector.reciprocal(rstd[0:B, i:i + 1], sd[0:B, i:i + 1]).then_inc(inv, 1)
                    else:
                        dve.wait_ge(inv, 2 * i + 1)
                        nc.vector.scalar_tensor_tensor(out=nmr[0:B, i:i + 1], in0=mv[0:B, i, 0:1], scalar=-1.0,
                                                       in1=rstd[0:B, i:i + 1], op0=ALU.mult, op1=ALU.mult).then_inc(inv, 1)
                for i in range(NB):
                    arrive(dve, i)
                    nc.vector.bn_stats(st[0:B, i, :], xin[:, i, :]).then_inc(stats, 1)
                    if i >= 1:
                        inverse(i - 1, 0)
                    dve.wait_ge(stats, i + 1)
                    nc.vector.bn_aggr(mv[0:B, i, :], st[0:B, i, :]).then_inc(aggr, 1)
                    if i >= 1:
                        inverse(i - 1, 1)
                inverse(NB - 1, 0)
                inverse(NB - 1, 1)

            def scalar(act):
                def norm(i):
                    act.wait_ge(inv, 2 * i + 2)
                    nc.scalar.activation(hout[:, i, :], xin[:, i, :], ACT.Relu, bias=nmr[0:B, i:i + 1],
                                         scale=rstd[0:B, i:i + 1]).then_inc(done, 1)

                def store(i):
                    act.wait_ge(turned, i + 1)
                    nc.scalar.activation(hT[:, :, i * B:(i + 1) * B],
                                         ps[:, bank0 + i % banks, 0:KT * B].rearrange("p (k b) -> p k b", b=B),
                                         ACT.Copy).then_inc(stored, 1)
                for i in range(NB):
                    act.wait_ge(aggr, i + 1)
                    nc.scalar.activation(sd[0:B, i:i + 1], mv[0:B, i, 1:2], ACT.Sqrt, bias=epst[0:B, :]).then_inc(root, 1)
                    if i >= 1:
                        norm(i - 1)
                    if i >= ahead + 1:
                        store(i - ahead - 1)
                norm(NB - 1)
                for i in range(NB - ahead - 1, NB):
                    store(i)

            def tensor(pe):
                def turn(i):
                    pe.wait_ge(done, i + 1)
                    if i >= banks:
                        pe.wait_ge(stored, i - banks + 1)
                    for k in range(KT):
                        last = nc.tensor.transpose(ps[:, bank0 + i % banks, k * B:(k + 1) * B],
                                                   hout[:, i, k * 128:(k + 1) * 128], ident[0:B, 0:B])
                    last.then_inc(turned, 1)
                for i in range(NB + ahead):
                    if i < NB and produce:
                        produce(pe, i)
                    if i >= ahead:
                        turn(i - ahead)

            return vector, scalar, tensor, done, stored

        s_x = [sem(f"x{j}_loaded") for j in range(NB // 2)]
        s_edges = sem("edges_loaded")
        s_attr = sem("attr_loaded")
        s_w = [sem(f"w{j}_loaded") for j in range(3)]
        s_par = sem("parameters_loaded")
        s_const = sem("constants")
        s_key = sem("edge_keys")
        s_exp = sem("edge_weights_ready")
        s_zero = sem("zeros_ready")
        s_keysave, s_rows = sem("keys_saved"), [sem(f"key_rows_loaded{j}") for j in range(2)]
        s_fill = sem("table_zeroed")
        E = Mem.probs
        e_int = view(E, 2, TILES, p=B).bitcast(I32)
        e_src = view(E + 2 * TILES, TILES, p=B)
        e_dst = view(E + 3 * TILES, TILES, p=B)
        e_key = view(E + 4 * TILES, TILES, p=B)
        e_rank = view(E + 5 * TILES, TILES, p=B)
        e_tmp = view(E + 6 * TILES, TILES, p=B)
        e_win = view(E + 7 * TILES, 2, TILES, p=B)
        e_srcf = view(E + 9 * TILES, TILES, p=B)
        e_bounds = view(E + 10 * TILES, 2, TILES, p=B)
        e_dummy = view(E + 12 * TILES, 1, p=B)
        e_rowkey = view(E + 12 * TILES + 2, 4, 2 * B, p=TILES // 2)
        lower = view(E + 12 * TILES + 2 + 8 * B, 64, p=B).bitcast(BF16)[:, 0:B]
        e_iota = view(E + 12 * TILES + 2 + 8 * B + 64, N // 2, p=B).bitcast(F16)
        assert E + 12 * TILES + 2 + 8 * B + 64 + N // 2 <= Mem.pad
        e_outside = view(s0 + 194, 1, p=B)
        outside = view(s0 + 195, 1, p=1).bitcast(I32)
        rows = view(Mem.counts, 2, BATCH, B, p=B)
        at = Mem.counts + 2 * BATCH * B
        same = [view(at + j * BATCH * 64, BATCH, 64, p=B).bitcast(BF16) for j in range(2)]
        before = view(at + 2 * BATCH * 64, BATCH, 64, p=B).bitcast(BF16)
        at += 3 * BATCH * 64
        e_parts = view(at, TILES * HEADS * 3 // 2, p=B).bitcast(BF16)
        e_parts = e_parts.rearrange("p (t h c) -> p t h c", h=HEADS, c=3)
        e_exp = view(at + TILES * HEADS * 3 // 2, TILES, HEADS, p=B)
        assert at + TILES * HEADS * 5 // 2 <= Mem.hT
        h0 = vn
        FILLS = 96
        FILL = TABLE_ROWS * HEADS // 128 // FILLS
        FILL_DMAS = 12
        zeros = view(Mem.zeros, FILL)

        def x_block_loaded(dve, i):
            if i % 2 == 0:
                dve.wait_ge(s_x[i // 2], 16)

        ln0_v, ln0_s, ln0_pe, _, h0_turned = norm_and_turn("ln0", h0, h0, x_block_loaded, ahead=1)
        with nc.Block() as block:
            @block.sync
            def _(sp):
                sp.dma_start(e_int[:, 0, :], src).then_inc(s_edges, 16)
                sp.dma_start(e_int[:, 1, :], dst).then_inc(s_edges, 16)
                sp.dma_start(e_rowkey[:, 0, :].bitcast(I32), srcrow).then_inc(s_edges, 16)
                sp.dma_start(e_rowkey[:, 1, :].bitcast(I32), dstrow).then_inc(s_edges, 16)
                sp.dma_start(e_bounds.rearrange("p a b -> p (a b)"), bounds.to_broadcast([B, 2 * TILES])).then_inc(s_edges, 16)
                for j in range(NB // 2):
                    pair = x[2 * j * B:(2 * j + 2) * B, :].rearrange("(a p) d -> p a d", p=B)
                    sp.dma_start(h0[:, 2 * j:2 * j + 2, :], pair).then_inc(s_x[j], 16)
                sp.dma_start(e_exp.rearrange("p a b -> p (a b)"), attr).then_inc(s_attr, 16)
                for j, a in ((1, wk0), (0, wq0), (2, wv0)):
                    sp.dma_start(w[j], a.rearrange("(k p) n -> p k n", p=128)).then_inc(s_w[j], 16)
                for a, b in ((bn0s, bn0), (par2s, par2), (par3s, par3)):
                    sp.dma_start(a.rearrange("p a b -> p (a b)"), b).then_inc(s_par, 16)
                sp.dma_start(b1s, b1).then_inc(s_par, 16)
                sp.wait_ge(s_key, 7)
                sp.dma_start(keys.rearrange("(t b) -> t b", t=TILES // 2), e_rowkey[:, 0, :]).then_inc(s_keysave, 16)

            @block.gpsimd
            def _(pool):
                nc.gpsimd.memset(ident[:], 0.0).then_inc(s_const, 1)
                nc.gpsimd.memset(ones[:], 1.0).then_inc(s_const, 1)
                nc.gpsimd.memset(lower[:], 1.0).then_inc(s_const, 1)
                nc.gpsimd.memset(epst[:], EPS).then_inc(s_const, 1)
                pool.wait_ge(s_const, 4)
                nc.gpsimd.affine_select(out=ident[:], in_=ident[:], compare_op=ALU.not_equal, fill=1.0, base=0,
                                        pattern=[[-1, 128]], channel_multiplier=1).then_inc(s_const, 1)
                nc.gpsimd.affine_select(out=lower[:], in_=lower[:], compare_op=ALU.is_gt, fill=0.0, base=0,
                                        pattern=[[-1, B]], channel_multiplier=1).then_inc(s_const, 1)
                nc.gpsimd.iota(e_dummy.bitcast(I32), pattern=[[0, 1]], base=N * N, channel_multiplier=1).then_inc(s_const, 1)
                nc.gpsimd.iota(e_iota, pattern=[[1, N]], base=0, channel_multiplier=0,
                               allow_small_or_imprecise_dtypes=True).then_inc(s_const, 1)

            @block.vector
            def _(dve):
                nc.vector.memset(zeros, 0.0).then_inc(s_zero, 1)
                dve.wait_ge(s_const, 8)
                dve.wait_ge(s_edges, 80)
                nc.vector.tensor_copy(e_srcf, e_int[:, 0, :]).then_inc(s_key, 1)
                nc.vector.tensor_copy(e_dst, e_int[:, 1, :]).then_inc(s_key, 1)
                dve.wait_ge(s_key, 2)
                nc.vector.scalar_tensor_tensor(out=e_key, in0=e_srcf, scalar=float(N), in1=e_dst,
                                               op0=ALU.mult, op1=ALU.add).then_inc(s_key, 1)
                nc.vector.tensor_copy(e_tmp[:, 0:1], e_dummy.bitcast(I32)).then_inc(s_key, 1)
                for j in range(2):
                    nc.vector.tensor_copy(e_rowkey[:, 2 + j, :], e_rowkey[:, j, :].bitcast(I32)).then_inc(s_key, 1)
                dve.wait_ge(s_key, 6)
                nc.vector.scalar_tensor_tensor(out=e_rowkey[:, 0, :], in0=e_rowkey[:, 2, :], scalar=float(N),
                                               in1=e_rowkey[:, 3, :], op0=ALU.mult, op1=ALU.add).then_inc(s_key, 1)
                ln0_v(dve)

            @block.tensor
            def _(pe):
                pe.wait_ge(s_const, 8)
                ln0_pe(pe)

            @block.scalar
            def _(act):
                act.wait_ge(s_const, 8)
                ln0_s(act)
                act.wait_ge(s_attr, 16)
                nc.scalar.activation(e_exp, e_exp, ACT.Exp).then_inc(s_exp, 1)

        def products(name, units, store, by, banks=8, first_bank=0):
            ready = sem(name + "_ready")
            done = {e: sem(f"{name}_stored_{e}") for e in set(by)}

            def engine_of(u):
                return by[u % len(by)]

            def stored(u):
                return sum(engine_of(v) == engine_of(u) for v in range(u + 1))

            def bank(u):
                return ps[0:units[u][0][0].shape[-1], first_bank + u % banks, :]

            def pe_(pe, before=None):
                for u, pairs in enumerate(units):
                    if before:
                        before(u)
                    if u >= banks:
                        pe.wait_ge(done[engine_of(u - banks)], stored(u - banks))
                    for j, (left, right) in enumerate(pairs):
                        last = nc.tensor.matmul(bank(u)[:, 0:right.shape[-1]], left, right,
                                                start=(j == 0), stop=(j == len(pairs) - 1))
                    last.then_inc(ready, 1)

            def run(letter):
                def go(eng):
                    for u in range(len(units)):
                        if engine_of(u) == letter:
                            eng.wait_ge(ready, u + 1)
                            store(letter, u, bank(u)).then_inc(done[letter], 1)
                return go
            return pe_, run("a"), run("d"), done, ready

        def copy_by(letter, o, s):
            return nc.scalar.activation(o, s, ACT.Copy) if letter == "a" else nc.vector.tensor_copy(o, s)

        MC = [(m, c0, cn) for m in range(KT) for c0, cn in CHUNKS]

        def turned_units(*terms):
            return [[(wt[:, k, m * 128:(m + 1) * 128], inp[:, k, c0:c0 + cn]) for wt, inp in terms for k in range(KT)]
                    for m, c0, cn in MC]

        def natural_units(*terms):
            return [[(inp[:, k, i * B:(i + 1) * B], wt[:, k, :]) for wt, inp in terms for k in range(KT)]
                    for i in range(NB)]

        def gather_units(inp):
            return [[(inp[:, i, m * 128:(m + 1) * 128], counts[:, i, c0:c0 + cn]) for i in range(NB)]
                    for m, c0, cn in MC]

        def turn_back(name, source, store, by):
            ready = sem(name + "_ready")
            done = {e: sem(f"{name}_stored_{e}") for e in set(by)}

            def engine_of(i):
                return by[i % len(by)]

            def pe_(pe):
                for i in range(NB):
                    if i >= 8:
                        pe.wait_ge(done[engine_of(i - 8)], sum(engine_of(v) == engine_of(i - 8) for v in range(i - 7)))
                    for k in range(KT):
                        last = nc.tensor.transpose(ps[0:B, i % 8, k * 128:(k + 1) * 128],
                                                   source[:, k, i * B:(i + 1) * B], ident)
                    last.then_inc(ready, 1)

            def run(letter):
                def go(eng):
                    for i in range(NB):
                        if engine_of(i) == letter:
                            eng.wait_ge(ready, i + 1)
                            store(letter, i, ps[0:B, i % 8, :]).then_inc(done[letter], 1)
                return go
            return pe_, run("a"), run("d"), done, ready

        def batch_norm(name, scale_shift, func, gamma, beta):
            stats, root, steps, out_a = (sem(f"{name}_{n}") for n in ("stats", "root", "steps", "applied"))
            scale, shift = scale_shift

            def vector(dve):
                for j, (m, c0, cn) in enumerate(MC):
                    nc.vector.bn_stats(st[:, j, :], aT[:, m, c0:c0 + cn]).then_inc(stats, 1)
                dve.wait_ge(stats, len(MC))
                for m in range(KT):
                    nc.vector.bn_aggr(mv[:, m, :], st[:, 3 * m:3 * m + 3, :].rearrange("p a b -> p (a b)")).then_inc(stats, 1)
                dve.wait_ge(root, 1)
                nc.vector.reciprocal(rstd[:, 0:KT], sd[:, 0:KT]).then_inc(steps, 1)
                dve.wait_ge(steps, 1)
                nc.vector.tensor_tensor(scale, rstd[:, 0:KT], gamma, ALU.mult).then_inc(steps, 1)
                dve.wait_ge(steps, 2)
                nc.vector.tensor_tensor(nmr[:, 0:KT], mv[:, 0:KT, 0], scale, ALU.mult).then_inc(steps, 1)
                dve.wait_ge(steps, 3)
                nc.vector.tensor_tensor(shift, beta, nmr[:, 0:KT], ALU.subtract).then_inc(steps, 1)

            def scalar(act):
                act.wait_ge(stats, len(MC) + KT)
                nc.scalar.activation(sd[:, 0:KT], mv[:, 0:KT, 1], ACT.Sqrt, bias=epst[:, :]).then_inc(root, 1)
                act.wait_ge(steps, 4)
                for m in range(KT):
                    nc.scalar.activation(aT[:, m, :], aT[:, m, :], func, bias=shift[:, m:m + 1],
                                         scale=scale[:, m:m + 1]).then_inc(out_a, 1)
            return vector, scalar, out_a

        s_padz = sem("pad_halves_zero")

        def store_padded(e, m, c0, cn, bank, f):
            f(e, pad[0:64, 2 * m, c0:c0 + cn], bank[0:64, 0:cn], slice(0, 64))
            return f(e, pad[64:128, 2 * m + 1, c0:c0 + cn], bank[64:128, 0:cn], slice(64, 128))

        def store_qk0(e, u, bank):
            m, c0, cn = MC[u % 12]
            if u < 12:
                return store_padded(e, m, c0, cn, bank, lambda e, o, s, _: copy_by(e, o, s))
            return copy_by(e, aT[:, m, c0:c0 + cn], bank[:, 0:cn])

        def store_qkv0(e, u, bank):
            return store_qk0(e, u, bank) if u < 24 else copy_by(e, vn[:, u - 24, :], bank)

        qkv0 = products("qkv0", turned_units((w[1], hT)) + turned_units((w[0], hT)) + natural_units((w[2], hT)),
                        store_qkv0, "a", banks=4)

        def zero_halves(engine):
            engine.memset(pad[64:128, 0:HEADS:2, :], 0.0).then_inc(s_padz, 1)
            engine.memset(pad[0:64, 1:HEADS:2, :], 0.0).then_inc(s_padz, 1)

        s_out, s_outsum = sem("edges_outside_bands"), sem("edges_outside_summed")
        s_part, s_same, s_before, s_rank, s_sums, s_wsum, e0 = (sem(n) for n in (
            "weight_parts", "same_key", "same_before", "rank", "weights_summed", "weights_stored", "index_steps"))
        BATCHES = TILES // BATCH
        with nc.Block() as block:
            @block.sync
            def _(sp):
                sp.wait_ge(s_keysave, 16)
                for n in range(BATCHES):
                    if n >= 2:
                        sp.wait_ge(s_same, n - 1)
                    flat = keys[n * BATCH * B:(n + 1) * BATCH * B].rearrange("(a b) -> a b", a=1)
                    sp.dma_start(rows[:, n % 2, :, :].rearrange("p a b -> p (a b)"), flat.to_broadcast([B, BATCH * B])).then_inc(s_rows[n % 2], 16)
                each = FILLS // FILL_DMAS
                for j in range(0, FILLS, each):
                    part = table.rearrange("(p r) h -> p (r h)", p=128)[:, j * FILL:(j + each) * FILL]
                    sp.dma_start(part.rearrange("p (f r) -> p f r", f=each),
                                 zeros.rearrange("p (a r) -> p a r", a=1).to_broadcast([128, each, FILL])).then_inc(s_fill, 16)

            @block.gpsimd
            def _(pool):
                zero_halves(nc.gpsimd)

            @block.tensor
            def _(pe):
                def sum_equal_edges(n):
                    if n == 0:
                        pe.wait_ge(s_out, 3)
                        nc.tensor.matmul(ps[0:1, 7, 0:1], e_outside, ones[0:B, 0:1], start=True, stop=True).then_inc(s_outsum, 1)
                        pe.wait_ge(s_part, 5)
                    pe.wait_ge(s_same, n + 1)
                    if n >= 2:
                        pe.wait_ge(s_wsum, n - 1)
                    for t in range(BATCH):
                        last = nc.tensor.matmul(ps[0:B, 4 + n % 2, t * 24:(t + 1) * 24], same[n % 2][:, t, 0:B],
                                                e_parts[:, n * BATCH + t, :, :].rearrange("p h c -> p (h c)"),
                                                start=True, stop=True)
                    last.then_inc(s_sums, 1)

                def before_unit(u):
                    if u == 12:
                        pe.wait_ge(s_w[0], 16)
                    if u == 24:
                        pe.wait_ge(s_w[2], 16)
                    if u >= 5 and (u - 5) % 3 == 0 and (u - 5) // 3 < BATCHES:
                        sum_equal_edges((u - 5) // 3)

                pe.wait_ge(s_w[1], 16)
                qkv0[0](pe, before_unit)

            @block.vector
            def _(dve):
                nc.vector.tensor_tensor(e_win[:, 0, :], e_dst, e_bounds[:, 0, :], ALU.is_lt).then_inc(s_out, 1)
                nc.vector.tensor_tensor(e_win[:, 1, :], e_dst, e_bounds[:, 1, :], ALU.is_ge).then_inc(s_out, 1)
                dve.wait_ge(s_out, 2)
                nc.vector.tensor_reduce(e_outside, e_win.rearrange("p a b -> p (a b)"), AX.X, ALU.add).then_inc(s_out, 1)
                dve.wait_ge(s_exp, 1)
                for c in range(3):
                    nc.vector.tensor_copy(e_parts[:, :, :, c], e_exp).then_inc(s_part, 1)
                    dve.wait_ge(s_part, 2 * c + 1)
                    if c < 2:
                        nc.vector.tensor_tensor(e_exp, e_exp, e_parts[:, :, :, c], ALU.subtract).then_inc(s_part, 1)
                        dve.wait_ge(s_part, 2 * c + 2)

                def store_sums(n):
                    dve.wait_ge(s_sums, n + 1)
                    nc.vector.tensor_reduce(wsum[:, n * BATCH:(n + 1) * BATCH, :],
                                            ps[0:B, 4 + n % 2, 0:BATCH * 24].rearrange("p (t h c) -> p t h c", h=HEADS, c=3),
                                            AX.X, ALU.add).then_inc(s_wsum, 1)

                for n in range(BATCHES):
                    t0 = n * BATCH
                    dve.wait_ge(s_rows[n % 2], 16 * (n // 2 + 1))
                    if n >= 2:
                        dve.wait_ge(s_sums, n - 1)
                    keycols = e_key[:, t0:t0 + BATCH].rearrange("p (t a) -> p t a", a=1).to_broadcast([B, BATCH, B])
                    nc.vector.tensor_tensor(same[n % 2][:, :, 0:B], rows[:, n % 2, :, :], keycols, ALU.is_equal).then_inc(s_same, 1)
                    dve.wait_ge(s_same, n + 1)
                    if n >= 1:
                        dve.wait_ge(s_rank, n)
                    nc.vector.tensor_tensor(before[:, :, 0:B], same[n % 2][:, :, 0:B],
                                            lower.rearrange("p (a b) -> p a b", a=1).to_broadcast([B, BATCH, B]), ALU.mult).then_inc(s_before, 1)
                    dve.wait_ge(s_before, n + 1)
                    nc.vector.tensor_reduce(e_rank[:, t0:t0 + BATCH], before[:, :, 0:B], AX.X, ALU.add).then_inc(s_rank, 1)
                    if n == 0:
                        dve.wait_ge(s_outsum, 1)
                        nc.vector.tensor_copy(outside, ps[0:1, 7, 0:1]).then_inc(s_out, 1)
                    else:
                        store_sums(n - 1)
                store_sums(BATCHES - 1)
                dve.wait_ge(s_rank, BATCHES)
                nc.vector.tensor_scalar(e_rank, e_rank, 1.0, None, ALU.min).then_inc(e0, 1)
                nc.vector.tensor_scalar(e_src, e_key, -1.0, e_tmp[:, 0:1], ALU.mult, ALU.add).then_inc(e0, 1)
                dve.wait_ge(e0, 2)
                nc.vector.tensor_tensor(e_rank, e_rank, e_src, ALU.mult).then_inc(e0, 1)
                dve.wait_ge(e0, 3)
                nc.vector.tensor_tensor(widx, e_rank, e_key, ALU.add).then_inc(e0, 1)

            @block.scalar
            def _(act):
                qkv0[1](act)
        if stop == "edges":
            with nc.Block() as block:
                @block.sync
                def _(sp):
                    for q, n in ((s_w[0], 16), (s_w[1], 16), (s_par, 64), (s_fill, 16 * FILL_DMAS)):
                        sp.wait_ge(q, n)
            return


        s_scat = sem("weights_scattered")

        scattered = [0]

        def scatter(pool, tiles):
            for t in range(scattered[0], scattered[0] + tiles):
                if t == 0:
                    pool.wait_ge(s_fill, 16 * FILL_DMAS)
                else:
                    pool.wait_ge(s_scat, 16 * t)
                pool.indirect_dma_start(table, bass.IndirectOffsetOnAxis(ap=widx[:, t:t + 1], axis=0), wsum[:, t, :],
                                        None, compute_op=ALU.add).then_inc(s_scat, 16)
            scattered[0] += tiles

        def scatter_in(block, tiles):
            @block.gpsimd
            def _(pool):
                scatter(pool, tiles)

        onehot_src = view(Mem.w, SLOTS, N // 2, p=B).bitcast(BF16)
        onehot_dst = view(Mem.w + SLOTS * N // 2, SLOTS, 64, p=B).bitcast(BF16)
        zero_bf = view(Mem.w + SLOTS * N // 2 + SLOTS * 64, BANK // 2, p=B).bitcast(BF16)
        assert SLOTS * N // 2 + SLOTS * 64 + BANK // 2 <= 3 * KT * D
        s_win = sem("window_targets")
        s_oh = sem("onehot_ready")
        s_ohfree = sem("onehot_free")
        s_cw = sem("window_counted")
        s_cev = sem("window_stored")
        s_zbf = sem("zero_rows")
        blocks_of = [(0, 4), (4, 4), (8, 2)]

        with nc.Block() as block:
            @block.gpsimd
            def _(pool):
                scatter(pool, 12)

            def make_onehots(dve, windows):
                made = 0
                for wd, (first, count) in enumerate(windows):
                    nc.vector.tensor_scalar(e_win[:, wd % 2, :], e_dst, float(-wd * B), None, ALU.add).then_inc(s_win, 1)
                    dve.wait_ge(s_win, wd + 1)
                    unroll = UNROLL[count]
                    with dve.Fori(0, count // unroll) as g:
                        for u in range(unroll):
                            slot = (made + u) % unroll
                            dve.wait_ge(s_ohfree, g * unroll + (made + u + 1))
                            at = bass.ds(g * unroll + (first + u), 1)
                            nc.vector.tensor_scalar(onehot_src[:, slot, :], e_iota, e_srcf[:, at], None, ALU.is_equal)
                            nc.vector.tensor_scalar(onehot_dst[:, slot, 0:B], e_iota[:, 0:B], e_win[:, wd % 2, at], None,
                                                    ALU.is_equal).then_inc(s_oh, 1)
                    made += count

            def count_windows(pe, windows):
                pe.sem_inc(s_ohfree, UNROLL[windows[0][1]])
                used = 0
                for wd, (first, count) in enumerate(windows):
                    base = 3 * (wd % 2)
                    if wd >= 2:
                        pe.wait_ge(s_cev, wd - 1)
                    for j in range(3):
                        nc.tensor.matmul(ps[0:B, base + j, :], zero_bf[:, 0:B], zero_bf[:, 0:BANK],
                                         start=True, stop=False)
                    unroll = UNROLL[count]
                    with pe.Fori(0, count // unroll) as g:
                        for u in range(unroll):
                            slot = (used + u) % unroll
                            pe.wait_ge(s_oh, g * unroll + (used + u + 1))
                            for j, (b0, nb) in enumerate(blocks_of):
                                for i in range(nb):
                                    last = nc.tensor.matmul(ps[0:B, base + j, i * B:(i + 1) * B],
                                                            onehot_src[:, slot, (b0 + i) * B:(b0 + i + 1) * B],
                                                            onehot_dst[:, slot, 0:B], start=False, stop=False,
                                                            skip_group_check=True)
                            last.then_inc(s_ohfree, 1)
                    used += count
                    for j in range(3):
                        last = nc.tensor.matmul(ps[0:B, base + j, :], zero_bf[:, 0:B], zero_bf[:, 0:BANK],
                                                start=False, stop=True)
                    last.then_inc(s_cw, 1)

            @block.vector
            def _(dve):
                nc.vector.memset(zero_bf, 0.0).then_inc(s_zbf, 1)
                found = dve.value_load(outside)
                with dve.If(found < 1):
                    make_onehots(dve, edge_windows(True))
                with dve.Else():
                    make_onehots(dve, edge_windows(False))

            @block.tensor
            def _(pe):
                pe.wait_ge(s_zbf, 1)
                found = pe.value_load(outside)
                with pe.If(found < 1):
                    count_windows(pe, edge_windows(True))
                with pe.Else():
                    count_windows(pe, edge_windows(False))

            @block.scalar
            def _(act):
                for wd in range(NB):
                    act.wait_ge(s_cw, wd + 1)
                    for j, (b0, nb) in enumerate(blocks_of):
                        last = nc.scalar.activation(counts[:, b0:b0 + nb, wd * B:(wd + 1) * B],
                                                    ps[0:B, 3 * (wd % 2) + j, 0:nb * B].rearrange("p (i b) -> p i b", b=B),
                                                    ACT.Copy)
                    last.then_inc(s_cev, 1)
        if stop == "counts":
            with nc.Block() as block:
                @block.sync
                def _(sp):
                    for q, n in ((s_w[0], 16), (s_w[1], 16), (s_w[2], 16), (s_par, 64), (s_fill, 16 * FILL_DMAS)):
                        sp.wait_ge(q, n)
            return
        bn_scale = (view(s0 + 194, KT), view(s0 + 1040, KT))

        probs = view(Mem.probs, 4, N, p=B)
        psums = view(Mem.w, 4, N, p=B)
        s_sc, s_exp0, s_clip, s_mask = (sem(n) for n in ("scores0", "exps0", "clipped0", "masked0"))
        s_pv, s_sum, s_oev, s_z, s_zev, s_norm = (sem(n) for n in ("pv0", "sums0", "output0_stored", "z0", "z0_read", "norm0"))
        LO, HI = 6.737946999085467e-03, 148.4131591025766
        STEPS = PAIRS * NB
        tiles = [(q, q // 2, q % 2) for q in range(2 * STEPS)]

        with nc.Block() as block:
            @block.gpsimd
            def _(pool):
                for q, s, hh in tiles:
                    i, pr = s % NB, s // NB
                    acc = psums[:, (pr % 2) * 2 + hh, :]
                    pool.wait_ge(s_mask, q + 1)
                    if i == 0:
                        if pr >= 2:
                            pool.wait_ge(s_z, 3 * (pr - 1))
                        nc.gpsimd.tensor_scalar(acc, probs[:, q % 4, :], 1.0, 0.0, ALU.mult, ALU.add).then_inc(s_sum, 1)
                    else:
                        pool.wait_ge(s_sum, q - 1)
                        nc.gpsimd.tensor_tensor(acc, acc, probs[:, q % 4, :], ALU.add).then_inc(s_sum, 1)
                    if q % 2:
                        scatter(pool, 1)

            @block.tensor
            def _(pe):
                def scores(s):
                    i, pr = s % NB, s // NB
                    for hh in range(2):
                        for c, (c0, cn) in enumerate(CHUNKS):
                            u = 6 * s + 3 * hh + c
                            if u >= 4:
                                pe.wait_ge(s_exp0, u - 3)
                            nc.tensor.matmul(ps[0:B, 3 + u % 4, 0:cn], pad[:, 2 * pr + hh, i * B:(i + 1) * B],
                                             aT[:, pr, c0:c0 + cn], start=True, stop=True).then_inc(s_sc, 1)

                def weighted(s):
                    i, pr = s % NB, s // NB
                    pe.wait_ge(s_mask, 2 * s + 2)
                    if i == 0 and pr >= 1:
                        pe.wait_ge(s_oev, pr)
                    for c, (c0, cn) in enumerate(CHUNKS):
                        for hh in range(2):
                            h = 2 * pr + hh
                            last = nc.tensor.matmul(ps[64 * hh:64 * hh + 64, c, 0:cn], vn[:, i, h * DH:(h + 1) * DH],
                                                    probs[:, (2 * s + hh) % 4, c0:c0 + cn], start=(i == 0), stop=(i == NB - 1))
                    last.then_inc(s_pv, 1)

                def denominators(pr, c):
                    c0, cn = CHUNKS[c]
                    if c == 0:
                        pe.wait_ge(s_sum, 2 * NB * (pr + 1))
                    if pr or c:
                        pe.wait_ge(s_zev, 3 * pr + c)
                    for hh in range(2):
                        last = nc.tensor.matmul(ps[64 * hh:64 * hh + 64, 7, 0:cn], ones[0:B, 0:64],
                                                psums[:, (pr % 2) * 2 + hh, c0:c0 + cn], start=True, stop=True)
                    last.then_inc(s_z, 1)

                scores(0)
                for s in range(STEPS):
                    if s + 1 < STEPS:
                        scores(s + 1)
                    weighted(s)
                    if 3 <= s % NB < 6 and s > NB:
                        denominators(s // NB - 1, s % NB - 3)
                for c in range(3):
                    denominators(PAIRS - 1, c)

            def store_outputs(act, pr):
                act.wait_ge(s_pv, NB * (pr + 1))
                for c, (c0, cn) in enumerate(CHUNKS):
                    last = nc.scalar.activation(aT[:, pr, c0:c0 + cn], ps[:, c, 0:cn], ACT.Copy)
                last.then_inc(s_oev, 1)

            @block.scalar
            def _(act):
                for q, s, hh in tiles:
                    for c, (c0, cn) in enumerate(CHUNKS):
                        act.wait_ge(s_sc, 3 * q + c + 1)
                        if c == 0 and q >= 4:
                            act.wait_ge(s_pv, (q - 4) // 2 + 1)
                            act.wait_ge(s_sum, q - 3)
                        nc.scalar.activation(probs[:, q % 4, c0:c0 + cn], ps[0:B, 3 + (3 * q + c) % 4, 0:cn], ACT.Exp,
                                             scale=SCALE).then_inc(s_exp0, 1)
                    if s % NB == 0 and s > 0 and hh == 1:
                        store_outputs(act, s // NB - 1)
                store_outputs(act, PAIRS - 1)

            @block.vector
            def _(dve):
                def normalise(pr, pieces):
                    for c in pieces:
                        c0, cn = CHUNKS[c]
                        n = 3 * pr + c
                        z = zt[:, n % 2, 0:cn]
                        dve.wait_ge(s_z, n + 1)
                        nc.vector.tensor_scalar(z, ps[:, 7, 0:cn], 1e-6, None, ALU.add).then_inc(s_zev, 1)
                        dve.wait_ge(s_zev, n + 1)
                        nc.vector.reciprocal(z, z).then_inc(s_norm, 1)
                        dve.wait_ge(s_norm, 3 * n + 1)
                        if c == 0:
                            dve.wait_ge(s_oev, pr + 1)
                        nc.vector.tensor_tensor(aT[:, pr, c0:c0 + cn], aT[:, pr, c0:c0 + cn], z, ALU.mult).then_inc(s_norm, 1)
                        dve.wait_ge(s_norm, 3 * n + 2)
                        nc.vector.tensor_tensor(aT[:, pr, c0:c0 + cn], aT[:, pr, c0:c0 + cn], hT[:, pr, c0:c0 + cn],
                                                ALU.add).then_inc(s_norm, 1)

                for q, s, hh in tiles:
                    dve.wait_ge(s_exp0, 3 * q + 3)
                    nc.vector.tensor_scalar(probs[:, q % 4, :], probs[:, q % 4, :], LO, HI, ALU.max, ALU.min).then_inc(s_clip, 1)
                    dve.wait_ge(s_clip, q + 1)
                    nc.vector.tensor_tensor(probs[:, q % 4, :], probs[:, q % 4, :], counts[:, s % NB, :], ALU.mult).then_inc(s_mask, 1)
                    if 4 <= s % NB < 7 and s > NB and hh == 1:
                        normalise(s // NB - 1, [s % NB - 4])
                normalise(PAIRS - 1, range(3))
        if stop == "att0":
            return
        xld = hn
        s_xre, s_wl = sem("x_reloaded"), [sem(f"l1_w{j}_loaded") for j in range(3)]
        s_b2 = sem("b2_loaded")
        b2B = view(Mem.probs + 2 * N, D, p=B)
        deg_units = [[(ones[0:B, :], counts[:, i, c0:c0 + cn]) for i in range(NB)] for c0, cn in CHUNKS]

        def store_degree(e, u, bank):
            c0, cn = CHUNKS[u]
            return copy_by(e, cntB[:, c0:c0 + cn], bank[:, 0:cn])
        deg = products("degree", deg_units[0:2], store_degree, "a")
        s_deg2, s_deg2ev = sem("degree_last"), sem("degree_last_stored")
        bn0_v, bn0_s, bn0_done = batch_norm("bn0", bn_scale, ACT.Identity, bn0s[:, 0, :], bn0s[:, 1, :])
        s_deg = sem("degree_steps")
        with nc.Block() as block:
            @block.sync
            def _(sp):
                for i in range(NB):
                    sp.dma_start(xld[:, i, :], x[i * B:(i + 1) * B, :]).then_inc(s_xre, 16)
                for j, a in enumerate((wl1, wr1, wl2)):
                    sp.dma_start(w[j], a.rearrange("(k p) n -> p k n", p=128)).then_inc(s_wl[j], 16)
                sp.dma_start(b2B, b2.to_broadcast([B, D])).then_inc(s_b2, 16)

            @block.gpsimd
            def _(pool):
                scatter(pool, 4)

            @block.tensor
            def _(pe):
                deg[0](pe)

            @block.scalar
            def _(act):
                act.wait_ge(s_par, 64)
                bn0_s(act)
                deg[1](act)

            @block.vector
            def _(dve):
                dve.wait_ge(s_par, 64)
                bn0_v(dve)

        def turned_block(source):
            def produce_into(signal, emptied):
                def produce(pe, i):
                    if i >= 4:
                        pe.wait_ge(emptied, i - 3)
                    for k in range(KT):
                        last = nc.tensor.transpose(ps[0:B, i % 4, k * 128:(k + 1) * 128],
                                                   source[:, k, i * B:(i + 1) * B], ident)
                    last.then_inc(signal, 1)
                return produce
            return produce_into

        def add_bank(ready, emptied, dest, other):
            def arrive(dve, i):
                dve.wait_ge(ready, i + 1)
                nc.vector.tensor_tensor(dest[:, i, :], ps[0:B, i % 4, :], other[:, i, :], ALU.add).then_inc(emptied, 1)
                dve.wait_ge(emptied, i + 1)
            return arrive

        def store_mean(e, u, bank):
            m, c0, cn = MC[u]
            return nc.vector.tensor_tensor(aT[:, m, c0:c0 + cn], bank[:, 0:cn], cntB[:, c0:c0 + cn], ALU.mult)

        s_rc, s_b2add = sem("reciprocals"), sem("x_plus_b2")
        s_dt, s_dc = sem("dinv_turned"), sem("dinv_copied")
        s_x1p, s_x1 = sem("x1_part"), sem("x1")
        back0 = turned_block(aT)(s_x1p, s_x1)

        def produce_x1(pe, i):
            back0(pe, i)
            if i >= 5:
                c0, cn = CHUNKS[2]
                for n in range(2 * (i - 5), 2 * (i - 4)):
                    last = nc.tensor.matmul(ps[:, 7, 0:cn], ones[0:B, :], counts[:, n, c0:c0 + cn],
                                            start=(n == 0), stop=(n == NB - 1))
                if i == NB - 1:
                    last.then_inc(s_deg2, 1)

        ln1_v, ln1_s, ln1_pe, ln1_done, h1_turned = norm_and_turn(
            "ln1", xn, hn, add_bank(s_x1p, s_x1, xn, xld), produce_x1, turn_banks=(4, 3))
        g1 = products("mean1", gather_units(hn), store_mean, "d", banks=4)
        with nc.Block() as block:
            @block.gpsimd
            def _(pool):
                pool.wait_ge(s_b2, 16)
                for i in range(NB):
                    pool.wait_ge(ln1_done, i + 1)
                    nc.gpsimd.tensor_tensor(xn[:, i, :], xn[:, i, :], b2B, ALU.add).then_inc(s_b2add, 1)
                scatter(pool, 22)

            @block.tensor
            def _(pe):
                ln1_pe(pe)
                pe.wait_ge(s_x1, NB)
                g1[0](pe)
                pe.wait_ge(s_rc, 2)
                pe.wait_ge(h1_turned, NB)
                for i in range(NB):
                    last = nc.tensor.transpose(ps[0:B, 4 + i // 4, (i % 4) * 128:(i % 4) * 128 + 128],
                                               dinvB[:, i * B:(i + 1) * B], ident)
                last.then_inc(s_dt, 1)

            @block.scalar
            def _(act):
                ln1_s(act)
                act.wait_ge(s_deg2, 1)
                c0, cn = CHUNKS[2]
                nc.scalar.activation(cntB[:, c0:c0 + cn], ps[:, 7, 0:cn], ACT.Copy).then_inc(s_deg2ev, 1)
                act.wait_ge(s_deg2ev, 1)
                nc.scalar.activation(dinvB, cntB, ACT.Sqrt, bias=ones[:, 0:1]).then_inc(s_deg, 1)

            @block.vector
            def _(dve):
                dve.wait_ge(s_xre, 16 * NB)
                ln1_v(dve)
                dve.wait_ge(s_deg, 1)
                nc.vector.tensor_scalar(cntB, cntB, 1.0, None, ALU.max).then_inc(s_rc, 1)
                nc.vector.reciprocal(dinvB, dinvB).then_inc(s_rc, 1)
                dve.wait_ge(s_rc, 2)
                nc.vector.reciprocal(cntB, cntB).then_inc(s_rc, 1)
                dve.wait_ge(s_rc, 3)
                g1[2](dve)
                dve.wait_ge(s_dt, 1)
                nc.vector.tensor_copy(dinv, ps[0:B, 4:7, :].rearrange("p a (b c) -> p (a b) c", c=128)[:, 0:NB, 0]).then_inc(s_dc, 1)

        def store_relu(e, u, bank):
            m, c0, cn = MC[u]
            return nc.scalar.activation(vT[:, m, c0:c0 + cn], bank[:, 0:cn], ACT.Relu, bias=b1s[:, m:m + 1])

        z1 = products("z1", turned_units((w[0], aT), (w[1], hT)), store_relu, "a")
        with nc.Block() as block:
            scatter_in(block, 22)

            @block.tensor
            def _(pe):
                pe.wait_ge(s_wl[0], 16)
                pe.wait_ge(s_wl[1], 16)
                z1[0](pe)

            @block.scalar
            def _(act):
                z1[1](act)

        s_wr2, s_w2 = sem("wr2_loaded"), sem("gcn_w_loaded")
        tb1 = turn_back("z1_back", vT, lambda e, i, bank: copy_by(e, hn[:, i, :], bank), "ad")
        with nc.Block() as block:
            scatter_in(block, 1)

            @block.sync
            def _(sp):
                sp.dma_start(w[0], wr2.rearrange("(k p) n -> p k n", p=128)).then_inc(s_wr2, 16)
                sp.dma_start(w[1], w2.rearrange("(k p) n -> p k n", p=128)).then_inc(s_w2, 16)

            @block.tensor
            def _(pe):
                tb1[0](pe)

            @block.scalar
            def _(act):
                tb1[1](act)

            @block.vector
            def _(dve):
                tb1[2](dve)

        g2 = products("mean2", gather_units(hn), store_mean, "d")
        with nc.Block() as block:
            scatter_in(block, 28)

            @block.tensor
            def _(pe):
                g2[0](pe)

            @block.vector
            def _(dve):
                g2[2](dve)

        s_x2p, s_x2, s_self = sem("x2_part"), sem("x2"), sem("self_loops")
        x2_units = natural_units((w[2], aT), (w[0], vT))

        def produce_x2(pe, i):
            if i >= 4:
                pe.wait_ge(s_x2, i - 3)
            for j, (left, right) in enumerate(x2_units[i]):
                last = nc.tensor.matmul(ps[0:B, i % 4, :], left, right, start=(j == 0), stop=(j == len(x2_units[i]) - 1))
            last.then_inc(s_x2p, 1)

        ln2_v, ln2_s, ln2_pe, _, h2_turned = norm_and_turn(
            "ln2", xn, hn, add_bank(s_x2p, s_x2, xn, xn), produce_x2, ahead=2)

        def store_scaled(e, u, bank):
            if e == "a":
                return nc.scalar.activation(vn[:, u, :], bank, ACT.Copy, scale=dinv[:, u:u + 1])
            return nc.vector.tensor_scalar(vn[:, u, :], bank, dinv[:, u:u + 1], None, ALU.mult)

        xw = products("xw", natural_units((w[1], hT)), store_scaled, "ad", banks=4)
        with nc.Block() as block:
            scatter_in(block, 35)

            @block.tensor
            def _(pe):
                pe.wait_ge(s_wl[2], 16)
                pe.wait_ge(s_wr2, 16)
                ln2_pe(pe)
                pe.wait_ge(s_w2, 16)
                pe.wait_ge(s_x2, NB)
                pe.wait_ge(h2_turned, NB)
                xw[0](pe)

            @block.scalar
            def _(act):
                ln2_s(act)
                xw[1](act)

            @block.vector
            def _(dve):
                ln2_v(dve)
                for i in range(NB):
                    nc.vector.tensor_tensor(counts[:, i, i * B:(i + 1) * B], counts[:, i, i * B:(i + 1) * B],
                                            ident[0:B, 0:B], ALU.add).then_inc(s_self, 1)
                xw[2](dve)

        def store_gcn(e, u, bank):
            m, c0, cn = MC[u]
            return nc.vector.tensor_tensor(aT[:, m, c0:c0 + cn], bank[:, 0:cn], dinvB[:, c0:c0 + cn], ALU.mult)

        g3 = products("gcn", gather_units(vn), store_gcn, "d")
        s_w3 = [sem(f"l3_w{j}_loaded") for j in range(3)]
        s_gb, s_gst, s_gag, s_grt, s_gin = (sem(n) for n in (
            "gcn_bias", "gcn_stats", "gcn_mean_var", "gcn_root", "gcn_scale_shift"))
        s_gel, s_res = sem("gelu"), sem("gelu_plus_h2")
        scale2, shift2 = bn_scale
        with nc.Block() as block:
            @block.gpsimd
            def _(pool):
                scatter(pool, 6)

            @block.sync
            def _(sp):
                for j, a in enumerate((wq3, wk3, wv3)):
                    sp.dma_start(w[j], a.rearrange("(k p) n -> p k n", p=128)).then_inc(s_w3[j], 16)

            @block.tensor
            def _(pe):
                g3[0](pe)

            @block.scalar
            def _(act):
                for m in range(KT):
                    act.wait_ge(s_gag, m + 1)
                    nc.scalar.activation(sd[:, m:m + 1], mv[:, m, 1:2], ACT.Sqrt, bias=epst[:, :]).then_inc(s_grt, 1)
                    act.wait_ge(s_gin, 4 * m + 4)
                    nc.scalar.activation(aT[:, m, :], aT[:, m, :], ACT.Gelu, bias=shift2[:, m:m + 1],
                                         scale=scale2[:, m:m + 1]).then_inc(s_gel, 1)

            @block.vector
            def _(dve):
                def residual(m):
                    dve.wait_ge(s_gel, m + 1)
                    nc.vector.tensor_tensor(aT[:, m, :], aT[:, m, :], hT[:, m, :], ALU.add).then_inc(s_res, 1)

                g3_ready, g3_done = g3[4], g3[3]["d"]
                for u, (m, c0, cn) in enumerate(MC):
                    piece = aT[:, m, c0:c0 + cn]
                    dve.wait_ge(g3_ready, u + 1)
                    store_gcn("d", u, ps[:, u % 8, :]).then_inc(g3_done, 1)
                    dve.wait_ge(g3_done, u + 1)
                    nc.vector.tensor_scalar(piece, piece, par2s[:, 0, m:m + 1], None, ALU.add).then_inc(s_gb, 1)
                    dve.wait_ge(s_gb, u + 1)
                    nc.vector.bn_stats(st[:, u, :], piece).then_inc(s_gst, 1)
                    if u % 3 == 2:
                        one = slice(m, m + 1)
                        dve.wait_ge(s_gst, u + 1)
                        nc.vector.bn_aggr(mv[:, m, :], st[:, 3 * m:3 * m + 3, :].rearrange("p a b -> p (a b)")).then_inc(s_gag, 1)
                        dve.wait_ge(s_grt, m + 1)
                        nc.vector.reciprocal(rstd[:, one], sd[:, one]).then_inc(s_gin, 1)
                        dve.wait_ge(s_gin, 4 * m + 1)
                        nc.vector.tensor_tensor(scale2[:, one], rstd[:, one], par2s[:, 1, one], ALU.mult).then_inc(s_gin, 1)
                        dve.wait_ge(s_gin, 4 * m + 2)
                        nc.vector.tensor_tensor(nmr[:, one], mv[:, m, 0:1], scale2[:, one], ALU.mult).then_inc(s_gin, 1)
                        dve.wait_ge(s_gin, 4 * m + 3)
                        nc.vector.tensor_tensor(shift2[:, one], par2s[:, 2, one], nmr[:, one], ALU.subtract).then_inc(s_gin, 1)
                        if m >= 1:
                            residual(m - 1)
                residual(KT - 1)

        weights = [view(a, N * HEADS, p=B).rearrange("p (t h) -> p t h", h=HEADS) for a in Mem.weights]
        s_tab = [sem(f"table_loaded{j}") for j in range(2)]
        table_rows = table[0:N * N, :].rearrange("(s t) h -> s (t h)", t=N)

        def load_weights(sp, i):
            for a, b in ((0, 112), (112, B)):
                sp.dma_start(weights[i % 2][a:b].rearrange("p t h -> p (t h)"),
                             table_rows[i * B + a:i * B + b, :]).then_inc(s_tab[i % 2], 16)

        bv3B = view(Mem.cntB, D, p=B)
        bo3B = view(Mem.cntB + D, D, p=B)
        s_b3, s_bo, s_xs, s_bq = sem("b3_loaded"), sem("x_plus_bo"), sem("x_saved_sem"), sem("negated_bq")
        s_x3p, s_x3 = sem("x3_part"), sem("x3")
        ln3_v, ln3_s, ln3_pe, ln3_done, h3_turned = norm_and_turn(
            "ln3", xn, hn, add_bank(s_x3p, s_x3, xn, xn), turned_block(aT)(s_x3p, s_x3))

        def store_qk3(e, u, bank):
            m, c0, cn = MC[u % 12]

            def scaled(e, o, s, rows):
                if e == "a":
                    return nc.scalar.activation(o, s, ACT.Identity, bias=bqs[rows, m:m + 1], scale=-SCALE)
                return nc.vector.tensor_scalar(o, s, par3s[rows, 0, m:m + 1], -SCALE, ALU.add, ALU.mult)
            if u >= 12:
                return store_padded(e, m, c0, cn, bank, scaled)
            if e == "a":
                return nc.scalar.activation(aT[:, m, c0:c0 + cn], bank[:, 0:cn], ACT.Identity, bias=par3s[:, 1, m:m + 1])
            return nc.vector.tensor_scalar(aT[:, m, c0:c0 + cn], bank[:, 0:cn], par3s[:, 1, m:m + 1], None, ALU.add)

        k3 = products("k3", turned_units((w[1], hT)), store_qk3, "ad", banks=4)
        v3 = products("v3", natural_units((w[2], hT)), lambda e, u, bank: nc.vector.tensor_tensor(
            vn[:, u, :], bank, bv3B, ALU.add), "d", banks=4, first_bank=4)
        q3 = products("q3", turned_units((w[0], hT)), lambda e, u, bank: store_qk3(e, u + 12, bank), "ad", banks=4)
        with nc.Block() as block:
            @block.sync
            def _(sp):
                sp.dma_start(bv3B, bv3.to_broadcast([B, D])).then_inc(s_b3, 16)
                sp.dma_start(bo3B, bo3.to_broadcast([B, D])).then_inc(s_b3, 16)
                assert scattered[0] == TILES
                sp.wait_ge(s_scat, 16 * TILES)
                load_weights(sp, 0)
                for i in range(NB):
                    sp.wait_ge(s_bo, i + 1)
                    sp.dma_start(xsave[i * B:(i + 1) * B, :], xn[:, i, :]).then_inc(s_xs, 16)

            @block.gpsimd
            def _(pool):
                pool.wait_ge(s_b3, 32)
                for i in range(NB):
                    pool.wait_ge(ln3_done, i + 1)
                    nc.gpsimd.tensor_tensor(xn[:, i, :], xn[:, i, :], bo3B, ALU.add).then_inc(s_bo, 1)
                pool.wait_ge(s_xs, 16 * NB)
                pool.wait_ge(h3_turned, NB)
                zero_halves(nc.gpsimd)

            @block.tensor
            def _(pe):
                ln3_pe(pe)
                for q in s_w3:
                    pe.wait_ge(q, 16)
                pe.wait_ge(s_x3, NB)
                pe.wait_ge(h3_turned, NB)
                k3[0](pe)
                v3[0](pe)
                for e, q in k3[3].items():
                    pe.wait_ge(q, 6)
                q3[0](pe)

            @block.scalar
            def _(act):
                ln3_s(act)
                k3[1](act)
                act.wait_ge(s_padz, 4)
                act.wait_ge(s_bq, 1)
                q3[1](act)

            @block.vector
            def _(dve):
                nc.vector.tensor_scalar(bqs, par3s[:, 0, :], -SCALE, None, ALU.mult).then_inc(s_bq, 1)
                ln3_v(dve)
                k3[2](dve)
                dve.wait_ge(s_b3, 32)
                v3[2](dve)
                dve.wait_ge(s_padz, 4)
                q3[2](dve)

        pslot = [view(a, N, p=B) for a in (Mem.probs3, Mem.probs3 + N, Mem.probs3b, Mem.probs3b + N)]
        wo = w[0]
        masks = [view(Mem.masks + j * N // 2, N // 2, p=B).bitcast(BF16) for j in range(2)]
        turnedp = [view(Mem.turned + 4 * j * B, 4, B, p=B) for j in range(4)]
        yT = [view(Mem.yT + j * KT * B, KT, B) for j in range(2)]
        xb = view(Mem.xb, D, p=B)
        GROUPS = [(0, 4), (4, 4), (8, 2)]
        s_wo, s_mask3 = sem("wo_loaded"), sem("masks3")
        s_qk, s_max, s_e3, s_wt, s_rd, s_p3 = (sem(n) for n in (
            "scores3", "masked3", "exps3", "weighted3", "recip_den3", "probs3"))
        s_tp, s_tps, s_y, s_ys, s_o, s_ob, s_xb, s_out = (sem(n) for n in (
            "probs_turned", "turned_stored", "y3", "y3_stored", "out3", "out3_added", "x_row_loaded", "out_stored"))
        HT = NB * HEADS

        SB, TB = 3, 3

        with nc.Block() as block:
            @block.sync
            def _(sp):
                sp.dma_start(wo, wo3.rearrange("(k p) n -> p k n", p=128)).then_inc(s_wo, 16)

                def load(i):
                    if i >= 2:
                        sp.wait_ge(s_wt, HEADS * (i - 1))
                        sp.wait_ge(s_mask3, HEADS * (i - 1))
                    load_weights(sp, i)
                load(1)
                sp.dma_start(xb, xsave[0:B, :]).then_inc(s_xb, 16)
                for i in range(NB):
                    if i + 2 < NB:
                        load(i + 2)
                    sp.wait_ge(s_ob, i + 1)
                    sp.dma_start(out[i * B:(i + 1) * B, :], xb).then_inc(s_out, 16)
                    if i + 1 < NB:
                        sp.wait_ge(s_out, 16 * (i + 1))
                        sp.dma_start(xb, xsave[(i + 1) * B:(i + 2) * B, :]).then_inc(s_xb, 16)
                sp.wait_ge(s_out, 16 * NB)

            @block.gpsimd
            def _(pool):
                for q in range(HT):
                    pool.wait_ge(s_rd, q + 1)
                    nc.gpsimd.tensor_scalar(pslot[q % 4], pslot[q % 4], rden[:, q % 4:q % 4 + 1], 1.0,
                                            ALU.mult, ALU.mult).then_inc(s_p3, 1)

            @block.tensor
            def _(pe):
                def scores(q):
                    i, h = divmod(q, HEADS)
                    for c, (c0, cn) in enumerate(CHUNKS):
                        u = 3 * q + c
                        if u >= SB:
                            pe.wait_ge(s_max, u - SB + 1)
                        nc.tensor.matmul(ps[0:B, u % SB, 0:cn], pad[:, h, i * B:(i + 1) * B], aT[:, h // 2, c0:c0 + cn],
                                         start=True, stop=True).then_inc(s_qk, 1)

                def turn_and_weigh(i, pr):
                    q0 = i * HEADS + 2 * pr
                    for g, (j0, nj) in enumerate(GROUPS):
                        for hh in range(2):
                            n = q0 // 2 * 6 + 2 * g + hh
                            if g == 0:
                                pe.wait_ge(s_p3, q0 + hh + 1)
                            if n >= TB:
                                pe.wait_ge(s_tps, n - TB + 1)
                            for j in range(nj):
                                last = nc.tensor.transpose(ps[0:B, SB + n % TB, j * B:(j + 1) * B],
                                                           pslot[(q0 + hh) % 4][:, (j0 + j) * B:(j0 + j + 1) * B],
                                                           ident[0:B, 0:B])
                            last.then_inc(s_tp, 1)
                        if g >= 1:
                            weigh(i, pr, g - 1)

                def weigh(i, pr, g):
                    q0 = i * HEADS + 2 * pr
                    j0, nj = GROUPS[g]
                    n = q0 // 2 * 6 + 2 * g
                    pe.wait_ge(s_tps, n + 2)
                    if pr == 0 and g == 0 and i >= 1:
                        pe.wait_ge(s_ys, i)
                    for j in range(nj):
                        for hh in range(2):
                            h = 2 * pr + hh
                            last = nc.tensor.matmul(ps[64 * hh:64 * hh + 64, 6, pr * B:(pr + 1) * B],
                                                    vn[:, j0 + j, h * DH:(h + 1) * DH], turnedp[(n + hh) % 4][:, j, :],
                                                    start=(pr == 0 and j0 + j == 0), stop=(pr == PAIRS - 1 and j0 + j == NB - 1),
                                                    skip_group_check=True)
                    last.then_inc(s_y, 1)

                def project(i):
                    pe.wait_ge(s_ys, i + 1)
                    if i >= 1:
                        pe.wait_ge(s_ob, i)
                    for k in range(KT):
                        last = nc.tensor.matmul(ps[0:B, 7, :], yT[i % 2][:, k, :], wo[:, k, :], start=(k == 0), stop=(k == KT - 1))
                    last.then_inc(s_o, 1)

                pe.wait_ge(s_wo, 16)
                scores(0)
                scores(1)
                for s in range(NB * PAIRS):
                    i, pr = divmod(s, PAIRS)
                    if s + 1 < NB * PAIRS:
                        scores(2 * s + 2)
                    if s >= 1:
                        weigh(*divmod(s - 1, PAIRS), 2)
                    if s + 1 < NB * PAIRS:
                        scores(2 * s + 3)
                    turn_and_weigh(i, pr)
                    if pr == 1 and i >= 1:
                        project(i - 1)
                weigh(NB - 1, PAIRS - 1, 2)
                project(NB - 1)

            @block.scalar
            def _(act):
                def exps(q):
                    act.wait_ge(s_max, 3 * q + 3)
                    nc.scalar.activation(pslot[q % 4], pslot[q % 4], ACT.Exp, bias=mx[:, q % 4, 2:3], scale=-1.0).then_inc(s_e3, 1)

                def store_turned(s, g):
                    j0, nj = GROUPS[g]
                    for hh in range(2):
                        n = 6 * s + 2 * g + hh
                        act.wait_ge(s_tp, n + 1)
                        if n >= 4:
                            act.wait_ge(s_y, (n - 4) // 2 + 1)
                        nc.scalar.activation(turnedp[n % 4][:, 0:nj, :], ps[0:B, SB + n % TB, 0:nj * B].rearrange("p (j b) -> p j b", b=B),
                                             ACT.Copy).then_inc(s_tps, 1)

                def store_y(i):
                    act.wait_ge(s_y, 12 * (i + 1))
                    if i >= 2:
                        act.wait_ge(s_o, i - 1)
                    nc.scalar.activation(yT[i % 2], ps[:, 6, 0:KT * B].rearrange("p (k b) -> p k b", b=B), ACT.Copy).then_inc(s_ys, 1)

                exps(0)
                exps(1)
                for s in range(NB * PAIRS):
                    i, pr = divmod(s, PAIRS)
                    more = s + 1 < NB * PAIRS
                    if more:
                        exps(2 * s + 2)
                    if pr == 0 and i >= 1:
                        store_y(i - 1)
                    store_turned(s, 0)
                    store_turned(s, 1)
                    if more:
                        exps(2 * s + 3)
                    store_turned(s, 2)
                store_y(NB - 1)

            @block.vector
            def _(dve):
                def mask(q):
                    i, h = divmod(q, HEADS)
                    if h == 0:
                        dve.wait_ge(s_tab[i % 2], 32 * (i // 2 + 1))
                    if q >= 2:
                        dve.wait_ge(s_max, 3 * (q - 1))
                    nc.vector.tensor_scalar(masks[q % 2], weights[i % 2][:, :, h], 0.0, EMPTY,
                                            ALU.is_le, ALU.mult).then_inc(s_mask3, 1)

                def masked(q):
                    dve.wait_ge(s_mask3, q + 1)
                    if q >= 4:
                        dve.wait_ge(s_tp, ((q - 4) // 2) * 6 + 6)
                        dve.wait_ge(s_p3, q - 3)
                    for c, (c0, cn) in enumerate(CHUNKS):
                        dve.wait_ge(s_qk, 3 * q + c + 1)
                        if c:
                            dve.wait_ge(s_max, 3 * q + c)
                        nc.vector.tensor_tensor_reduce(pslot[q % 4][:, c0:c0 + cn], ps[0:B, (3 * q + c) % SB, 0:cn], masks[q % 2][:, c0:c0 + cn],
                                                       1.0, mx[:, q % 4, c - 1:c] if c else CEILING, ALU.add, ALU.min,
                                                       mx[:, q % 4, c:c + 1]).then_inc(s_max, 1)

                def weigh(q):
                    i, h = divmod(q, HEADS)
                    dve.wait_ge(s_e3, q + 1)
                    nc.vector.tensor_tensor_reduce(pslot[q % 4], pslot[q % 4], weights[i % 2][:, :, h], 1.0, NOTHING,
                                                   ALU.mult, ALU.add, den[:, q % 4:q % 4 + 1]).then_inc(s_wt, 1)
                    dve.wait_ge(s_wt, q + 1)
                    nc.vector.reciprocal(rden[:, q % 4:q % 4 + 1], den[:, q % 4:q % 4 + 1]).then_inc(s_rd, 1)

                def add_out(i):
                    dve.wait_ge(s_o, i + 1)
                    dve.wait_ge(s_xb, 16 * (i + 1))
                    nc.vector.tensor_tensor(xb, ps[0:B, 7, :], xb, ALU.add).then_inc(s_ob, 1)

                mask(0)
                for q in range(HT):
                    masked(q)
                    if q + 1 < HT:
                        mask(q + 1)
                    if q % 2:
                        weigh(q - 1)
                        weigh(q)
                    i, h = divmod(q, HEADS)
                    if h == 6 and i >= 1:
                        add_out(i - 1)
                add_out(NB - 1)


def layout(x, src, dst, edge_attr_8, **p):
    import numpy as np

    def cols(*vectors):
        return np.concatenate([np.asarray(v).reshape(KT, 128).T for v in vectors], axis=1)

    return {
        "x": x, "src": src.reshape(TILES, B).T, "dst": dst.reshape(TILES, B).T,
        "bounds": np.asarray(tile_bounds(), np.float32).reshape(1, 2 * TILES),
        "srcrow": src.reshape(TILES // 2, 2 * B), "dstrow": dst.reshape(TILES // 2, 2 * B),
        "attr": edge_attr_8.reshape(TILES, B, HEADS).transpose(1, 0, 2).reshape(B, TILES * HEADS),
        "wq0": p["L0_gnn_Wq"], "wk0": p["L0_gnn_Wk"], "wv0": p["L0_gnn_Wv"],
        "bn0": cols(p["L0_gnn_bn_gamma"], p["L0_gnn_bn_beta"]),
        "wl1": p["L1_gnn_Wl1"].T, "wr1": p["L1_gnn_Wr1"].T, "b1": cols(p["L1_gnn_b1"]),
        "wl2": p["L1_gnn_Wl2"].T, "wr2": p["L1_gnn_Wr2"].T, "b2": p["L1_gnn_b2"].reshape(1, D),
        "w2": p["L2_gnn_W"].T, "par2": cols(p["L2_gnn_b"], p["L2_gnn_gamma"], p["L2_gnn_beta"]),
        "wq3": p["L3_gnn_Wq"], "wk3": p["L3_gnn_Wk"], "wv3": p["L3_gnn_Wv"], "wo3": p["L3_gnn_Wo"],
        "par3": cols(p["L3_gnn_bq"], p["L3_gnn_bk"]), "bv3": p["L3_gnn_bv"].reshape(1, D),
        "bo3": p["L3_gnn_bo"].reshape(1, D),
    }


def kernel(**inputs):
    import numpy as np
    import concourse.bacc as bacc
    from concourse.bass_utils import run_bass_kernel_spmd

    nc = bacc.Bacc("TRN2", target_bir_lowering=False, num_devices=1)
    arrays, args = {}, {}
    for name, a in layout(**{k: np.asarray(v) for k, v in inputs.items()}).items():
        a = np.ascontiguousarray(a)
        arrays[f"in_{name}"] = a
        args[name] = nc.dram_tensor(f"in_{name}", a.shape, mybir.dt.from_np(a.dtype), kind="ExternalInput").ap()
    out = nc.dram_tensor("out_x", (N, D), F32, kind="ExternalOutput").ap()
    table = nc.dram_tensor("edge_weights", (TABLE_ROWS, HEADS), F32, kind="Internal").ap()
    xsave = nc.dram_tensor("x_saved", (N, D), F32, kind="Internal").ap()
    keys = nc.dram_tensor("edge_keys_row", (EDGES,), F32, kind="Internal").ap()
    graph_kernel(nc, **args, out=out, table=table, xsave=xsave, keys=keys)
    r = run_bass_kernel_spmd(nc, [arrays], core_ids=[0])
    return r.results[0]["out_x"]
```
